# Optimizing a Trainium2 kernel written in Bass

```python
import numpy as np
import jax
import jax.numpy as jnp

def _softmax(x, axis=-1):
    return jax.nn.softmax(x, axis=axis)

def _gelu(x):
    return jax.nn.gelu(x, approximate=True)

def _silu(x):
    return jax.nn.silu(x)

def _sigmoid(x):
    return jax.nn.sigmoid(x)

def _layernorm(x, axis=-1, eps=1e-05):
    m = jnp.mean(x, axis=axis, keepdims=True)
    v = jnp.var(x, axis=axis, keepdims=True)
    return (x - m) / jnp.sqrt(v + eps)

def _scatter_add(tgt, idx, src, axis=0):
    return tgt.at[idx].add(src)

def _segment_sum(src, seg, n):
    return jax.ops.segment_sum(src, seg, n)
kernel_name = 'mk_perceiver_d1_seqx_r4_a5baca'

def setup_inputs(seed: int=0):
    np.random.seed(seed)
    _w = jnp.asarray

    def _rec_inputs():
        import jax
        import jax.numpy as jnp
        _rk = jax.random.key(seed)
        x = 7.22e-05 + 1 * jax.random.normal(jax.random.fold_in(_rk, 1), (128, 32, 256), jnp.float32)
        _lenS = 32 - jax.random.randint(jax.random.fold_in(_rk, 7), (128,), 0, max(1, 32 // 4) + 1, jnp.int32)
        _lenS2 = 257 - jax.random.randint(jax.random.fold_in(_rk, 8), (128,), 0, max(1, 257 // 4) + 1, jnp.int32)
        _ctx_1024P = jax.random.normal(jax.random.fold_in(_rk, 11), (128, 16, 256), jnp.float32)
        _ctx_1024c = jax.random.dirichlet(jax.random.fold_in(_rk, 511), 0.3 * jnp.ones((16,), jnp.float32), (128, 257))
        _ctx_1024t = jnp.einsum('bsk,bkd->bsd', _ctx_1024c, _ctx_1024P)
        _ctx_1024t = _ctx_1024t * jax.lax.rsqrt(jnp.mean(jnp.square(_ctx_1024t)) + 1e-12) * 0.953939
        ctx_1024 = 4.13588e-05 + 0.999923 * (_ctx_1024t + 0.3 * jax.random.normal(jax.random.fold_in(_rk, 611), (128, 257, 256), jnp.float32))
        _validS = jnp.arange(32)[None, :] < _lenS[:, None]
        _validS2 = jnp.arange(257)[None, :] < _lenS2[:, None]
        _causal = jnp.tril(jnp.ones((32, 32), dtype=bool))
        mask_1x1xSxS2_bk0 = jnp.logical_not(jnp.broadcast_to(_validS2[0:1, None, None, :], (1, 1, 32, 257)))
        return (x, ctx_1024, mask_1x1xSxS2_bk0)
    x, ctx_1024, mask_1x1xSxS2_bk0 = _rec_inputs()

    def _L0_xattn_setup():
        import jax, jax.numpy as jnp
        import numpy as np
        import math
        D_MODEL = 256
        NUM_HEADS = 16
        B, S = (4, 512)
        key = jax.random.key(seed)
        ks = jax.random.split(key, 12)
        d = D_MODEL
        sc = 1.0 / math.sqrt(d)
        inp = {'q': jax.random.normal(ks[0], (B, S, d), jnp.float32), 'k': jax.random.normal(ks[1], (B, S, d), jnp.float32), 'v': jax.random.normal(ks[2], (B, S, d), jnp.float32), 'mask': jnp.tril(jnp.ones((S, S), bool))[None, None, :, :], 'Wq': jax.random.normal(ks[3], (d, d), jnp.float32) * sc, 'bq': jnp.zeros((d,), jnp.float32), 'Wk': jax.random.normal(ks[4], (d, d), jnp.float32) * sc, 'bk': jnp.zeros((d,), jnp.float32), 'Wv': jax.random.normal(ks[5], (d, d), jnp.float32) * sc, 'bv': jnp.zeros((d,), jnp.float32), 'Wo': jax.random.normal(ks[6], (d, d), jnp.float32) * sc, 'bo': jnp.zeros((d,), jnp.float32)}
        return inp
    _L0_xattn_all = _L0_xattn_setup()
    _L0_xattn_in = {k: v for k, v in _L0_xattn_all.items() if k in ('Wq', 'bq', 'Wk', 'bk', 'Wv', 'bv', 'Wo', 'bo')}
    del _L0_xattn_all

    def _L0_attn_setup():
        import jax, jax.numpy as jnp
        import numpy as np
        D_MODEL = 256
        D_STATE = 16
        D_CONV = 4
        EXPAND = 2
        E = EXPAND * D_MODEL
        B, L = (4, 1024)
        key = jax.random.key(seed)
        ks = jax.random.split(key, 8)
        x = jax.random.normal(ks[0], (B, L, D_MODEL), dtype=jnp.float32)
        W_in = jax.random.normal(ks[1], (D_MODEL, 2 * E), dtype=jnp.float32) * 0.02
        b_in = jnp.zeros((2 * E,), dtype=jnp.float32)
        conv_w = jax.random.normal(ks[2], (E, 1, D_CONV), dtype=jnp.float32) * 0.1
        conv_b = jnp.zeros((E,), dtype=jnp.float32)
        A = jax.random.normal(ks[3], (E, D_STATE), dtype=jnp.float32) * 0.01
        C = jax.random.normal(ks[4], (E, D_STATE), dtype=jnp.float32) * 0.01
        Dp = jnp.ones((E,), dtype=jnp.float32) * 0.01
        W_out = jax.random.normal(ks[5], (E, D_MODEL), dtype=jnp.float32) * 0.02
        b_out = jnp.zeros((D_MODEL,), dtype=jnp.float32)
        return {'x': x, 'W_in': W_in, 'b_in': b_in, 'conv_w': conv_w, 'conv_b': conv_b, 'A': A, 'C': C, 'Dp': Dp, 'W_out': W_out, 'b_out': b_out}
    _L0_attn_all = _L0_attn_setup()
    _L0_attn_in = {k: v for k, v in _L0_attn_all.items() if k in ('W_in', 'b_in', 'conv_w', 'conv_b', 'A', 'C', 'Dp', 'W_out', 'b_out')}
    del _L0_attn_all

    def _L0_ffn_setup():
        import jax, jax.numpy as jnp
        import numpy as np
        HIDDEN = 256
        INTER = 128
        N_EXPERTS = 16
        N_GROUP = 4
        TOPK_GROUP = 2
        TOP_K = 4
        SCALING = 2.5

        def _gate(x_flat, gate_w, e_bias):
            logits = x_flat @ gate_w.T
            scores = jax.nn.sigmoid(logits)
            scores_for_choice = scores + e_bias[None, :]
            T = x_flat.shape[0]
            per_group = N_EXPERTS // N_GROUP
            grouped = scores_for_choice.reshape(T, N_GROUP, per_group)
            top2, _ = jax.lax.top_k(grouped, 2)
            group_scores = top2.sum(-1)
            _, group_idx = jax.lax.top_k(group_scores, TOPK_GROUP)
            group_mask = jax.nn.one_hot(group_idx, N_GROUP, dtype=jnp.float32).sum(1) > 0
            score_mask = jnp.repeat(group_mask, per_group, axis=-1)
            tmp_scores = jnp.where(score_mask, scores_for_choice, 0.0)
            _, topk_idx = jax.lax.top_k(tmp_scores, TOP_K)
            topk_weight = jnp.take_along_axis(scores, topk_idx, axis=1)
            topk_weight = topk_weight / (topk_weight.sum(-1, keepdims=True) + 1e-20)
            topk_weight = topk_weight * SCALING
            return (topk_idx, topk_weight)
        key = jax.random.key(seed)
        ks = jax.random.split(key, 8)
        B, S = (2, 512)
        hidden_states = jax.random.normal(ks[0], (B, S, HIDDEN), dtype=jnp.float32)
        gate_w = jax.random.normal(ks[1], (N_EXPERTS, HIDDEN), dtype=jnp.float32) * 0.02
        e_bias = jnp.zeros((N_EXPERTS,), dtype=jnp.float32)
        gate_proj = jax.random.normal(ks[2], (N_EXPERTS, INTER, HIDDEN), dtype=jnp.float32) * 0.02
        up_proj = jax.random.normal(ks[3], (N_EXPERTS, INTER, HIDDEN), dtype=jnp.float32) * 0.02
        down_proj = jax.random.normal(ks[4], (N_EXPERTS, HIDDEN, INTER), dtype=jnp.float32) * 0.02
        shared_gate_w = jax.random.normal(ks[5], (INTER, HIDDEN), dtype=jnp.float32) * 0.02
        shared_up_w = jax.random.normal(ks[6], (INTER, HIDDEN), dtype=jnp.float32) * 0.02
        shared_down_w = jax.random.normal(ks[7], (HIDDEN, INTER), dtype=jnp.float32) * 0.02
        return {'hidden_states': hidden_states, 'gate_w': gate_w, 'e_bias': e_bias, 'gate_proj': gate_proj, 'up_proj': up_proj, 'down_proj': down_proj, 'shared_gate_w': shared_gate_w, 'shared_up_w': shared_up_w, 'shared_down_w': shared_down_w}
    _L0_ffn_all = _L0_ffn_setup()
    _L0_ffn_in = {k: v for k, v in _L0_ffn_all.items() if k in ('gate_w', 'e_bias', 'gate_proj', 'up_proj', 'down_proj', 'shared_gate_w', 'shared_up_w', 'shared_down_w')}
    del _L0_ffn_all
    return {'x': x, 'ctx_1024': ctx_1024, 'mask_1x1xSxS2_bk0': mask_1x1xSxS2_bk0, 'L0_xattn_Wq': _L0_xattn_in['Wq'], 'L0_xattn_bq': _L0_xattn_in['bq'], 'L0_xattn_Wk': _L0_xattn_in['Wk'], 'L0_xattn_bk': _L0_xattn_in['bk'], 'L0_xattn_Wv': _L0_xattn_in['Wv'], 'L0_xattn_bv': _L0_xattn_in['bv'], 'L0_xattn_Wo': _L0_xattn_in['Wo'], 'L0_xattn_bo': _L0_xattn_in['bo'], 'L0_attn_W_in': _L0_attn_in['W_in'], 'L0_attn_b_in': _L0_attn_in['b_in'], 'L0_attn_conv_w': _L0_attn_in['conv_w'], 'L0_attn_conv_b': _L0_attn_in['conv_b'], 'L0_attn_A': _L0_attn_in['A'], 'L0_attn_C': _L0_attn_in['C'], 'L0_attn_Dp': _L0_attn_in['Dp'], 'L0_attn_W_out': _L0_attn_in['W_out'], 'L0_attn_b_out': _L0_attn_in['b_out'], 'L0_ffn_gate_w': _L0_ffn_in['gate_w'], 'L0_ffn_e_bias': _L0_ffn_in['e_bias'], 'L0_ffn_gate_proj': _L0_ffn_in['gate_proj'], 'L0_ffn_up_proj': _L0_ffn_in['up_proj'], 'L0_ffn_down_proj': _L0_ffn_in['down_proj'], 'L0_ffn_shared_gate_w': _L0_ffn_in['shared_gate_w'], 'L0_ffn_shared_up_w': _L0_ffn_in['shared_up_w'], 'L0_ffn_shared_down_w': _L0_ffn_in['shared_down_w']}

def reference(x, ctx_1024, mask_1x1xSxS2_bk0, L0_xattn_Wq, L0_xattn_bq, L0_xattn_Wk, L0_xattn_bk, L0_xattn_Wv, L0_xattn_bv, L0_xattn_Wo, L0_xattn_bo, L0_attn_W_in, L0_attn_b_in, L0_attn_conv_w, L0_attn_conv_b, L0_attn_A, L0_attn_C, L0_attn_Dp, L0_attn_W_out, L0_attn_b_out, L0_ffn_gate_w, L0_ffn_e_bias, L0_ffn_gate_proj, L0_ffn_up_proj, L0_ffn_down_proj, L0_ffn_shared_gate_w, L0_ffn_shared_up_w, L0_ffn_shared_down_w):
    import jax
    import jax.numpy as jnp

    def _L0_xattn_ref(q, k, v, mask, Wq, bq, Wk, bk, Wv, bv, Wo, bo):
        import jax, jax.numpy as jnp
        import numpy as np
        import math
        D_MODEL = 256
        NUM_HEADS = 16
        B, S = (4, 512)
        b, s, d = q.shape
        h = NUM_HEADS
        dk = d // h

        def split(x):
            return x.reshape(b, -1, h, dk).transpose(0, 2, 1, 3)
        Q = split(q @ Wq + bq)
        K = split(k @ Wk + bk)
        V = split(v @ Wv + bv)
        scores = jnp.einsum('bhqd,bhkd->bhqk', Q, K) / jnp.sqrt(jnp.float32(dk))
        scores = jnp.where(mask, scores, jnp.float32(-jnp.inf))
        attn = jax.nn.softmax(scores, axis=-1)
        ctx = jnp.einsum('bhqk,bhkd->bhqd', attn, V)
        ctx = ctx.transpose(0, 2, 1, 3).reshape(b, -1, d)
        return ctx @ Wo + bo

    def _L0_attn_ref(x, W_in, b_in, conv_w, conv_b, A, C, Dp, W_out, b_out):
        import jax, jax.numpy as jnp
        import numpy as np
        D_MODEL = 256
        D_STATE = 16
        D_CONV = 4
        EXPAND = 2
        E = EXPAND * D_MODEL
        B, L = (4, 1024)
        Bb, Ll, _ = x.shape
        x_and_z = x @ W_in + b_in
        x_proj, z = jnp.split(x_and_z, 2, axis=-1)
        xc = jnp.transpose(x_proj, (0, 2, 1))
        xc = jax.lax.conv_general_dilated(xc, conv_w, window_strides=(1,), padding=[(D_CONV - 1, 0)], dimension_numbers=('NCH', 'OIH', 'NCH'), feature_group_count=E)
        x_conv = jnp.transpose(xc + conv_b[None, :, None], (0, 2, 1))

        def step(h, xt):
            h = jnp.tanh(xt @ A + h)
            yt = h @ C.T + Dp * xt
            return (h, yt)
        h0 = jnp.zeros((Bb, D_STATE), dtype=x.dtype)
        _, ys = jax.lax.scan(step, h0, jnp.transpose(x_conv, (1, 0, 2)))
        x_s4 = jnp.transpose(ys, (1, 0, 2))
        y = jax.nn.sigmoid(z) * x_s4
        return y @ W_out + b_out

    def _L0_ffn_ref(hidden_states, gate_w, e_bias, gate_proj, up_proj, down_proj, shared_gate_w, shared_up_w, shared_down_w):
        import jax, jax.numpy as jnp
        import numpy as np
        HIDDEN = 256
        INTER = 128
        N_EXPERTS = 16
        N_GROUP = 4
        TOPK_GROUP = 2
        TOP_K = 4
        SCALING = 2.5

        def _gate(x_flat, gate_w, e_bias):
            logits = x_flat @ gate_w.T
            scores = jax.nn.sigmoid(logits)
            scores_for_choice = scores + e_bias[None, :]
            T = x_flat.shape[0]
            per_group = N_EXPERTS // N_GROUP
            grouped = scores_for_choice.reshape(T, N_GROUP, per_group)
            top2, _ = jax.lax.top_k(grouped, 2)
            group_scores = top2.sum(-1)
            _, group_idx = jax.lax.top_k(group_scores, TOPK_GROUP)
            group_mask = jax.nn.one_hot(group_idx, N_GROUP, dtype=jnp.float32).sum(1) > 0
            score_mask = jnp.repeat(group_mask, per_group, axis=-1)
            tmp_scores = jnp.where(score_mask, scores_for_choice, 0.0)
            _, topk_idx = jax.lax.top_k(tmp_scores, TOP_K)
            topk_weight = jnp.take_along_axis(scores, topk_idx, axis=1)
            topk_weight = topk_weight / (topk_weight.sum(-1, keepdims=True) + 1e-20)
            topk_weight = topk_weight * SCALING
            return (topk_idx, topk_weight)
        B, S, H = hidden_states.shape
        x = hidden_states.reshape(-1, H)
        T = x.shape[0]
        topk_idx, topk_weight = _gate(x, gate_w, e_bias)
        g = jnp.einsum('th,eih->eti', x, gate_proj)
        u = jnp.einsum('th,eih->eti', x, up_proj)
        inter = jax.nn.silu(g) * u
        expert_out = jnp.einsum('eti,ehi->eth', inter, down_proj)
        sel = expert_out[topk_idx, jnp.arange(T)[:, None]]
        y = jnp.einsum('tkh,tk->th', sel, topk_weight)
        y = y.reshape(B, S, H)
        sg = hidden_states @ shared_gate_w.T
        su = hidden_states @ shared_up_w.T
        shared_out = jax.nn.silu(sg) * su @ shared_down_w.T
        return y + shared_out
    x = x + _L0_xattn_ref(_layernorm(x, axis=-1), ctx_1024, ctx_1024, mask_1x1xSxS2_bk0, L0_xattn_Wq, L0_xattn_bq, L0_xattn_Wk, L0_xattn_bk, L0_xattn_Wv, L0_xattn_bv, L0_xattn_Wo, L0_xattn_bo)
    x = x + _L0_attn_ref(_layernorm(x, axis=-1), L0_attn_W_in, L0_attn_b_in, L0_attn_conv_w, L0_attn_conv_b, L0_attn_A, L0_attn_C, L0_attn_Dp, L0_attn_W_out, L0_attn_b_out)
    x = x + _L0_ffn_ref(_layernorm(x, axis=-1), L0_ffn_gate_w, L0_ffn_e_bias, L0_ffn_gate_proj, L0_ffn_up_proj, L0_ffn_down_proj, L0_ffn_shared_gate_w, L0_ffn_shared_up_w, L0_ffn_shared_down_w)
    return x

_drawn_inputs = setup_inputs


def setup_inputs(seed=0):
    import zlib

    import numpy as np

    out = dict(_drawn_inputs(seed))
    spreads = {'L0_xattn_bq': (0.0, 0.325),
     'L0_xattn_bk': (0.0, 0.8),
     'L0_xattn_bv': (0.0, 0.1),
     'L0_xattn_bo': (0.0, 0.1),
     'L0_attn_b_in': (0.0, 0.8),
     'L0_attn_conv_b': (0.0, 0.8),
     'L0_attn_Dp': (0.009999999776482582, 0.6),
     'L0_attn_b_out': (0.0, 0.1),
     'L0_ffn_e_bias': (0.0, 0.57)}
    factors = {'L0_attn_W_in': 8.0,
     'L0_attn_conv_w': 8.0,
     'L0_attn_A': 8.0,
     'L0_attn_C': 8.0,
     'L0_attn_W_out': 8.0,
     'L0_ffn_gate_w': 8.0,
     'L0_ffn_gate_proj': 4.452,
     'L0_ffn_up_proj': 4.399,
     'L0_ffn_down_proj': 4.406,
     'L0_ffn_shared_gate_w': 5.064,
     'L0_ffn_shared_up_w': 5.284,
     'L0_ffn_shared_down_w': 5.032}
    for name, (base, spread) in spreads.items():
        noise = np.random.default_rng([zlib.crc32(name.encode()), seed]).standard_normal(out[name].shape)
        drawn = base * np.exp(spread * noise) if base else spread * noise
        out[name] = jnp.asarray(drawn.astype(out[name].dtype))
    for name, factor in factors.items():
        out[name] = (out[name] * factor).astype(out[name].dtype)
    return out
```

```python
import concourse.bass as bass
from concourse import mybir
from concourse.alu_op_type import AluOpType as ALU
from contextlib import ExitStack

F32 = mybir.dt.float32
F32R = mybir.dt.float32r
ACT = mybir.ActivationFunctionType
AX = mybir.AxisListType.X

P = 128
BATCH, SEQ, DM = 128, 32, 256
KEYS = 257
HEADS, DK = 16, 16
TOK = BATCH * SEQ
NT = TOK // P
CH = DM // P
BLK = 512
NB = TOK // BLK
TPB = BLK // P
BPB = BLK // SEQ
EI = 512
ECH = EI // P
NS = 16
TAPS = 4
NE = 16
NG = 4
PG = NE // NG
EPS = 1e-5
NEG = -3.0e38
SCALE = 0.25
PAIRS = BATCH // 2
PK = 2 * KEYS
WIN = 258


def wait(eng, sem, count):
    if isinstance(count, int) and count <= 0:
        return
    eng.wait_ge(sem, count)


class Chain:

    def __init__(self, eng, sem):
        self.eng, self.sem, self.base, self.n = eng, sem, 0, 0

    def at(self, base):
        self.base, self.n = base, 0

    def add(self, ins):
        self.n += 1
        ins.then_inc(self.sem, 1)

    def sync(self):
        wait(self.eng, self.sem, self.base + self.n)

    def link(self, ins):
        self.add(ins)
        self.sync()


def settle(nc, spot):
    nc.vector.memset(spot, 0.0)


def split_matmul(nc, out, lhs, rhs, start, stop, **kw):
    nc.tensor.matmul(out, lhs[0], rhs[0], start=start, stop=False, **kw)
    nc.tensor.matmul(out, lhs[1], rhs[0], start=False, stop=False, **kw)
    return nc.tensor.matmul(out, lhs[0], rhs[1], start=False, stop=stop, **kw)


class Mem:

    def __init__(self, nc, ctx, tag):
        self.nc, self.ctx, self.tag = nc, ctx, tag

    def sb(self, name, shape, dt=F32):
        return self.ctx.enter_context(self.nc.sbuf_tensor(f"{self.tag}_{name}", shape, dt))

    def ps(self, name, shape=(P, 512)):
        return self.ctx.enter_context(self.nc.psum_tensor(f"{self.tag}_{name}", list(shape), F32))

    def sem(self, name):
        return self.ctx.enter_context(self.nc.semaphore(f"{self.tag}_{name}"))


def inverse_deviation(nc, tag, mv, rstd):
    with ExitStack() as ctx:
        m = Mem(nc, ctx, tag)
        ve, sd = m.sb("ve", [P, NT]), m.sb("sd", [P, NT])
        var_ready, sqrt_ready, rstd_ready = m.sem("var_ready"), m.sem("sqrt_ready"), m.sem("rstd_ready")
        block = ctx.enter_context(nc.Block())

        @block.vector
        def _(dve):
            nc.vector.tensor_scalar(ve[:, :], mv[:, :, 1], EPS, None, ALU.add).then_inc(var_ready, 1)
            dve.wait_ge(sqrt_ready, 1)
            nc.vector.reciprocal(rstd[:, :], sd[:, :]).then_inc(rstd_ready, 1)
            dve.wait_ge(rstd_ready, 1)

        @block.scalar
        def _(act):
            act.wait_ge(var_ready, 1)
            nc.scalar.activation(sd[:, :], ve[:, :], ACT.Sqrt).then_inc(sqrt_ready, 1)


def normalise_and_transpose(nc, tag, x_tok, mv, rstd, ident, xTh, xTl):
    with ExitStack() as ctx:
        m = Mem(nc, ctx, tag)
        xn = [m.sb(f"xn{i}", [P, TPB, DM]) for i in range(2)]
        tp = [m.ps(f"tp{i}", [P, CH, BLK]) for i in range(2)]
        xn_ready, tp_ready = m.sem("xn_ready"), m.sem("tp_ready")
        hi_ready, lo_ready = m.sem("hi_ready"), m.sem("lo_ready")
        block = ctx.enter_context(nc.Block())

        def normalise(dve, n, par):
            wait(dve, tp_ready, n - 1)
            for t in range(TPB):
                ti = n * TPB + t
                last = nc.vector.tensor_scalar(
                    xn[par][:, t, :], x_tok[:, bass.ds(ti, 1), :].rearrange("p a d -> p (a d)"),
                    mv[:, bass.ds(ti, 1), 0], rstd[:, bass.ds(ti, 1)], ALU.subtract, ALU.mult)
            last.then_inc(xn_ready, 1)

        def low_part(dve, n, par):
            dve.wait_ge(hi_ready, n + 1)
            cols = bass.ds(n * BLK, BLK)
            nc.vector.tensor_tensor(xTl[:, :, cols], tp[par][:, :, :], xTh[:, :, cols].bitcast(F32),
                                    ALU.subtract).then_inc(lo_ready, 1)

        @block.vector
        def _(dve):
            normalise(dve, 0, 0)
            normalise(dve, 1, 1)
            low_part(dve, 0, 0)
            with dve.Fori(0, NB // 2 - 1) as k:
                normalise(dve, k * 2 + 2, 0)
                low_part(dve, k * 2 + 1, 1)
                normalise(dve, k * 2 + 3, 1)
                low_part(dve, k * 2 + 2, 0)
            low_part(dve, NB - 1, 1)
            dve.wait_ge(lo_ready, NB)

        def transposes(pe, n, par):
            pe.wait_ge(xn_ready, n + 1)
            wait(pe, hi_ready, n - 1)
            wait(pe, lo_ready, n - 1)
            for c in range(CH):
                for t in range(TPB):
                    last = nc.tensor.transpose(tp[par][:, c, t * P:(t + 1) * P],
                                               xn[par][:, t, c * P:(c + 1) * P], ident[:, :])
            last.then_inc(tp_ready, 1)

        @block.tensor
        def _(pe):
            transposes(pe, 0, 0)
            transposes(pe, 1, 1)
            with pe.Fori(0, NB // 2 - 1) as k:
                transposes(pe, k * 2 + 2, 0)
                transposes(pe, k * 2 + 3, 1)

        @block.scalar
        def _(act):
            with act.Fori(0, NB // 2) as k:
                for par in range(2):
                    n = k * 2 + par
                    act.wait_ge(tp_ready, n + 1)
                    nc.scalar.activation(xTh[:, :, bass.ds(n * BLK, BLK)], tp[par][:, :, :],
                                         ACT.Copy).then_inc(hi_ready, 1)


def set_up(nc, a, c):
    with ExitStack() as ctx:
        m = Mem(nc, ctx, "set")
        w_raw = m.sb("w_raw", [P, 3, CH, DM])
        mask_i = m.sb("mask_i", [P, KEYS], mybir.dt.int32)
        mask_f = m.sb("mask_f", [P, KEYS])
        keep = m.sb("keep", [P, 2])
        stats = m.sb("stats", [P, NT, 6])
        x_in, w_in, b_in = m.sem("x_in"), m.sem("w_in"), m.sem("b_in")
        made, chain, aggr = m.sem("made"), m.sem("chain"), m.sem("aggr")
        block = ctx.enter_context(nc.Block())

        @block.sync
        def _(sp):
            sp.dma_start(c["x_tok"][:, :, :], a["x"].rearrange("(t p) d -> p t d", p=P)).then_inc(x_in, 16)
            for i, w in enumerate(("Wq", "Wk", "Wv")):
                sp.dma_start(w_raw[:, i, :, :], a[w].rearrange("(c p) n -> p c n", p=P)).then_inc(w_in, 16)
            sp.dma_start(c["w_o"][:, :, :], a["Wo"].rearrange("(c p) n -> p c n", p=P)).then_inc(b_in, 16)

        @block.scalar
        def _(act):
            act.dma_start(mask_i[:, :], a["mask"]).then_inc(b_in, 16)
            act.dma_start(c["b_qk"][:, :, :], a["b_qk"]).then_inc(b_in, 16)
            act.dma_start(c["b_v"][:, :], a["b_v"]).then_inc(b_in, 16)
            act.dma_start(c["b_o"][:, :], a["b_o"]).then_inc(b_in, 16)

        @block.gpsimd
        def _(pool):
            ch = Chain(pool, made)
            ch.add(pool.memset(c["ones"][:, :, :, :], 1.0))
            ch.add(pool.memset(c["ident"][:, :], 0.0))
            ch.add(pool.memset(c["head_rows"][:, :], 1.0))
            ch.add(pool.memset(c["last_rows"][:, :, :], 0.0))
            ch.sync()
            ch.link(pool.affine_select(out=c["ident"][:, :], in_=c["ident"][:, :], compare_op=ALU.not_equal,
                                       fill=1.0, base=0, pattern=[[-1, P]], channel_multiplier=1))
            ch.link(pool.affine_select(out=c["head_rows"][:, :], in_=c["head_rows"][:, :], compare_op=ALU.is_ge,
                                       fill=0.0, base=0, pattern=[[-DK, 8]], channel_multiplier=1))
            ch.link(pool.affine_select(out=c["head_rows"][:, :], in_=c["head_rows"][:, :], compare_op=ALU.is_ge,
                                       fill=0.0, base=DK - 1, pattern=[[DK, 8]], channel_multiplier=-1))
            ch.link(pool.affine_select(out=c["last_rows"][:, :, :], in_=c["last_rows"][:, :, :],
                                       compare_op=ALU.not_equal, fill=1.0, base=0,
                                       pattern=[[-1, 8], [0, 64]], channel_multiplier=1))

        @block.vector
        def _(dve):
            ch = Chain(dve, chain)
            dve.wait_ge(x_in, 16)
            with dve.Fori(0, NT // 4) as k:
                for i in range(4):
                    t = k * 4 + i
                    nc.vector.bn_stats(stats[:, bass.ds(t, 1), :].rearrange("p a d -> p (a d)"),
                                       c["x_tok"][:, bass.ds(t, 1), :].rearrange("p a d -> p (a d)")
                                       ).then_inc(aggr, 1)
            dve.wait_ge(aggr, NT)
            for t in range(NT):
                nc.vector.bn_aggr(c["mv"][:, t, :], stats[:, t, :]).then_inc(aggr, 1)
            dve.wait_ge(w_in, 48)
            ch.link(nc.vector.tensor_copy(c["wh"][:, :, :, :], w_raw[:, :, :, :]))
            ch.add(nc.vector.tensor_tensor(c["wl"][:, :, :, :], w_raw[:, :, :, :],
                                           c["wh"][:, :, :, :].bitcast(F32), ALU.subtract))
            ch.add(nc.vector.tensor_copy(c["wv_raw"][:, :, :], w_raw[:, 2, :, :]))
            dve.wait_ge(b_in, 80)
            ch.link(nc.vector.tensor_copy(mask_f[:, :], mask_i[:, :]))
            ch.link(nc.vector.tensor_scalar(c["mask_add"][:, :], mask_f[:, :], -NEG, NEG, ALU.mult, ALU.add))
            ch.link(nc.vector.reduce_sum(keep[:, 0:1], mask_f[:, :], AX))
            ch.link(nc.vector.reciprocal(keep[:, 1:2], keep[:, 0:1]))
            ch.link(nc.vector.tensor_scalar(c["any_key"][:, :], keep[:, 1:2], 0.0, 1.0, ALU.mult, ALU.add))
            dve.wait_ge(made, 8)
            ch.link(nc.vector.tensor_reduce(c["odd_even"][:, :],
                                            c["head_rows"][:, :].rearrange("p (j e) -> p e j", e=2), AX, ALU.add))
            dve.wait_ge(aggr, 2 * NT)


def queries(nc, c, xTh, xTl):
    with ExitStack() as ctx:
        m = Mem(nc, ctx, "q")
        qp = [m.ps(f"qp{i}") for i in range(4)]
        q_ready, qh_ready, ql_ready, biased = m.sem("q_ready"), m.sem("qh_ready"), m.sem("ql_ready"), m.sem("biased")
        block = ctx.enter_context(nc.Block())

        @block.tensor
        def _(pe):
            def block_of_queries(n):
                cols = bass.ds(n * BLK, BLK)
                for o in range(CH):
                    wait(pe, qh_ready, (n - 1) * CH + o + 1)
                    wait(pe, ql_ready, (n - 1) * CH + o + 1)
                    for ci in range(CH):
                        last = split_matmul(nc, qp[o][:, :], (c["wh"][:, 0, ci, o * P:(o + 1) * P],
                                                              c["wl"][:, 0, ci, o * P:(o + 1) * P]),
                                            (xTh[:, ci, cols], xTl[:, ci, cols]), ci == 0, ci == CH - 1)
                    last.then_inc(q_ready, 1)

            block_of_queries(0)
            with pe.Fori(1, NB) as n:
                block_of_queries(n)

        @block.scalar
        def _(act):
            with act.Fori(0, NB) as n:
                for o in range(CH):
                    act.wait_ge(q_ready, n * CH + o + 1)
                    nc.scalar.activation(c["qTh"][:, o, bass.ds(n * BLK, BLK)], qp[o][:, :], ACT.Identity,
                                         bias=c["b_qk"][:, 0, o:o + 1]).then_inc(qh_ready, 1)

        @block.vector
        def _(dve):
            with dve.Fori(0, NB) as n:
                for o in range(CH):
                    dve.wait_ge(qh_ready, n * CH + o + 1)
                    cols = bass.ds(n * BLK, BLK)
                    nc.vector.scalar_tensor_tensor(
                        out=c["qTl"][:, o, cols], in0=qp[o][:, :], scalar=c["b_qk"][:, 0, o:o + 1],
                        in1=c["qTh"][:, o, cols].bitcast(F32), op0=ALU.add, op1=ALU.subtract).then_inc(ql_ready, 1)
            dve.wait_ge(ql_ready, NB * CH)

        @block.gpsimd
        def _(pool):
            pool.tensor_tensor(c["x_tok"][:, :, :], c["x_tok"][:, :, :],
                               c["b_o"][:, :].unsqueeze(1).to_broadcast([P, NT, DM]), ALU.add).then_inc(biased, 1)
            pool.wait_ge(biased, 1)


def attention(nc, a, c):
    with ExitStack() as ctx:
        m = Mem(nc, ctx, "at")
        ctx_raw = [m.sb(f"ctx_raw{i}", [P, CH, PK]) for i in range(2)]
        ctx_hi = [m.sb(f"ctx_hi{i}", [P, CH, PK], F32R) for i in range(2)]
        ctx_lo = [m.sb(f"ctx_lo{i}", [P, CH, PK], F32R) for i in range(2)]
        ctx_last = [m.sb(f"ctx_last{i}", [P, CH, 2, 4]) for i in range(2)]
        k_hi, k_lo = m.sb("k_hi", [P, CH, PK], F32R), m.sb("k_lo", [P, CH, PK], F32R)
        v_sb = [m.sb(f"v_sb{i}", [P, 2, 2, DM]) for i in range(2)]
        v_last_row = m.sb("v_last_row", [8, DM])
        v_last = [m.sb(f"v_last{i}", [8, 2, DM]) for i in range(2)]
        q_hi = [m.sb(f"q_hi{i}", [P, CH, 8, SEQ], F32R) for i in range(2)]
        q_lo = [m.sb(f"q_lo{i}", [P, CH, 8, SEQ], F32R) for i in range(2)]
        prob = m.sb("prob", [P, 2, 4, KEYS])
        mx = [m.sb(f"mx{i}", [P, 4]) for i in range(2)]
        shift = [m.sb(f"shift{i}", [P, 4]) for i in range(2)]
        total = [m.sb(f"total{i}", [P, 4]) for i in range(2)]
        inv = [m.sb(f"inv{i}", [P, 4]) for i in range(2)]
        inv_n = [m.sb(f"inv_n{i}", [P, 4]) for i in range(2)]
        pT = [m.sb(f"pT{i}", [P, 2, 512]) for i in range(2)]
        p_last = m.sb("p_last", [8, P])
        o_even = m.sb("o_even", [P, CH, SEQ])
        oT = m.sb("oT", [P, CH, P])
        spot = m.sb("spot", [1, 10])
        stats, mv_tile = m.sb("stats", [P, 6]), m.sb("mv_tile", [P, 2])

        proj = [m.ps(f"proj{i}") for i in range(2)]
        sc = [m.ps(f"sc{i}") for i in range(2)]
        tp = [m.ps(f"tp{i}") for i in range(2)]
        ob = m.ps("ob")
        yb = m.ps("yb")
        o_ps = [ob[:, i * 128:(i + 1) * 128] for i in range(2)]
        last_ps = ob[0:8, 256:384]

        S = {k: m.sem(k) for k in (
            "ctx_in0", "ctx_in1", "ctx_hi_ready", "ctx_lo_ready", "ctx_last_ready",
            "proj_ready", "k_hi_ready", "k_lo_ready", "v_ready", "v_row_ready", "v_last_ready",
            "q_ready", "s_ready", "s_pair_done", "masked", "mx_ready", "shift_ready", "exp_ready", "inv_ready",
            "norm_ready", "t_ready", "t_last_ready", "pT0_ready", "pT1_ready", "p_last_ready",
            "av_ready", "o_half", "oT_ready", "y_ready", "x_ready", "dve_chain", "av_pair")}

        NU = 7

        block = ctx.enter_context(nc.Block())

        def load(sp, n, par):
            if not isinstance(n, int):
                n = sp.snap(n)
            wait(sp, S["proj_ready"], (n - 1) * NU)
            sp.dma_start(ctx_raw[par][:, :, :], a["ctxT"][:, :, bass.ds(n * PK, PK)]
                         ).then_inc(S[f"ctx_in{par}"], 16)

        @block.sync
        def _(sp):
            load(sp, 0, 0)
            load(sp, 1, 1)
            with sp.Fori(0, PAIRS // 2 - 1) as k:
                load(sp, k * 2 + 2, 0)
                load(sp, k * 2 + 3, 1)

        def arrived(eng, n, par):
            eng.wait_ge(S[f"ctx_in{par}"], (half_of(n, par) + 1) * 16)

        def half_of(n, par):
            return n // 2 if isinstance(n, int) else half[0] + 1

        half = [0]
        def pe_k(pe, n, par):
            pe.wait_ge(S["ctx_hi_ready"], n + 1)
            pe.wait_ge(S["ctx_lo_ready"], n + 1)
            for o in range(CH):
                for w, (lo, cols) in enumerate(((0, WIN), (WIN, PK - WIN))):
                    u = o * 2 + w
                    proj_free(pe, n, par, u)
                    bank = proj[(par * NU + u) % 2]
                    for ci in range(CH):
                        last = split_matmul(nc, bank[:, 0:cols],
                                            (c["wh"][:, 1, ci, o * P:(o + 1) * P], c["wl"][:, 1, ci, o * P:(o + 1) * P]),
                                            (ctx_hi[par][:, ci, lo:lo + cols], ctx_lo[par][:, ci, lo:lo + cols]),
                                            ci == 0, ci == CH - 1)
                    last.then_inc(S["proj_ready"], 1)

        def proj_free(pe, n, par, u):
            v, pn = u - 2, n
            if v < 0:
                v, pn = v + NU, n - 1
            if v < 4:
                wait(pe, S["k_lo_ready"], pn * 4 + v + 1)
            elif v < 6:
                wait(pe, S["v_ready"], pn * 2 + v - 4 + 1)
            else:
                wait(pe, S["v_row_ready"], pn + 1)

        def pe_v(pe, n, par):
            for b in range(2):
                u = 4 + b
                proj_free(pe, n, par, u)
                bank = proj[(par * NU + u) % 2]
                for kt in range(2):
                    lo = b * KEYS + kt * P
                    for ci in range(CH):
                        last = split_matmul(nc, bank[:, kt * DM:(kt + 1) * DM],
                                            (ctx_hi[par][:, ci, lo:lo + P], ctx_lo[par][:, ci, lo:lo + P]),
                                            (c["wh"][:, 2, ci, :], c["wl"][:, 2, ci, :]), ci == 0, ci == CH - 1)
                last.then_inc(S["proj_ready"], 1)
            u = 6
            proj_free(pe, n, par, u)
            pe.wait_ge(S["ctx_last_ready"], n + 1)
            bank = proj[(par * NU + u) % 2]
            for ci in range(CH):
                rows = ctx_last[par][:, ci, :, :].rearrange("p b r -> p (b r)")
                last = nc.tensor.matmul(bank[0:8, 0:DM], rows, c["wv_raw"][:, ci, :],
                                        start=ci == 0, stop=ci == CH - 1)
            last.then_inc(S["proj_ready"], 1)

        def pe_scores(pe, n, par, b):
            pe.wait_ge(S["q_ready"], n * 2 + b + 1)
            if b == 0:
                pe.wait_ge(S["k_lo_ready"], n * 4 + 4)
            off = 0 if b == 0 else KEYS - 1
            for g in range(4):
                i = b * 4 + g
                wait(pe, S["masked"], n * 8 + i - 1)
                ci, q0 = g // 2, (g % 2) * P
                qh = q_hi[b][:, ci, :, :].rearrange("p h q -> p (h q)")[:, q0:q0 + P]
                ql = q_lo[b][:, ci, :, :].rearrange("p h q -> p (h q)")[:, q0:q0 + P]
                split_matmul(nc, sc[i % 2][:, 0:WIN], (qh, ql),
                             (k_hi[:, ci, off:off + WIN], k_lo[:, ci, off:off + WIN]), True, True
                             ).then_inc(S["s_ready"], 1)

        def pe_transposes(pe, p, b):
            pe.wait_ge(S["norm_ready"], p * 2 + b + 1)
            for kt in range(2):
                wait(pe, S[f"pT{kt}_ready"], p * 2 + b)
                for g in range(4):
                    last = nc.tensor.transpose(tp[kt][:, g * P:(g + 1) * P], prob[:, b, g, kt * P:(kt + 1) * P],
                                               c["ident"][:, :])
                last.then_inc(S["t_ready"], 1)

        def pe_last_transpose(pe, p):
            wait(pe, S["oT_ready"], p * 2)
            wait(pe, S["p_last_ready"], p)
            nc.tensor.transpose(last_ps, prob[:, :, :, KEYS - 1].rearrange("p b g -> p (b g)"), c["ident"][:, :]
                                ).then_inc(S["t_last_ready"], 1)

        def pe_av(pe, p, ppar, b):
            pe.wait_ge(S["pT0_ready"], p * 2 + b + 1)
            pe.wait_ge(S["pT1_ready"], p * 2 + b + 1)
            pe.wait_ge(S["p_last_ready"], p + 1)
            pe.wait_ge(S["v_ready"], p * 2 + b + 1)
            pe.wait_ge(S["v_last_ready"], p + 1)
            wait(pe, S["oT_ready"], p * 2 + b)
            for g in range(CH):
                for kt in range(3):
                    for j in range(4):
                        h0 = g * 8 + 2 * j
                        hd = slice(g * P + 32 * j, g * P + 32 * j + 32)
                        out = o_ps[b][32 * j:32 * j + 32, g * 64:(g + 1) * 64]
                        if kt < 2:
                            last = nc.tensor.matmul(out, v_sb[ppar][:, b, kt, hd], pT[b][:, kt, h0 * SEQ:(h0 + 2) * SEQ],
                                                    start=kt == 0, stop=False, tile_position=(0, 32 * j))
                        else:
                            q0 = (h0 % 4) * SEQ
                            last = nc.tensor.matmul(out, v_last[ppar][0:8, b, hd], p_last[0:8, q0:q0 + 2 * SEQ],
                                                    start=False, stop=True, tile_position=(0, 32 * j))
            last.then_inc(S["av_ready"], 1)

        def pe_out(pe, t):
            pe.wait_ge(S["oT_ready"], t * 4 + 4)
            wait(pe, S["x_ready"], t)
            for ci in range(CH):
                last = nc.tensor.matmul(yb[:, 0:DM], oT[:, ci, :], c["w_o"][:, ci, :], start=ci == 0, stop=ci == CH - 1)
            last.then_inc(S["y_ready"], 1)

        def pe_step(pe, n, par, t=None):
            pe_k(pe, n, par)
            if t is not None:
                pe_out(pe, t)
            later = not isinstance(n, int) or n > 0
            if later:
                pe_transposes(pe, n - 1, 0)
            pe_v(pe, n, par)
            if later:
                pe_transposes(pe, n - 1, 1)
                pe_last_transpose(pe, n - 1)
            for b in range(2):
                pe_scores(pe, n, par, b)
                if later:
                    pe_av(pe, n - 1, 1 - par, b)

        @block.tensor
        def _(pe):
            pe_step(pe, 0, 0)
            pe_step(pe, 1, 1)
            with pe.Fori(0, PAIRS // 2 - 1) as k:
                pe_step(pe, k * 2 + 2, 0)
                pe_step(pe, k * 2 + 3, 1, k)
            pe_transposes(pe, PAIRS - 1, 0)
            pe_transposes(pe, PAIRS - 1, 1)
            pe_last_transpose(pe, PAIRS - 1)
            pe_av(pe, PAIRS - 1, 1, 0)
            pe_av(pe, PAIRS - 1, 1, 1)
            pe_out(pe, NT - 1)

        def act_k(act, n, par):
            if not (isinstance(n, int) and n == 0):
                act.wait_ge(S["s_ready"], n * 8)
            for u in range(4):
                act.wait_ge(S["proj_ready"], n * NU + u + 1)
                o, w = u // 2, u % 2
                lo, cols = ((0, WIN), (WIN, PK - WIN))[w]
                nc.scalar.activation(k_hi[:, o, lo:lo + cols], proj[(par * NU + u) % 2][:, 0:cols], ACT.Identity,
                                     bias=c["b_qk"][:, 1, o:o + 1]).then_inc(S["k_hi_ready"], 1)

        def act_pT(act, p, b):
            act.wait_ge(S["t_ready"], p * 4 + b * 2 + 1)
            wait(act, S["av_ready"], p * 2 + b - 1)
            nc.scalar.activation(pT[b][:, 0, :], tp[0][:, :], ACT.Copy).then_inc(S["pT0_ready"], 1)

        def act_exp(act, n, b):
            act.wait_ge(S["shift_ready"], n * 2 + b + 1)
            wait(act, S["inv_ready"], n * 2 + b - 1)
            for g in range(4):
                nc.scalar.activation(prob[:, b, g, :], prob[:, b, g, :], ACT.Exp, bias=shift[b][:, g:g + 1],
                                     scale=SCALE, accum_out=total[b][:, g:g + 1]).then_inc(S["exp_ready"], 1)

        def act_step(act, n, par):
            later = not isinstance(n, int) or n > 0
            act_k(act, n, par)
            if later:
                act_pT(act, n - 1, 0)
                act_pT(act, n - 1, 1)
            act_exp(act, n, 0)
            act_exp(act, n, 1)

        @block.scalar
        def _(act):
            act_step(act, 0, 0)
            act_step(act, 1, 1)
            with act.Fori(0, PAIRS // 2 - 1) as k:
                act_step(act, k * 2 + 2, 0)
                act_step(act, k * 2 + 3, 1)
            act_pT(act, PAIRS - 1, 0)
            act_pT(act, PAIRS - 1, 1)

        def pool_ctx(pool, n, par):
            arrived(pool, n, par)
            wait(pool, S["proj_ready"], (n - 1) * NU)
            nc.gpsimd.tensor_tensor(ctx_last[par][:, :, :, :],
                                    ctx_raw[par][:, :, KEYS - 1:PK:KEYS].unsqueeze(3).to_broadcast([P, CH, 2, 4]),
                                    c["ones"][:, :, :, :], ALU.mult).then_inc(S["ctx_last_ready"], 1)
            nc.gpsimd.tensor_copy(ctx_hi[par][:, :, :], ctx_raw[par][:, :, :]).then_inc(S["ctx_hi_ready"], 1)

        def pool_q(pool, n, b):
            wait(pool, S["s_ready"], n * 8 - 4 + b * 4)
            for src, dst in ((c["qTh"], q_hi[b]), (c["qTl"], q_lo[b])):
                q = src[:, :, bass.ds((n * 2 + b) * SEQ, SEQ)].bitcast(F32)
                for ci in range(CH):
                    last = nc.gpsimd.tensor_tensor(
                        dst[:, ci, :, :], q[:, ci, :].unsqueeze(1).to_broadcast([P, 8, SEQ]),
                        c["head_rows"][:, :].unsqueeze(2).to_broadcast([P, 8, SEQ]), ALU.mult)
            last.then_inc(S["q_ready"], 1)

        def pool_norm(pool, n, b):
            pool.wait_ge(S["inv_ready"], n * 2 + b + 1)
            nc.gpsimd.tensor_tensor(prob[:, b, :, :], prob[:, b, :, :],
                                    inv_n[b][:, :].unsqueeze(2).to_broadcast([P, 4, KEYS]), ALU.mult
                                    ).then_inc(S["norm_ready"], 1)

        def pool_v_last(pool, n, par):
            pool.wait_ge(S["v_row_ready"], n + 1)
            wait(pool, S["av_ready"], n * 2 - 2)
            nc.gpsimd.tensor_tensor(
                v_last[par][:, :, :],
                v_last_row[:, :].unsqueeze(1).to_broadcast([8, 2, DM]),
                c["last_rows"][:, :, :].rearrange("r (b g) n -> r b (g n)", b=2), ALU.mult).then_inc(S["v_last_ready"], 1)

        def pool_step(pool, n, par, more=True):
            later = not isinstance(n, int) or n > 0
            if later:
                pool_norm(pool, n - 1, 1)
            if more:
                pool_ctx(pool, n + 1, 1 - par)
            pool_q(pool, n, 0)
            pool_q(pool, n, 1)
            pool_v_last(pool, n, par)
            pool_norm(pool, n, 0)

        @block.gpsimd
        def _(pool):
            pool_ctx(pool, 0, 0)
            pool_step(pool, 0, 0)
            half[0] = 0
            pool_step(pool, 1, 1)
            with pool.Fori(0, PAIRS // 2 - 2) as k:
                half[0] = k
                pool_step(pool, k * 2 + 2, 0)
                half[0] = k + 1
                pool_step(pool, k * 2 + 3, 1)
            pool_step(pool, PAIRS - 2, 0)
            pool_step(pool, PAIRS - 1, 1, False)
            pool_norm(pool, PAIRS - 1, 1)

        def dve_ctx(dve, n, par):
            dve.wait_ge(S["ctx_hi_ready"], n + 1)
            nc.vector.tensor_tensor(ctx_lo[par][:, :, :], ctx_raw[par][:, :, :], ctx_hi[par][:, :, :].bitcast(F32),
                                    ALU.subtract).then_inc(S["ctx_lo_ready"], 1)

        def dve_k(dve, n, par, u):
            dve.wait_ge(S["k_hi_ready"], n * 4 + u + 1)
            o, w = u // 2, u % 2
            lo, cols = ((0, WIN), (WIN, PK - WIN))[w]
            nc.vector.scalar_tensor_tensor(
                out=k_lo[:, o, lo:lo + cols], in0=proj[(par * NU + u) % 2][:, 0:cols],
                scalar=c["b_qk"][:, 1, o:o + 1], in1=k_hi[:, o, lo:lo + cols].bitcast(F32),
                op0=ALU.add, op1=ALU.subtract).then_inc(S["k_lo_ready"], 1)

        def dve_pT(dve, p, b):
            dve.wait_ge(S["t_ready"], p * 4 + b * 2 + 2)
            wait(dve, S["av_ready"], p * 2 + b - 1)
            nc.vector.tensor_copy(pT[b][:, 1, :], tp[1][:, :]).then_inc(S["pT1_ready"], 1)

        def dve_v(dve, n, par, b):
            dve.wait_ge(S["proj_ready"], n * NU + 5 + b)
            wait(dve, S["av_ready"], n * 2 - 2)
            nc.vector.tensor_tensor(v_sb[par][:, b, :, :], proj[(par * NU + 4 + b) % 2][:, :].rearrange("p (k n) -> p k n", k=2),
                                    c["b_v"][:, :].unsqueeze(1).to_broadcast([P, 2, DM]), ALU.add
                                    ).then_inc(S["v_ready"], 1)

        def dve_v_row(dve, n, par):
            dve.wait_ge(S["proj_ready"], n * NU + 7)
            wait(dve, S["v_last_ready"], n)
            nc.vector.tensor_tensor(v_last_row[:, :], proj[(par * NU + 6) % 2][0:8, 0:DM], c["b_v"][0:8, :], ALU.add
                                    ).then_inc(S["v_row_ready"], 1)

        def dve_p_last(dve, p):
            dve.wait_ge(S["t_last_ready"], p + 1)
            wait(dve, S["av_ready"], p * 2)
            nc.vector.tensor_copy(p_last[:, :], last_ps).then_inc(S["p_last_ready"], 1)

        def dve_mask_max(dve, n, b):
            off = b
            for g in range(4):
                i = b * 4 + g
                dve.wait_ge(S["s_ready"], n * 8 + i + 1)
                if g == 0:
                    wait(dve, S["t_ready"], (n - 1) * 4 + b * 2 + 2)
                    wait(dve, S["t_last_ready"], n)
                settle(nc, spot[0:1, i:i + 1])
                nc.vector.tensor_tensor_reduce(
                    out=prob[:, b, g, :], in0=sc[i % 2][:, off:off + KEYS], in1=c["mask_add"][:, :],
                    scale=1.0, scalar=NEG, op0=ALU.add, op1=ALU.max, accum_out=mx[b][:, g:g + 1]
                ).then_inc(S["masked"], 1)
            dve.wait_ge(S["masked"], n * 8 + b * 4 + 4)
            wait(dve, S["exp_ready"], n * 8 + b * 4 - 4)
            nc.vector.tensor_scalar(shift[b][:, :], mx[b][:, :], -SCALE, None, ALU.mult).then_inc(S["shift_ready"], 1)

        def dve_inv(dve, ch, n, b):
            dve.wait_ge(S["exp_ready"], n * 8 + b * 4 + 4)
            ch.link(nc.vector.reciprocal(inv[b][:, :], total[b][:, :]))
            wait(dve, S["norm_ready"], n * 2 + b - 1)
            nc.vector.tensor_scalar(inv_n[b][:, :], inv[b][:, :], c["any_key"][:, 0:1], None, ALU.mult
                                    ).then_inc(S["inv_ready"], 1)

        def dve_o(dve, ch, p, ppar, b):
            dve.wait_ge(S["av_ready"], p * 2 + b + 1)
            o = o_ps[b].rearrange("p (g e q) -> p g e q", g=CH, e=2)
            ch.link(nc.vector.tensor_scalar(o_even[:, :, :], o[:, :, 0, :], c["odd_even"][:, 0:1], None, ALU.mult))
            if b == 0 and ppar == 0:
                wait(dve, S["y_ready"], p // 2 if isinstance(p, int) else half[0])
            q0 = (ppar * 2 + b) * SEQ
            nc.vector.scalar_tensor_tensor(out=oT[:, :, q0:q0 + SEQ], in0=o[:, :, 1, :], scalar=c["odd_even"][:, 1:2],
                                           in1=o_even[:, :, :], op0=ALU.mult, op1=ALU.add).then_inc(S["oT_ready"], 1)
            dve.wait_ge(S["oT_ready"], p * 2 + b + 1)

        def dve_x(dve, ch, t):
            dve.wait_ge(S["y_ready"], t + 1)
            xt = c["x_tok"][:, bass.ds(t, 1), :].rearrange("p a d -> p (a d)")
            nc.vector.tensor_tensor(xt, yb[:, 0:DM], xt, ALU.add).then_inc(S["x_ready"], 1)
            dve.wait_ge(S["x_ready"], t + 1)
            settle(nc, spot[0:1, 8:9])
            ch.link(nc.vector.bn_stats(stats[:, :], xt))
            settle(nc, spot[0:1, 9:10])
            ch.link(nc.vector.bn_aggr(mv_tile[:, :], stats[:, :]))
            ch.link(nc.vector.tensor_copy(c["mv"][:, bass.ds(t, 1), :].rearrange("p a d -> p (a d)"), mv_tile[:, :]))

        def dve_step(dve, ch, n, par, t=None, more=True):
            later = not isinstance(n, int) or n > 0
            dve_k(dve, n, par, 0)
            dve_k(dve, n, par, 1)
            if later:
                dve_inv(dve, ch, n - 1, 1)
            dve_k(dve, n, par, 2)
            dve_k(dve, n, par, 3)
            if t is not None:
                dve_x(dve, ch, t)
            if later:
                dve_pT(dve, n - 1, 0)
            dve_v(dve, n, par, 0)
            dve_v(dve, n, par, 1)
            dve_v_row(dve, n, par)
            if more:
                dve_ctx(dve, n + 1, 1 - par)
            if later:
                dve_pT(dve, n - 1, 1)
                dve_p_last(dve, n - 1)
            dve_mask_max(dve, n, 0)
            if later:
                dve_o(dve, ch, n - 1, 1 - par, 0)
            dve_mask_max(dve, n, 1)
            dve_inv(dve, ch, n, 0)
            if later:
                dve_o(dve, ch, n - 1, 1 - par, 1)

        @block.vector
        def _(dve):
            ch = Chain(dve, S["dve_chain"])
            dve_ctx(dve, 0, 0)
            dve_step(dve, ch, 0, 0)
            dve_step(dve, ch, 1, 1)
            first = ch.n
            with dve.Fori(0, PAIRS // 2 - 2) as k:
                per = 2 * 4 + 3
                ch.at(k * per + first)
                half[0] = k
                dve_step(dve, ch, k * 2 + 2, 0)
                half[0] = k + 1
                dve_step(dve, ch, k * 2 + 3, 1, k)
                assert ch.n == per
            ch.at(first + per * (PAIRS // 2 - 2))
            dve_step(dve, ch, PAIRS - 2, 0)
            dve_step(dve, ch, PAIRS - 1, 1, NT - 2, False)
            dve_inv(dve, ch, PAIRS - 1, 1)
            dve_pT(dve, PAIRS - 1, 0)
            dve_pT(dve, PAIRS - 1, 1)
            dve_p_last(dve, PAIRS - 1)
            dve_o(dve, ch, PAIRS - 1, 1, 0)
            dve_o(dve, ch, PAIRS - 1, 1, 1)
            dve_x(dve, ch, NT - 1)


HALF = 2
HB = NB // HALF
HTOK = TOK // HALF
HBATCH = BATCH // HALF


def recurrent_inputs(nc, a, c):
    with ExitStack() as ctx:
        m = Mem(nc, ctx, "rin")
        raw = m.sb("raw", [P, CH, 2 * EI])
        w_in, rest_in, split = m.sem("w_in"), m.sem("rest_in"), m.sem("split")
        block = ctx.enter_context(nc.Block())

        @block.sync
        def _(sp):
            sp.dma_start(raw[:, :, :], a["W_in"].rearrange("(c p) n -> p c n", p=P)).then_inc(w_in, 16)
            for name, src in (("A", a["A"].rearrange("(c p) n -> p c n", p=P)), ("C_T", a["C_T"]),
                              ("w_out", a["W_out"].rearrange("(c p) n -> p c n", p=P)), ("cols", a["cols"]),
                              ("b_out", a["b_out"])):
                dst = c[name]
                sp.dma_start(dst[tuple([slice(None)] * len(dst.shape))], src).then_inc(rest_in, 16)
            sp.wait_ge(rest_in, 5 * 16)

        @block.vector
        def _(dve):
            dve.wait_ge(w_in, 16)
            nc.vector.tensor_copy(c["wih"][:, :, :], raw[:, :, :]).then_inc(split, 1)
            dve.wait_ge(split, 1)
            nc.vector.tensor_tensor(c["wil"][:, :, :], raw[:, :, :], c["wih"][:, :, :].bitcast(F32), ALU.subtract
                                    ).then_inc(split, 1)
            dve.wait_ge(split, 2)


def recurrent(nc, c, xTh, xTl):
    with ExitStack() as ctx:
        m = Mem(nc, ctx, "rec")
        xpad = [m.sb(f"xpad{i}", [P, BPB, SEQ + TAPS - 1]) for i in range(2)]
        conv_sum = m.sb("conv_sum", [P, BPB, SEQ])
        conv = m.sb("conv", [P, ECH, HTOK])
        gate = m.sb("gate", [P, ECH, HTOK])
        state = m.sb("state", [P, HTOK])
        step_sum = m.sb("step_sum", [NS, HBATCH])
        y = m.sb("y", [P, ECH, BLK])
        spot = m.sb("spot", [1, 4])
        stats, mv_tile = m.sb("stats", [P, 6]), m.sb("mv_tile", [P, 2])
        proj = [m.ps(f"proj{i}") for i in range(2)]
        up = m.ps("up", (NS, 512))
        yp = [m.ps(f"yp{i}") for i in range(2)]
        op = [m.ps(f"op{i}") for i in range(2)]
        S = {k: m.sem(k) for k in ("proj_ready", "proj_read", "padded", "conv_step", "conv_ready", "up_ready", "u_ready",
                                   "sum_ready", "h_ready", "yp_ready", "dir_ready", "gated", "op_ready", "x_ready",
                                   "biased", "stat_step")}
        block = ctx.enter_context(nc.Block())
        E2 = 2 * ECH

        @block.tensor
        def _(pe):
            def inputs(g):
                cols = bass.ds(g * BLK, BLK)
                for e in range(E2):
                    wait(pe, S["proj_read"], g * E2 + e - 1)
                    for ci in range(CH):
                        last = split_matmul(nc, proj[e % 2][:, :], (c["wih"][:, ci, e * P:(e + 1) * P],
                                                                    c["wil"][:, ci, e * P:(e + 1) * P]),
                                            (xTh[:, ci, cols], xTl[:, ci, cols]), ci == 0, ci == CH - 1)
                    last.then_inc(S["proj_ready"], 1)

            def state_inputs(g, q):
                pe.wait_ge(S["conv_ready"], g * ECH + ECH)
                wait(pe, S["u_ready"], g)
                for j in range(ECH):
                    last = nc.tensor.matmul(up[:, :], c["A"][:, j, :], conv[:, j, bass.ds(q * BLK, BLK)],
                                            start=j == 0, stop=j == ECH - 1)
                last.then_inc(S["up_ready"], 1)

            def direct(half, g, q):
                pe.wait_ge(S["h_ready"], half * SEQ + SEQ)
                for j in range(ECH):
                    wait(pe, S["dir_ready"], g * ECH + j - 1)
                    nc.tensor.matmul(yp[j % 2][:, :], c["C_T"][:, j * P:(j + 1) * P],
                                     state[:, bass.ds(q * BLK, BLK)], start=True, stop=True
                                     ).then_inc(S["yp_ready"], 1)

            def outputs(g):
                pe.wait_ge(S["gated"], g * ECH + ECH)
                for t in range(TPB):
                    wait(pe, S["x_ready"], g * TPB + t - 1)
                    for j in range(ECH):
                        last = nc.tensor.matmul(op[t % 2][:, 0:DM], y[:, j, t * P:(t + 1) * P], c["w_out"][:, j, :],
                                                start=j == 0, stop=j == ECH - 1)
                    last.then_inc(S["op_ready"], 1)

            for half in range(HALF):
                g0 = half * HB
                inputs(g0)
                state_inputs(g0, 0)
                with pe.Fori(1, HB) as q:
                    inputs(q + g0)
                    state_inputs(q + g0, q)
                direct(half, g0, 0)
                outputs(g0)
                with pe.Fori(1, HB) as q:
                    direct(half, q + g0, q)
                    outputs(q + g0)

        @block.scalar
        def _(act):
            def inputs(g, q):
                cols = bass.ds(q * BLK, BLK)
                for e in range(E2):
                    act.wait_ge(S["proj_ready"], g * E2 + e + 1)
                    src = proj[e % 2][:, :]
                    if e < ECH:
                        wait(act, S["conv_ready"], g * ECH + e - 1)
                        dst, f = xpad[e % 2][:, :, TAPS - 1:TAPS - 1 + SEQ], ACT.Identity
                        src = src.rearrange("p (b s) -> p b s", s=SEQ)
                    else:
                        dst, f = gate[:, e - ECH, cols], ACT.Sigmoid
                    nc.scalar.activation(dst, src, f, bias=c["cols"][:, e:e + 1]).then_inc(S["proj_read"], 1)

            def state_inputs(g, q):
                act.wait_ge(S["up_ready"], g + 1)
                nc.scalar.activation(state[0:NS, bass.ds(q * BLK, BLK)], up[:, :], ACT.Copy).then_inc(S["u_ready"], 1)

            hs = state[0:NS, :].rearrange("n (b s) -> n b s", s=SEQ)
            act.wait_ge(S["padded"], 3)
            for half in range(HALF):
                g0 = half * HB
                if half:
                    act.wait_ge(S["yp_ready"], g0 * ECH)
                    act.wait_ge(S["gated"], g0 * ECH)
                inputs(g0, 0)
                state_inputs(g0, 0)
                with act.Fori(1, HB) as q:
                    inputs(q + g0, q)
                    state_inputs(q + g0, q)
                act.wait_ge(S["u_ready"], g0 + HB)
                nc.scalar.activation(hs[:, :, 0], hs[:, :, 0], ACT.Tanh).then_inc(S["h_ready"], 1)
                with act.Fori(1, SEQ) as s:
                    act.wait_ge(S["sum_ready"], s + half * (SEQ - 1))
                    nc.scalar.activation(hs[:, :, bass.ds(s, 1)].rearrange("n b s -> n (b s)"), step_sum[:, :], ACT.Tanh
                                         ).then_inc(S["h_ready"], 1)

        @block.gpsimd
        def _(pool):
            pool.memset(state[:, :], 0.0).then_inc(S["padded"], 1)
            pool.memset(xpad[0][:, :, 0:TAPS - 1], 0.0).then_inc(S["padded"], 1)
            pool.memset(xpad[1][:, :, 0:TAPS - 1], 0.0).then_inc(S["padded"], 1)
            pool.tensor_tensor(c["x_tok"][:, :, :], c["x_tok"][:, :, :],
                               c["b_out"][:, :].unsqueeze(1).to_broadcast([P, NT, DM]), ALU.add
                               ).then_inc(S["biased"], 1)

            def gated(g, q):
                for j in range(ECH):
                    pool.wait_ge(S["dir_ready"], g * ECH + j + 1)
                    nc.gpsimd.tensor_tensor(y[:, j, :], y[:, j, :], gate[:, j, bass.ds(q * BLK, BLK)], ALU.mult
                                            ).then_inc(S["gated"], 1)

            for half in range(HALF):
                g0 = half * HB
                gated(g0, 0)
                with pool.Fori(1, HB) as q:
                    gated(q + g0, q)

        @block.vector
        def _(dve):
            dve.wait_ge(S["padded"], 3)
            cv = c["cols"]

            def convolution(g, q):
                for j in range(ECH):
                    dve.wait_ge(S["proj_read"], g * E2 + j + 1)
                    acc = conv_sum[:, :, :]
                    dst = conv[:, j, bass.ds(q * BLK, BLK)].rearrange("p (b s) -> p b s", s=SEQ)
                    tap = [cv[:, 12 + j * TAPS + i:13 + j * TAPS + i] for i in range(TAPS)]
                    wait(dve, S["conv_ready"], g * ECH + j)
                    nc.vector.tensor_scalar(acc, xpad[j % 2][:, :, 0:SEQ], tap[0], cv[:, 8 + j:9 + j], ALU.mult, ALU.add
                                            ).then_inc(S["conv_step"], 1)
                    for i in range(1, TAPS):
                        dve.wait_ge(S["conv_step"], (g * ECH + j) * (TAPS - 1) + i)
                        ins = nc.vector.scalar_tensor_tensor(
                            out=dst if i == TAPS - 1 else acc, in0=xpad[j % 2][:, :, i:i + SEQ], scalar=tap[i],
                            in1=acc, op0=ALU.mult, op1=ALU.add)
                        ins.then_inc(S["conv_ready"] if i == TAPS - 1 else S["conv_step"], 1)

            def direct(g, q):
                for j in range(ECH):
                    dve.wait_ge(S["yp_ready"], g * ECH + j + 1)
                    wait(dve, S["op_ready"], g * TPB)
                    nc.vector.scalar_tensor_tensor(
                        out=y[:, j, :], in0=conv[:, j, bass.ds(q * BLK, BLK)], scalar=cv[:, 28 + j:29 + j],
                        in1=yp[j % 2][:, :], op0=ALU.mult, op1=ALU.add).then_inc(S["dir_ready"], 1)

            def outputs(g):
                for t in range(TPB):
                    ti = g * TPB + t
                    dve.wait_ge(S["op_ready"], ti + 1)
                    xt = c["x_tok"][:, bass.ds(ti, 1), :].rearrange("p a d -> p (a d)")
                    nc.vector.tensor_tensor(xt, op[t % 2][:, 0:DM], xt, ALU.add).then_inc(S["x_ready"], 1)
                    dve.wait_ge(S["x_ready"], ti + 1)
                    settle(nc, spot[0:1, (t % 2) * 2:(t % 2) * 2 + 1])
                    nc.vector.bn_stats(stats[:, :], xt).then_inc(S["stat_step"], 1)
                    dve.wait_ge(S["stat_step"], ti * 3 + 1)
                    settle(nc, spot[0:1, (t % 2) * 2 + 1:(t % 2) * 2 + 2])
                    nc.vector.bn_aggr(mv_tile[:, :], stats[:, :]).then_inc(S["stat_step"], 1)
                    dve.wait_ge(S["stat_step"], ti * 3 + 2)
                    nc.vector.tensor_copy(c["mv"][:, bass.ds(ti, 1), :].rearrange("p a d -> p (a d)"), mv_tile[:, :]
                                          ).then_inc(S["stat_step"], 1)

            hs = state[0:NS, :].rearrange("n (b s) -> n b s", s=SEQ)
            for half in range(HALF):
                g0 = half * HB
                convolution(g0, 0)
                with dve.Fori(1, HB) as q:
                    convolution(q + g0, q)
                with dve.Fori(1, SEQ) as s:
                    dve.wait_ge(S["h_ready"], s + half * SEQ)
                    nc.vector.tensor_tensor(step_sum[:, :], hs[:, :, bass.ds(s, 1)].rearrange("n b s -> n (b s)"),
                                            hs[:, :, bass.ds(s - 1, 1)].rearrange("n b s -> n (b s)"), ALU.add
                                            ).then_inc(S["sum_ready"], 1)
                dve.wait_ge(S["biased"], 1)
                direct(g0, 0)
                outputs(g0)
                with dve.Fori(1, HB) as q:
                    direct(q + g0, q)
                    outputs(q + g0)
            dve.wait_ge(S["stat_step"], NT * 3)


def routing(nc, a, c, xTh, xTl):
    with ExitStack() as ctx:
        m = Mem(nc, ctx, "rt")
        gw_raw = m.sb("gw_raw", [P, CH, P])
        gwh, gwl = m.sb("gwh", [P, CH, P], F32R), m.sb("gwl", [P, CH, P], F32R)
        e_bias = m.sb("e_bias", [P, NE])
        logT = m.sb("logT", [NE, TOK])
        score, choice = m.sb("score", [P, NT, NE]), m.sb("choice", [P, NT, NE])
        beats = m.sb("beats", [P, NT, NE])
        rank, grank = m.sb("rank", [P, NT, NE]), m.sb("grank", [P, NT, NG])
        pair = [m.sb(f"pair{i}", [P, NT, NG]) for i in range(8)]
        norm = [m.sb(f"norm{i}", [P, NT]) for i in range(2)]
        weight = m.sb("weight", [P, NT, NE])
        lg = [m.ps(f"lg{i}") for i in range(2)]
        tk = m.ps("tk")
        wp = [m.ps(f"wp{i}") for i in range(2)]
        S = {k: m.sem(k) for k in ("gw_in", "bias_in", "zeroed", "gw_ready", "lg_ready", "logT_ready", "tk_ready",
                                   "score_ready", "chain", "weight_ready", "wp_ready", "wh_ready", "wl_ready")}
        block = ctx.enter_context(nc.Block())

        @block.sync
        def _(sp):
            sp.wait_ge(S["zeroed"], 1)
            sp.dma_start(gw_raw[:, :, 0:NE], a["gate_wT"].rearrange("(c p) n -> p c n", p=P)).then_inc(S["gw_in"], 16)
            sp.dma_start(e_bias[:, :], a["e_bias"]).then_inc(S["bias_in"], 16)

        @block.gpsimd
        def _(pool):
            pool.memset(gw_raw[:, :, :], 0.0).then_inc(S["zeroed"], 1)
            for i in range(NG):
                last = pool.memset(grank[:, :, i:i + 1], float(NG - 1 - i))
            for i in range(NE):
                last = pool.memset(rank[:, :, i:i + 1], float(NE - 1 - i))
            last.then_inc(S["zeroed"], 1)
            pool.memset(c["wT"][:, :].bitcast(F32), 0.0).then_inc(S["zeroed"], 1)
            pool.memset(c["eye"][:, :], 0.0).then_inc(S["zeroed"], 1)
            pool.wait_ge(S["zeroed"], 4)
            pool.memset(c["wT"][0:NE + 1, :].bitcast(F32), 1.0).then_inc(S["zeroed"], 1)
            pool.affine_select(out=c["eye"][:, 1:], in_=c["eye"][:, 1:], compare_op=ALU.not_equal, fill=1.0,
                               base=0, pattern=[[-1, NE]], channel_multiplier=1).then_inc(S["zeroed"], 1)
            pool.wait_ge(S["zeroed"], 6)
            pool.affine_select(out=c["eye"][:, 1:], in_=c["eye"][:, 1:], compare_op=ALU.not_equal, fill=1.0,
                               base=-32, pattern=[[-1, NE]], channel_multiplier=1).then_inc(S["zeroed"], 1)
            pool.wait_ge(S["zeroed"], 7)
            pool.affine_select(out=c["eye"][:, 0:1], in_=c["eye"][:, 0:1], compare_op=ALU.not_equal, fill=1.0,
                               base=-NE, pattern=[[0, 1]], channel_multiplier=1).then_inc(S["zeroed"], 1)
            pool.wait_ge(S["zeroed"], 8)

        @block.tensor
        def _(pe):
            pe.wait_ge(S["gw_ready"], 2)
            for n in range(NB):
                wait(pe, S["logT_ready"], n - 1)
                for ci in range(CH):
                    cols = slice(n * BLK, (n + 1) * BLK)
                    last = split_matmul(nc, lg[n % 2][:, :], (gwh[:, ci, :], gwl[:, ci, :]),
                                        (xTh[:, ci, cols], xTl[:, ci, cols]), ci == 0, ci == CH - 1)
                last.then_inc(S["lg_ready"], 1)
            pe.wait_ge(S["logT_ready"], NB)
            for t in range(NT):
                last = nc.tensor.transpose(tk[:, t * NE:(t + 1) * NE], logT[:, t * P:(t + 1) * P],
                                           c["ident"][0:NE, 0:NE])
            last.then_inc(S["tk_ready"], 1)
            pe.wait_ge(S["weight_ready"], 1)
            for n in range(NB):
                wait(pe, S["wl_ready"], n - 1)
                for t in range(TPB):
                    last = nc.tensor.transpose(wp[n % 2][0:NE, t * P:(t + 1) * P], weight[:, n * TPB + t, :],
                                               c["ident"][:, :])
                last.then_inc(S["wp_ready"], 1)

        @block.scalar
        def _(act):
            for n in range(NB):
                act.wait_ge(S["lg_ready"], n + 1)
                nc.scalar.activation(logT[:, n * BLK:(n + 1) * BLK], lg[n % 2][0:NE, :], ACT.Copy
                                     ).then_inc(S["logT_ready"], 1)
            act.wait_ge(S["tk_ready"], 1)
            nc.scalar.activation(score[:, :, :].rearrange("p t e -> p (t e)"), tk[:, :], ACT.Sigmoid
                                 ).then_inc(S["score_ready"], 1)
            act.wait_ge(S["zeroed"], 8)
            for n in range(NB):
                act.wait_ge(S["wp_ready"], n + 1)
                nc.scalar.activation(c["wT"][0:NE, n * BLK:(n + 1) * BLK], wp[n % 2][0:NE, :], ACT.Copy
                                     ).then_inc(S["wh_ready"], 1)

        @block.vector
        def _(dve):
            ch = Chain(dve, S["chain"])
            dve.wait_ge(S["gw_in"], 16)
            nc.vector.tensor_copy(gwh[:, :, :], gw_raw[:, :, :]).then_inc(S["gw_ready"], 1)
            dve.wait_ge(S["gw_ready"], 1)
            nc.vector.tensor_tensor(gwl[:, :, :], gw_raw[:, :, :], gwh[:, :, :].bitcast(F32), ALU.subtract
                                    ).then_inc(S["gw_ready"], 1)
            dve.wait_ge(S["score_ready"], 1)
            dve.wait_ge(S["bias_in"], 16)
            dve.wait_ge(S["zeroed"], 8)
            tt = nc.vector.tensor_tensor
            ch.link(tt(choice[:, :, :], score[:, :, :], e_bias[:, :].unsqueeze(1).to_broadcast([P, NT, NE]), ALU.add))
            four = [choice[:, :, :].rearrange("p t (g i) -> p t g i", i=PG)[:, :, :, i] for i in range(PG)]
            q = [x[:, :, :] for x in pair]
            ch.add(tt(q[0], four[0], four[1], ALU.max))
            ch.add(tt(q[1], four[0], four[1], ALU.min))
            ch.add(tt(q[2], four[2], four[3], ALU.max))
            ch.link(tt(q[3], four[2], four[3], ALU.min))
            ch.add(tt(q[4], q[0], q[2], ALU.max))
            ch.add(tt(q[5], q[0], q[2], ALU.min))
            ch.link(tt(q[6], q[1], q[3], ALU.max))
            ch.link(tt(q[7], q[5], q[6], ALU.max))
            ch.link(tt(q[0], q[4], q[7], ALU.add))

            def ranks(value, place, n):
                for d in range(1, n):
                    b = beats[:, :, 0:n - d]
                    ch.link(tt(b, value[:, :, 0:n - d], value[:, :, d:n], ALU.is_ge))
                    ch.link(tt(place[:, :, d:n], place[:, :, d:n], b, ALU.add))
                    ch.link(tt(place[:, :, 0:n - d], place[:, :, 0:n - d], b, ALU.subtract))

            ranks(q[0], grank, NG)
            ch.link(nc.vector.tensor_scalar(q[1], grank[:, :, :], 2.0, None, ALU.is_lt))
            ch.link(tt(choice[:, :, :].rearrange("p t (g i) -> p (t g) i", i=PG),
                       choice[:, :, :].rearrange("p t (g i) -> p (t g) i", i=PG),
                       pair[1][:, :, :].rearrange("p t g -> p (t g)").unsqueeze(2).to_broadcast([P, NT * NG, PG]),
                       ALU.mult))
            ranks(choice, rank, NE)
            ch.link(nc.vector.tensor_scalar(beats[:, :, :], rank[:, :, :], 4.0, None, ALU.is_lt))
            ch.link(tt(weight[:, :, :], score[:, :, :], beats[:, :, :], ALU.mult))
            ch.link(nc.vector.reduce_sum(norm[0][:, :], weight[:, :, :], AX))
            ch.link(nc.vector.tensor_scalar(norm[0][:, :], norm[0][:, :], 1e-20, None, ALU.add))
            ch.link(nc.vector.reciprocal(norm[1][:, :], norm[0][:, :]))
            ch.link(tt(weight[:, :, :], weight[:, :, :], norm[1][:, :].unsqueeze(2).to_broadcast([P, NT, NE]), ALU.mult))
            nc.vector.tensor_scalar(weight[:, :, :], weight[:, :, :], 2.5, None, ALU.mult).then_inc(S["weight_ready"], 1)
            for n in range(NB):
                dve.wait_ge(S["wh_ready"], n + 1)
                cols = slice(n * BLK, (n + 1) * BLK)
                tt(c["wT"][32:32 + NE, cols], wp[n % 2][0:NE, :], c["wT"][0:NE, cols].bitcast(F32), ALU.subtract
                   ).then_inc(S["wl_ready"], 1)
            dve.wait_ge(S["wl_ready"], NB)


def experts(nc, a, c, xTh, xTl, out):
    with ExitStack() as ctx:
        m = Mem(nc, ctx, "ex")
        WG, WD = 2 * CH * P, DM
        w_raw = [m.sb(f"w_raw{i}", [P, WG + WD]) for i in range(2)]
        w_hi = [m.sb(f"w_hi{i}", [P, WG + WD], F32R) for i in range(2)]
        w_lo = [m.sb(f"w_lo{i}", [P, WG + WD], F32R) for i in range(2)]
        row = [m.sb(f"row{i}", [48, P], F32R) for i in range(2)]
        act_g = m.sb("act_g", [P, BLK])
        gu = m.sb("gu", [P, BLK])
        h = [m.sb(f"h{i}", [P, BLK]) for i in range(2)]
        h_hi = [m.sb(f"h_hi{i}", [P, BLK], F32R) for i in range(2)]
        h_lo = [m.sb(f"h_lo{i}", [P, BLK], F32R) for i in range(2)]
        gp = [m.ps(f"gp{i}") for i in range(2)]
        up = [m.ps(f"up{i}") for i in range(2)]
        wp = [m.ps(f"wp{i}") for i in range(2)]
        yp = m.ps("yp", (P, TPB, DM))
        S = {k: m.sem(k) for k in ("w_in0", "w_in1", "w_hi_ready", "w_lo_ready", "row_ready", "g_ready", "u_ready", "wp_ready",
                                   "act_ready", "gu_ready", "h_ready", "h_hi_ready", "h_lo_ready",
                                   "y_ready", "x_ready", "stored")}
        N = NE + 1
        block = ctx.enter_context(nc.Block())

        def over_experts(eng, start, first, other, end):
            def expert(e, par):
                first(e, par)
                other(e, 1, par, 1)
                with eng.Fori(1, NB // 2) as k:
                    other(e, k * 2, par, 0)
                    other(e, k * 2 + 1, par, 1)
            start()
            expert(0, 0)
            with eng.Fori(0, NE // 2) as k:
                expert(k * 2 + 1, 1)
                expert(k * 2 + 2, 0)
            end()

        def of(e, b):
            return e * NB + b

        @block.sync
        def _(sp):
            def load(e, par):
                if not isinstance(e, int):
                    e = sp.snap(e)
                wait(sp, S["w_lo_ready"], e - 1)
                sp.dma_start(w_raw[par][:, :], a["w_exp"][bass.ds(e, 1), :, :].rearrange("a p n -> (a p) n")
                             ).then_inc(S[f"w_in{par}"], 16)
            load(0, 0)
            load(1, 1)
            with sp.Fori(1, NE // 2) as k:
                load(k * 2, 0)
                load(k * 2 + 1, 1)
            load(NE, 0)
            for b in range(NB):
                sp.wait_ge(S["x_ready"], of(NE, b) + 1)
                sp.dma_start(out[b * BLK:(b + 1) * BLK, :].rearrange("(t p) d -> p t d", p=P),
                             c["x_tok"][:, b * TPB:(b + 1) * TPB, :]).then_inc(S["stored"], 16)
            sp.wait_ge(S["stored"], NB * 16)

        @block.tensor
        def _(pe):
            def up_products(e, b, par, bpar):
                i = of(e, b)
                wait(pe, S["act_ready"], i - 1)
                wait(pe, S["gu_ready"], i - 1)
                wait(pe, S["h_ready"], i - 1)
                cols = bass.ds(b * BLK, BLK)
                for kind, bank, done in ((0, gp[bpar], "g_ready"), (1, up[bpar], "u_ready")):
                    for ci in range(CH):
                        w0 = (kind * CH + ci) * P
                        last = split_matmul(nc, bank[:, :], (w_hi[par][:, w0:w0 + P], w_lo[par][:, w0:w0 + P]),
                                            (xTh[:, ci, cols], xTl[:, ci, cols]), ci == 0, ci == CH - 1)
                    last.then_inc(S[done], 1)
                nc.tensor.matmul(wp[bpar][:, :], row[par][:, :], c["wT"][:, cols], start=True, stop=True
                                 ).then_inc(S["wp_ready"], 1)

            def down_product(i, par, bpar):
                pe.wait_ge(S["h_hi_ready"], i + 1)
                pe.wait_ge(S["h_lo_ready"], i + 1)
                wait(pe, S["x_ready"], i)
                for t in range(TPB):
                    hs = slice(t * P, (t + 1) * P)
                    last = split_matmul(nc, yp[:, t, :], (h_hi[bpar][:, hs], h_lo[bpar][:, hs]),
                                        (w_hi[par][:, WG:WG + WD], w_lo[par][:, WG:WG + WD]), True, True)
                last.then_inc(S["y_ready"], 1)

            def first(e, par):
                pe.wait_ge(S["w_lo_ready"], e + 1)
                pe.wait_ge(S["row_ready"], e + 1)
                up_products(e, 0, par, 0)
                if not (isinstance(e, int) and e == 0):
                    down_product(of(e, 0) - 1, 1 - par, 1)

            def other(e, b, par, bpar):
                up_products(e, b, par, bpar)
                down_product(of(e, b) - 1, par, 1 - bpar)

            over_experts(pe, lambda: None, first, other, lambda: down_product(N * NB - 1, 0, 1))

        @block.scalar
        def _(act):
            def split(e, par):
                act.wait_ge(S["w_in%d" % par], pair_of(e) * 16)
                wait(act, S["y_ready"], (e - 1) * NB)
                nc.scalar.activation(w_hi[par][:, :], w_raw[par][:, :], ACT.Copy).then_inc(S["w_hi_ready"], 1)

            def block_of(i, bpar):
                act.wait_ge(S["g_ready"], i + 1)
                wait(act, S["gu_ready"], i)
                nc.scalar.activation(act_g[:, :], gp[bpar][:, :], ACT.Silu).then_inc(S["act_ready"], 1)
                act.wait_ge(S["h_ready"], i + 1)
                wait(act, S["y_ready"], i - 1)
                nc.scalar.activation(h_hi[bpar][:, :], h[bpar][:, :], ACT.Copy).then_inc(S["h_hi_ready"], 1)

            def pair_of(e):
                return e // 2 + 1 if isinstance(e, int) else half[0] + 1

            half = [0]

            def expert(e, par, more=True):
                block_of(of(e, 0), 0)
                block_of(of(e, 1), 1)
                if more:
                    split(e + 1, 1 - par)
                with act.Fori(1, NB // 2) as k:
                    block_of(of(e, 0) + k * 2, 0)
                    block_of(of(e, 0) + k * 2 + 1, 1)

            split(0, 0)
            expert(0, 0)
            with act.Fori(0, NE // 2 - 1) as k:
                half[0] = k + 1
                expert(k * 2 + 1, 1)
                half[0] = k + 1
                expert(k * 2 + 2, 0)
            expert(NE - 1, 1)
            expert(NE, 0, False)

        @block.gpsimd
        def _(pool):
            def low(i, bpar):
                pool.wait_ge(S["h_hi_ready"], i + 1)
                nc.gpsimd.tensor_tensor(h_lo[bpar][:, :], h[bpar][:, :], h_hi[bpar][:, :].bitcast(F32), ALU.subtract
                                        ).then_inc(S["h_lo_ready"], 1)

            with pool.Fori(0, N * NB // 2) as k:
                low(k * 2, 0)
                low(k * 2 + 1, 1)

        @block.vector
        def _(dve):
            def prepare(e, par):
                wait(dve, S["y_ready"], (e - 1) * NB)
                nc.vector.tensor_copy(row[par][:, :], c["eye"][:, bass.ds(e, 1)].to_broadcast([48, P])
                                      ).then_inc(S["row_ready"], 1)
                dve.wait_ge(S["w_hi_ready"], e + 1)
                nc.vector.tensor_tensor(w_lo[par][:, :], w_raw[par][:, :], w_hi[par][:, :].bitcast(F32), ALU.subtract
                                        ).then_inc(S["w_lo_ready"], 1)

            def hidden(i, bpar):
                dve.wait_ge(S["act_ready"], i + 1)
                dve.wait_ge(S["u_ready"], i + 1)
                nc.vector.tensor_tensor(gu[:, :], act_g[:, :], up[bpar][:, :], ALU.mult).then_inc(S["gu_ready"], 1)
                dve.wait_ge(S["gu_ready"], i + 1)
                dve.wait_ge(S["wp_ready"], i + 1)
                wait(dve, S["h_lo_ready"], i - 1)
                nc.vector.tensor_tensor(h[bpar][:, :], gu[:, :], wp[bpar][:, :], ALU.mult).then_inc(S["h_ready"], 1)

            def add(e, i, b):
                dve.wait_ge(S["y_ready"], i + 1)
                xt = c["x_tok"][:, bass.ds(b * TPB, TPB), :]
                nc.vector.tensor_tensor(xt, yp[:, :, :], xt, ALU.add).then_inc(S["x_ready"], 1)

            def expert(e, par, more=True):
                i0 = of(e, 0)
                hidden(i0, 0)
                if not (isinstance(e, int) and e == 0):
                    add(e, i0 - 1, NB - 1)
                hidden(i0 + 1, 1)
                add(e, i0, 0)
                if more:
                    prepare(e + 1, 1 - par)
                with dve.Fori(1, NB // 2) as k:
                    hidden(i0 + k * 2, 0)
                    add(e, i0 + k * 2 - 1, k * 2 - 1)
                    hidden(i0 + k * 2 + 1, 1)
                    add(e, i0 + k * 2, k * 2)

            prepare(0, 0)
            expert(0, 0)
            with dve.Fori(0, NE // 2 - 1) as k:
                expert(k * 2 + 1, 1)
                expert(k * 2 + 2, 0)
            expert(NE - 1, 1)
            expert(NE, 0, False)
            add(NE, N * NB - 1, NB - 1)


def build(nc, a, out):
    with ExitStack() as ctx:
        m = Mem(nc, ctx, "g")
        c = {"x_tok": m.sb("x_tok", [P, NT, DM]), "mv": m.sb("mv", [P, NT, 2]), "rstd": m.sb("rstd", [P, NT]),
             "ident": m.sb("ident", [P, P])}
        with ExitStack() as actx:
            ma = Mem(nc, actx, "c")
            for name, shape, dt in (
                    ("head_rows", [P, 8], F32), ("ones", [P, CH, 2, 4], F32), ("last_rows", [8, 8, 64], F32), ("odd_even", [P, 2], F32),
                    ("any_key", [P, 1], F32), ("mask_add", [P, KEYS], F32), ("b_qk", [P, 2, CH], F32),
                    ("b_v", [P, DM], F32), ("b_o", [P, DM], F32), ("w_o", [P, CH, DM], F32),
                    ("wv_raw", [P, CH, DM], F32), ("wh", [P, 3, CH, DM], F32R), ("wl", [P, 3, CH, DM], F32R),
                    ("qTh", [P, CH, TOK], F32R), ("qTl", [P, CH, TOK], F32R)):
                c[name] = ma.sb(name, shape, dt)
            set_up(nc, a, c)
            inverse_deviation(nc, "n1", c["mv"], c["rstd"])
            with ExitStack() as tctx:
                mt = Mem(nc, tctx, "xt1")
                xTh, xTl = mt.sb("xTh", [P, CH, TOK], F32R), mt.sb("xTl", [P, CH, TOK], F32R)
                normalise_and_transpose(nc, "nt1", c["x_tok"], c["mv"], c["rstd"], c["ident"], xTh, xTl)
                queries(nc, c, xTh, xTl)
            attention(nc, a, c)
        inverse_deviation(nc, "n2", c["mv"], c["rstd"])
        with ExitStack() as rctx:
            mr = Mem(nc, rctx, "r")
            for name, shape, dt in (
                    ("A", [P, ECH, NS], F32), ("C_T", [P, EI], F32), ("w_out", [P, ECH, DM], F32),
                    ("cols", [P, 32], F32), ("b_out", [P, DM], F32),
                    ("wih", [P, CH, 2 * EI], F32R), ("wil", [P, CH, 2 * EI], F32R)):
                c[name] = mr.sb(name, shape, dt)
            recurrent_inputs(nc, a, c)
            xTh, xTl = mr.sb("xTh", [P, CH, TOK], F32R), mr.sb("xTl", [P, CH, TOK], F32R)
            normalise_and_transpose(nc, "nt2", c["x_tok"], c["mv"], c["rstd"], c["ident"], xTh, xTl)
            recurrent(nc, c, xTh, xTl)
        inverse_deviation(nc, "n3", c["mv"], c["rstd"])
        with ExitStack() as ectx:
            me = Mem(nc, ectx, "e")
            xTh, xTl = me.sb("xTh", [P, CH, TOK], F32R), me.sb("xTl", [P, CH, TOK], F32R)
            c["wT"], c["eye"] = me.sb("wT", [48, TOK], F32R), me.sb("eye", [48, NE + 1])
            normalise_and_transpose(nc, "nt3", c["x_tok"], c["mv"], c["rstd"], c["ident"], xTh, xTl)
            routing(nc, a, c, xTh, xTl)
            experts(nc, a, c, xTh, xTl, out)


def kernel(**inputs):
    import numpy as np
    import concourse.bacc as bacc
    from concourse.bass_utils import run_bass_kernel_spmd as run

    def f(name):
        return np.asarray(inputs[name])

    def padded_bytes(v):
        return np.pad(v.view(np.uint8)[..., None], ((0, 0), (0, 0), (0, 3))).view(np.int32)[..., 0]

    def per_row(v, n):
        return v.reshape(n, P).T

    arrays = {
        "x": f("x").reshape(TOK, DM),
        "ctxT": f("ctx_1024").reshape(BATCH * KEYS, CH, P).transpose(2, 1, 0),
        "mask": padded_bytes(np.tile(f("mask_1x1xSxS2_bk0")[0, 0], (4, 1))),
        "Wq": f("L0_xattn_Wq"), "Wk": f("L0_xattn_Wk"), "Wv": f("L0_xattn_Wv"), "Wo": f("L0_xattn_Wo"),
        "b_qk": np.stack([per_row(f("L0_xattn_bq"), CH), per_row(f("L0_xattn_bk"), CH)], axis=1),
        "b_v": np.broadcast_to(f("L0_xattn_bv"), (P, DM)),
        "b_o": np.broadcast_to(f("L0_xattn_bo"), (P, DM)),
    }
    def transposed(w):
        return w.reshape(w.shape[0], P, CH, P).transpose(0, 3, 2, 1)

    gate, up, down = (np.concatenate([f(f"L0_ffn_shared_{s}")[None], f(f"L0_ffn_{r}")])
                      for s, r in (("gate_w", "gate_proj"), ("up_w", "up_proj"), ("down_w", "down_proj")))
    arrays |= {
        "W_in": f("L0_attn_W_in"), "A": f("L0_attn_A"), "C_T": np.pad(f("L0_attn_C").T, ((0, P - NS), (0, 0))), "W_out": f("L0_attn_W_out"),
        "b_out": np.broadcast_to(f("L0_attn_b_out"), (P, DM)),
        "cols": np.concatenate([per_row(f("L0_attn_b_in"), 8), per_row(f("L0_attn_conv_b"), ECH),
                                f("L0_attn_conv_w").reshape(ECH, P, TAPS).transpose(1, 0, 2).reshape(P, -1),
                                per_row(f("L0_attn_Dp"), ECH)], axis=1),
        "gate_wT": f("L0_ffn_gate_w").T, "e_bias": np.broadcast_to(f("L0_ffn_e_bias"), (P, NE)),
        "w_exp": np.concatenate([transposed(gate).reshape(NE + 1, P, -1), transposed(up).reshape(NE + 1, P, -1),
                                 down.transpose(0, 2, 1)], axis=2),
    }
    arrays = {f"in_{n}": np.ascontiguousarray(v) for n, v in arrays.items()}
    nc = bacc.Bacc("TRN2", target_bir_lowering=False, num_devices=1)
    a = {n[3:]: nc.dram_tensor(n, v.shape, mybir.dt.from_np(v.dtype), kind="ExternalInput").ap()
         for n, v in arrays.items()}
    out = nc.dram_tensor("out", (TOK, DM), F32, kind="ExternalOutput").ap()
    build(nc, a, out)
    r = run(nc, [arrays], core_ids=[0])
    return np.asarray(r.results[0]["out"]).reshape(BATCH, SEQ, DM)
```

```python
import concourse.bass as bass
from concourse import mybir
from concourse.alu_op_type import AluOpType as ALU
from contextlib import ExitStack

F32 = mybir.dt.float32
F32R = mybir.dt.float32r
ACT = mybir.ActivationFunctionType
AX = mybir.AxisListType.X

P = 128
BATCH, SEQ, DM = 128, 32, 256
KEYS = 257
HEADS, DK = 16, 16
TOK = BATCH * SEQ
NT = TOK // P
CH = DM // P
BLK = 512
NB = TOK // BLK
TPB = BLK // P
BPB = BLK // SEQ
EI = 512
ECH = EI // P
NS = 16
TAPS = 4
NE = 16
NG = 4
PG = NE // NG
EPS = 1e-5
NEG = -3.0e38
SCALE = 0.25
PAIRS = BATCH // 2
PK = 2 * KEYS
WIN = 258


def wait(eng, sem, count):
    if isinstance(count, int) and count <= 0:
        return
    eng.wait_ge(sem, count)


class Chain:

    def __init__(self, eng, sem):
        self.eng, self.sem, self.base, self.n = eng, sem, 0, 0

    def at(self, base):
        self.base, self.n = base, 0

    def add(self, ins):
        self.n += 1
        ins.then_inc(self.sem, 1)

    def sync(self):
        wait(self.eng, self.sem, self.base + self.n)

    def link(self, ins):
        self.add(ins)
        self.sync()


def settle(nc, spot):
    nc.vector.memset(spot, 0.0)


def split_matmul(nc, out, lhs, rhs, start, stop, **kw):
    nc.tensor.matmul(out, lhs[0], rhs[0], start=start, stop=False, **kw)
    nc.tensor.matmul(out, lhs[1], rhs[0], start=False, stop=False, **kw)
    return nc.tensor.matmul(out, lhs[0], rhs[1], start=False, stop=stop, **kw)


class Mem:

    def __init__(self, nc, ctx, tag):
        self.nc, self.ctx, self.tag = nc, ctx, tag

    def sb(self, name, shape, dt=F32):
        return self.ctx.enter_context(self.nc.sbuf_tensor(f"{self.tag}_{name}", shape, dt))

    def ps(self, name, shape=(P, 512)):
        return self.ctx.enter_context(self.nc.psum_tensor(f"{self.tag}_{name}", list(shape), F32))

    def sem(self, name):
        return self.ctx.enter_context(self.nc.semaphore(f"{self.tag}_{name}"))


def inverse_deviation(nc, tag, mv, rstd):
    with ExitStack() as ctx:
        m = Mem(nc, ctx, tag)
        ve, sd = m.sb("ve", [P, NT]), m.sb("sd", [P, NT])
        var_ready, sqrt_ready, rstd_ready = m.sem("var_ready"), m.sem("sqrt_ready"), m.sem("rstd_ready")
        block = ctx.enter_context(nc.Block())

        @block.vector
        def _(dve):
            nc.vector.tensor_scalar(ve[:, :], mv[:, :, 1], EPS, None, ALU.add).then_inc(var_ready, 1)
            dve.wait_ge(sqrt_ready, 1)
            nc.vector.reciprocal(rstd[:, :], sd[:, :]).then_inc(rstd_ready, 1)
            dve.wait_ge(rstd_ready, 1)

        @block.scalar
        def _(act):
            act.wait_ge(var_ready, 1)
            nc.scalar.activation(sd[:, :], ve[:, :], ACT.Sqrt).then_inc(sqrt_ready, 1)


def normalise_and_transpose(nc, tag, x_tok, mv, rstd, ident, xTh, xTl):
    with ExitStack() as ctx:
        m = Mem(nc, ctx, tag)
        xn = [m.sb(f"xn{i}", [P, TPB, DM]) for i in range(2)]
        tp = [m.ps(f"tp{i}", [P, CH, BLK]) for i in range(2)]
        xn_ready, tp_ready = m.sem("xn_ready"), m.sem("tp_ready")
        hi_ready, lo_ready = m.sem("hi_ready"), m.sem("lo_ready")
        block = ctx.enter_context(nc.Block())

        def normalise(dve, n, par):
            wait(dve, tp_ready, n - 1)
            for t in range(TPB):
                ti = n * TPB + t
                last = nc.vector.tensor_scalar(
                    xn[par][:, t, :], x_tok[:, bass.ds(ti, 1), :].rearrange("p a d -> p (a d)"),
                    mv[:, bass.ds(ti, 1), 0], rstd[:, bass.ds(ti, 1)], ALU.subtract, ALU.mult)
            last.then_inc(xn_ready, 1)

        def low_part(dve, n, par):
            dve.wait_ge(hi_ready, n + 1)
            cols = bass.ds(n * BLK, BLK)
            nc.vector.tensor_tensor(xTl[:, :, cols], tp[par][:, :, :], xTh[:, :, cols].bitcast(F32),
                                    ALU.subtract).then_inc(lo_ready, 1)

        @block.vector
        def _(dve):
            normalise(dve, 0, 0)
            normalise(dve, 1, 1)
            low_part(dve, 0, 0)
            with dve.Fori(0, NB // 2 - 1) as k:
                normalise(dve, k * 2 + 2, 0)
                low_part(dve, k * 2 + 1, 1)
                normalise(dve, k * 2 + 3, 1)
                low_part(dve, k * 2 + 2, 0)
            low_part(dve, NB - 1, 1)
            dve.wait_ge(lo_ready, NB)

        def transposes(pe, n, par):
            pe.wait_ge(xn_ready, n + 1)
            wait(pe, hi_ready, n - 1)
            wait(pe, lo_ready, n - 1)
            for c in range(CH):
                for t in range(TPB):
                    last = nc.tensor.transpose(tp[par][:, c, t * P:(t + 1) * P],
                                               xn[par][:, t, c * P:(c + 1) * P], ident[:, :])
            last.then_inc(tp_ready, 1)

        @block.tensor
        def _(pe):
            transposes(pe, 0, 0)
            transposes(pe, 1, 1)
            with pe.Fori(0, NB // 2 - 1) as k:
                transposes(pe, k * 2 + 2, 0)
                transposes(pe, k * 2 + 3, 1)

        @block.scalar
        def _(act):
            with act.Fori(0, NB // 2) as k:
                for par in range(2):
                    n = k * 2 + par
                    act.wait_ge(tp_ready, n + 1)
                    nc.scalar.activation(xTh[:, :, bass.ds(n * BLK, BLK)], tp[par][:, :, :],
                                         ACT.Copy).then_inc(hi_ready, 1)


def set_up(nc, a, c):
    with ExitStack() as ctx:
        m = Mem(nc, ctx, "set")
        w_raw = m.sb("w_raw", [P, 3, CH, DM])
        mask_i = m.sb("mask_i", [P, KEYS], mybir.dt.int32)
        mask_f = m.sb("mask_f", [P, KEYS])
        keep = m.sb("keep", [P, 3])
        stats = m.sb("stats", [P, NT, 6])
        x_in, w_in, b_in = m.sem("x_in"), m.sem("w_in"), m.sem("b_in")
        made, chain, aggr = m.sem("made"), m.sem("chain"), m.sem("aggr")
        block = ctx.enter_context(nc.Block())

        @block.sync
        def _(sp):
            sp.dma_start(c["x_tok"][:, :, :], a["x"].rearrange("(t p) d -> p t d", p=P)).then_inc(x_in, 16)
            for i, w in enumerate(("Wq", "Wk", "Wv")):
                sp.dma_start(w_raw[:, i, :, :], a[w].rearrange("(c p) n -> p c n", p=P)).then_inc(w_in, 16)
            sp.dma_start(c["w_o"][:, :, :], a["Wo"].rearrange("(c p) n -> p c n", p=P)).then_inc(b_in, 16)

        @block.scalar
        def _(act):
            act.dma_start(mask_i[:, :], a["mask"]).then_inc(b_in, 16)
            act.dma_start(c["b_qk"][:, :, :], a["b_qk"]).then_inc(b_in, 16)
            act.dma_start(c["b_v"][:, :], a["b_v"]).then_inc(b_in, 16)
            act.dma_start(c["b_o"][:, :], a["b_o"]).then_inc(b_in, 16)

        @block.gpsimd
        def _(pool):
            ch = Chain(pool, made)
            ch.add(pool.memset(c["ident"][:, :], 0.0))
            ch.add(pool.memset(c["head_rows"][:, :], 1.0))
            ch.sync()
            ch.link(pool.affine_select(out=c["ident"][:, :], in_=c["ident"][:, :], compare_op=ALU.not_equal,
                                       fill=1.0, base=0, pattern=[[-1, P]], channel_multiplier=1))
            ch.link(pool.affine_select(out=c["head_rows"][:, :], in_=c["head_rows"][:, :], compare_op=ALU.is_ge,
                                       fill=0.0, base=0, pattern=[[-DK, 8]], channel_multiplier=1))
            ch.link(pool.affine_select(out=c["head_rows"][:, :], in_=c["head_rows"][:, :], compare_op=ALU.is_ge,
                                       fill=0.0, base=DK - 1, pattern=[[DK, 8]], channel_multiplier=-1))

        @block.vector
        def _(dve):
            ch = Chain(dve, chain)
            dve.wait_ge(x_in, 16)
            with dve.Fori(0, NT // 4) as k:
                for i in range(4):
                    t = k * 4 + i
                    nc.vector.bn_stats(stats[:, bass.ds(t, 1), :].rearrange("p a d -> p (a d)"),
                                       c["x_tok"][:, bass.ds(t, 1), :].rearrange("p a d -> p (a d)")
                                       ).then_inc(aggr, 1)
            dve.wait_ge(aggr, NT)
            for t in range(NT):
                nc.vector.bn_aggr(c["mv"][:, t, :], stats[:, t, :]).then_inc(aggr, 1)
            dve.wait_ge(w_in, 48)
            ch.link(nc.vector.tensor_copy(c["wh"][:, :, :, :], w_raw[:, :, :, :]))
            ch.add(nc.vector.tensor_tensor(c["wl"][:, :, :, :], w_raw[:, :, :, :],
                                           c["wh"][:, :, :, :].bitcast(F32), ALU.subtract))
            dve.wait_ge(b_in, 80)
            ch.link(nc.vector.tensor_copy(mask_f[:, :], mask_i[:, :]))
            ch.link(nc.vector.tensor_scalar(c["mask_add"][:, :], mask_f[:, :], -NEG, NEG, ALU.mult, ALU.add))
            ch.link(nc.vector.reduce_sum(keep[:, 0:1], mask_f[:, :], AX))
            ch.link(nc.vector.reciprocal(keep[:, 1:2], keep[:, 0:1]))
            ch.link(nc.vector.tensor_scalar(keep[:, 2:3], keep[:, 1:2], 0.0, None, ALU.mult))
            ch.link(nc.vector.tensor_scalar(c["mask_add"][:, :], c["mask_add"][:, :], keep[:, 2:3], None, ALU.add))
            dve.wait_ge(made, 5)
            ch.link(nc.vector.tensor_reduce(c["odd_even"][:, :],
                                            c["head_rows"][:, :].rearrange("p (j e) -> p e j", e=2), AX, ALU.add))
            dve.wait_ge(aggr, 2 * NT)


def queries(nc, a, c, xTh, xTl):
    with ExitStack() as ctx:
        m = Mem(nc, ctx, "q")
        qp = [m.ps(f"qp{i}") for i in range(2)]
        vp = m.ps("vp")
        last_raw = m.sb("last_raw", [P, CH, BATCH])
        last_hi, last_lo = m.sb("last_hi", [P, CH, BATCH], F32R), m.sb("last_lo", [P, CH, BATCH], F32R)
        v_rows = m.sb("v_rows", [BATCH, 4, DM])
        S = {k: m.sem(k) for k in ("last_in", "rows_zero", "last_hi_ready", "last_lo_ready", "v_ready", "rows_ready",
                                   "rows_out")}
        q_ready, qh_ready, ql_ready, biased = m.sem("q_ready"), m.sem("qh_ready"), m.sem("ql_ready"), m.sem("biased")
        block = ctx.enter_context(nc.Block())

        @block.tensor
        def _(pe):
            pe.wait_ge(S["last_lo_ready"], 1)
            for ci in range(CH):
                last = split_matmul(nc, vp[:, 0:DM], (last_hi[:, ci, :], last_lo[:, ci, :]),
                                    (c["wh"][:, 2, ci, :], c["wl"][:, 2, ci, :]), ci == 0, ci == CH - 1)
            last.then_inc(S["v_ready"], 1)

            def block_of_queries(n):
                cols = bass.ds(n * BLK, BLK)
                for o in range(CH):
                    wait(pe, qh_ready, (n - 1) * CH + o + 1)
                    wait(pe, ql_ready, (n - 1) * CH + o + 1)
                    for ci in range(CH):
                        last = split_matmul(nc, qp[o][:, :], (c["wh"][:, 0, ci, o * P:(o + 1) * P],
                                                              c["wl"][:, 0, ci, o * P:(o + 1) * P]),
                                            (xTh[:, ci, cols], xTl[:, ci, cols]), ci == 0, ci == CH - 1)
                    last.then_inc(q_ready, 1)

            block_of_queries(0)
            with pe.Fori(1, NB) as n:
                block_of_queries(n)

        @block.scalar
        def _(act):
            with act.Fori(0, NB) as n:
                for o in range(CH):
                    act.wait_ge(q_ready, n * CH + o + 1)
                    nc.scalar.activation(c["qTh"][:, o, bass.ds(n * BLK, BLK)], qp[o][:, :], ACT.Identity,
                                         bias=c["b_qk"][:, 0, o:o + 1]).then_inc(qh_ready, 1)

        @block.sync
        def _(sp):
            sp.dma_start(last_raw[:, :, :], a["ctx_lastT"]).then_inc(S["last_in"], 16)
            sp.wait_ge(S["rows_ready"], 4)
            sp.dma_start(a["v_last"], v_rows[:, :, :]).then_inc(S["rows_out"], 16)
            sp.wait_ge(S["rows_out"], 16)

        @block.vector
        def _(dve):
            dve.wait_ge(S["last_in"], 16)
            nc.vector.tensor_copy(last_hi[:, :, :], last_raw[:, :, :]).then_inc(S["last_hi_ready"], 1)
            dve.wait_ge(S["last_hi_ready"], 1)
            nc.vector.tensor_tensor(last_lo[:, :, :], last_raw[:, :, :], last_hi[:, :, :].bitcast(F32), ALU.subtract
                                    ).then_inc(S["last_lo_ready"], 1)
            dve.wait_ge(S["rows_zero"], 1)
            dve.wait_ge(S["v_ready"], 1)
            for g in range(4):
                cols = slice(g * 64, (g + 1) * 64)
                nc.vector.tensor_tensor(v_rows[:, g, cols], vp[:, cols], c["b_v"][:, cols], ALU.add
                                        ).then_inc(S["rows_ready"], 1)
            with dve.Fori(0, NB) as n:
                for o in range(CH):
                    dve.wait_ge(qh_ready, n * CH + o + 1)
                    cols = bass.ds(n * BLK, BLK)
                    nc.vector.scalar_tensor_tensor(
                        out=c["qTl"][:, o, cols], in0=qp[o][:, :], scalar=c["b_qk"][:, 0, o:o + 1],
                        in1=c["qTh"][:, o, cols].bitcast(F32), op0=ALU.add, op1=ALU.subtract).then_inc(ql_ready, 1)
            dve.wait_ge(ql_ready, NB * CH)

        @block.gpsimd
        def _(pool):
            pool.memset(v_rows[:, :, :], 0.0).then_inc(S["rows_zero"], 1)
            pool.tensor_tensor(c["x_tok"][:, :, :], c["x_tok"][:, :, :],
                               c["b_o"][:, :].unsqueeze(1).to_broadcast([P, NT, DM]), ALU.add).then_inc(biased, 1)
            pool.wait_ge(biased, 1)


def attention(nc, a, c):
    with ExitStack() as ctx:
        m = Mem(nc, ctx, "at")
        ctx_raw = [m.sb(f"ctx_raw{i}", [P, CH, PK]) for i in range(2)]
        ctx_hi = [m.sb(f"ctx_hi{i}", [P, CH, PK], F32R) for i in range(2)]
        ctx_lo = [m.sb(f"ctx_lo{i}", [P, CH, PK], F32R) for i in range(2)]
        k_hi, k_lo = m.sb("k_hi", [P, CH, PK], F32R), m.sb("k_lo", [P, CH, PK], F32R)
        v_sb = [m.sb(f"v_sb{i}", [P, 2, 2, DM]) for i in range(2)]
        v_last = [m.sb(f"v_last{i}", [8, 2, DM]) for i in range(2)]
        q_hi = [m.sb(f"q_hi{i}", [P, CH, 8, SEQ], F32R) for i in range(2)]
        q_lo = [m.sb(f"q_lo{i}", [P, CH, 8, SEQ], F32R) for i in range(2)]
        prob = m.sb("prob", [P, 2, 4, KEYS])
        least = [m.sb(f"least{i}", [P, 4]) for i in range(2)]
        total = [m.sb(f"total{i}", [P, 4]) for i in range(2)]
        inv = [m.sb(f"inv{i}", [P, 4]) for i in range(2)]
        pT = [m.sb(f"pT{i}", [P, 2, 512]) for i in range(2)]
        p_last = m.sb("p_last", [8, P])
        o_even = [m.sb(f"o_even{i}", [P, CH, SEQ]) for i in range(2)]
        oT = m.sb("oT", [P, CH, P])
        spot = m.sb("spot", [1, 10])
        stats, mv_tile = m.sb("stats", [P, 6]), m.sb("mv_tile", [P, 2])

        proj = [m.ps(f"proj{i}") for i in range(3)]
        sc = [m.ps(f"sc{i}") for i in range(2)] + [proj[1]]
        tp = [m.ps(f"tp{i}") for i in range(2)]
        ob = m.ps("ob")
        o_ps = [ob[:, 0:P], proj[2][:, 0:P]]
        yb = ob[:, DM:2 * DM]
        last_ps = proj[0][0:8, 0:P]

        S = {k: m.sem(k) for k in (
            "ctx_in0", "ctx_in1", "ctx_hi_ready", "ctx_lo_ready", 
            "proj_ready", "k_hi_ready", "k_lo_ready", "v_ready", "v_last_in0", "v_last_in1", "v_last_zero",
            "q_ready", "s_ready", "masked", "exp_ready", "inv_ready", 
            "norm_ready", "t_ready", "t_last_ready", "pT0_ready", "pT1_ready", "p_last_ready",
            "av_ready", "oT_ready", "y_ready", "x_ready", "dve_chain")}

        NU = 6

        block = ctx.enter_context(nc.Block())

        def load(sp, n, par):
            if not isinstance(n, int):
                n = sp.snap(n)
            wait(sp, S["proj_ready"], (n - 1) * NU)
            sp.dma_start(ctx_raw[par][:, :, :], a["ctxT"][:, :, bass.ds(n * PK, PK)]
                         ).then_inc(S[f"ctx_in{par}"], 16)

        def load_last(eng, n, par):
            if not isinstance(n, int):
                n = eng.snap(n)
            wait(eng, S["av_ready"], n * 2 - 2)
            for b in range(2):
                eng.dma_start(v_last[par][4 * b:4 * b + 4, b, :],
                              a["v_last"][bass.ds(n * 2 + b, 1), :, :].rearrange("a g n -> (a g) n")
                              ).then_inc(S[f"v_last_in{par}"], 16)

        @block.sync
        def _(sp):
            load(sp, 0, 0)
            load(sp, 1, 1)
            sp.wait_ge(S["v_last_zero"], 2)
            load_last(sp, 0, 0)
            load_last(sp, 1, 1)
            with sp.Fori(1, PAIRS // 2) as k:
                load(sp, k * 2, 0)
                load_last(sp, k * 2, 0)
                load(sp, k * 2 + 1, 1)
                load_last(sp, k * 2 + 1, 1)

        def arrived(eng, n, par):
            eng.wait_ge(S[f"ctx_in{par}"], (n // 2 + 1 if isinstance(n, int) else turn[0] + 3 - par) * 16)

        def so_far(p, ppar):
            return p // 2 + 1 if isinstance(p, int) else turn[0] + 2 - ppar

        turn = [None]

        def pe_k(pe, n, par):
            pe.wait_ge(S["ctx_hi_ready"], n + 1)
            pe.wait_ge(S["ctx_lo_ready"], n + 1)
            for o in range(CH):
                for w, (lo, cols) in enumerate(((0, WIN), (WIN, PK - WIN))):
                    u = o * 2 + w
                    proj_free(pe, n, par, u)
                    bank = proj[u % 3]
                    for ci in range(CH):
                        last = split_matmul(nc, bank[:, 0:cols],
                                            (c["wh"][:, 1, ci, o * P:(o + 1) * P], c["wl"][:, 1, ci, o * P:(o + 1) * P]),
                                            (ctx_hi[par][:, ci, lo:lo + cols], ctx_lo[par][:, ci, lo:lo + cols]),
                                            ci == 0, ci == CH - 1)
                    last.then_inc(S["proj_ready"], 1)

        def proj_free(pe, n, par, u):
            if u == 0:
                wait(pe, S["k_lo_ready"], n * 4)
                wait(pe, S["p_last_ready"], n - 1)
            elif u == 1:
                wait(pe, S["masked"], n * 8 - 2)
            elif u == 2:
                wait(pe, S["oT_ready"], n * 2 - 2)
            else:
                wait(pe, S["k_lo_ready"], n * 4 + u - 2)

        def pe_v(pe, n, par):
            for b in range(2):
                u = 4 + b
                proj_free(pe, n, par, u)
                bank = proj[u % 3]
                for kt in range(2):
                    lo = b * KEYS + kt * P
                    for ci in range(CH):
                        last = split_matmul(nc, bank[:, kt * DM:(kt + 1) * DM],
                                            (ctx_hi[par][:, ci, lo:lo + P], ctx_lo[par][:, ci, lo:lo + P]),
                                            (c["wh"][:, 2, ci, :], c["wl"][:, 2, ci, :]), ci == 0, ci == CH - 1)
                last.then_inc(S["proj_ready"], 1)

        def pe_scores(pe, n, par, first, end):
            for i in range(first, end):
                b, g = i // 4, i % 4
                off = 0 if b == 0 else KEYS - 1
                if g == 0:
                    pe.wait_ge(S["q_ready"], n * 2 + b + 1)
                if i == 0:
                    pe.wait_ge(S["k_lo_ready"], n * 4 + 4)
                    wait(pe, S["masked"], n * 8 - 1)
                elif i == 1:
                    wait(pe, S["masked"], n * 8)
                elif i == 2:
                    pe.wait_ge(S["v_ready"], n * 2 + 1)
                else:
                    pe.wait_ge(S["masked"], n * 8 + i - 2)
                ci, q0 = g // 2, (g % 2) * P
                qh = q_hi[b][:, ci, :, :].rearrange("p h q -> p (h q)")[:, q0:q0 + P]
                ql = q_lo[b][:, ci, :, :].rearrange("p h q -> p (h q)")[:, q0:q0 + P]
                split_matmul(nc, sc[i % 3][:, 0:WIN], (qh, ql),
                             (k_hi[:, ci, off:off + WIN], k_lo[:, ci, off:off + WIN]), True, True
                             ).then_inc(S["s_ready"], 1)

        def pe_transposes(pe, p, b):
            pe.wait_ge(S["norm_ready"], p * 2 + b + 1)
            for kt in range(2):
                wait(pe, S[f"pT{kt}_ready"], p * 2 + b)
                for g in range(4):
                    last = nc.tensor.transpose(tp[kt][:, g * P:(g + 1) * P], prob[:, b, g, kt * P:(kt + 1) * P],
                                               c["ident"][:, :])
                last.then_inc(S["t_ready"], 1)

        def pe_last_transpose(pe, p, last_pair=False):
            pe.wait_ge(S["k_lo_ready"], p * 4 + 8 if not last_pair else p * 4 + 4)
            wait(pe, S["p_last_ready"], p)
            nc.tensor.transpose(last_ps, prob[:, :, :, KEYS - 1].rearrange("p b g -> p (b g)"), c["ident"][:, :]
                                ).then_inc(S["t_last_ready"], 1)

        def pe_av(pe, p, ppar, b, g):
            if g == 0:
                pe.wait_ge(S["pT0_ready"], p * 2 + b + 1)
                pe.wait_ge(S["pT1_ready"], p * 2 + b + 1)
                pe.wait_ge(S["p_last_ready"], p + 1)
                pe.wait_ge(S["v_ready"], p * 2 + b + 1)
                pe.wait_ge(S[f"v_last_in{ppar}"], so_far(p, ppar) * 32)
                wait(pe, S["oT_ready"], p * 2 + b - 1)
            for kt in range(3):
                for j in range(4):
                    h0 = g * 8 + 2 * j
                    hd = slice(g * P + 32 * j, g * P + 32 * j + 32)
                    out = o_ps[b][32 * j:32 * j + 32, g * 64:(g + 1) * 64]
                    if kt < 2:
                        last = nc.tensor.matmul(out, v_sb[ppar][:, b, kt, hd], pT[b][:, kt, h0 * SEQ:(h0 + 2) * SEQ],
                                                start=kt == 0, stop=False, tile_position=(0, 32 * j))
                    else:
                        q0 = (h0 % 4) * SEQ
                        last = nc.tensor.matmul(out, v_last[ppar][0:8, b, hd], p_last[0:8, q0:q0 + 2 * SEQ],
                                                start=False, stop=True, tile_position=(0, 32 * j))
            if g == CH - 1:
                last.then_inc(S["av_ready"], 1)

        def pe_out(pe, t):
            pe.wait_ge(S["oT_ready"], t * 4 + 4)
            wait(pe, S["x_ready"], t)
            for ci in range(CH):
                last = nc.tensor.matmul(yb, oT[:, ci, :], c["w_o"][:, ci, :], start=ci == 0, stop=ci == CH - 1)
            last.then_inc(S["y_ready"], 1)

        def pe_step(pe, n, par, t=None):
            pe_k(pe, n, par)
            if t is not None:
                pe_out(pe, t)
            later = not isinstance(n, int) or n > 0
            if later:
                pe_transposes(pe, n - 1, 0)
            pe_v(pe, n, par)
            if later:
                pe_transposes(pe, n - 1, 1)
                pe_last_transpose(pe, n - 1)
            done = 0
            for i, end in enumerate((3, 5, 7, 8)):
                pe_scores(pe, n, par, done, end)
                done = end
                if later:
                    pe_av(pe, n - 1, 1 - par, i // 2, i % 2)

        @block.tensor
        def _(pe):
            pe_step(pe, 0, 0)
            pe_step(pe, 1, 1)
            with pe.Fori(0, PAIRS // 2 - 1) as k:
                turn[0] = k
                pe_step(pe, k * 2 + 2, 0)
                pe_step(pe, k * 2 + 3, 1, k)
            pe_transposes(pe, PAIRS - 1, 0)
            pe_transposes(pe, PAIRS - 1, 1)
            pe_last_transpose(pe, PAIRS - 1, True)
            for b in range(2):
                for g in range(2):
                    pe_av(pe, PAIRS - 1, 1, b, g)
            pe_out(pe, NT - 1)

        def act_k(act, n, par, u):
            act.wait_ge(S["proj_ready"], n * NU + u + 1)
            if u == 0:
                wait(act, S["s_ready"], n * 8)
            o, w = u // 2, u % 2
            lo, cols = ((0, WIN), (WIN, PK - WIN))[w]
            nc.scalar.activation(k_hi[:, o, lo:lo + cols], proj[u % 3][:, 0:cols], ACT.Identity,
                                 bias=c["b_qk"][:, 1, o:o + 1]).then_inc(S["k_hi_ready"], 1)

        def act_ctx(act, n, par):
            arrived(act, n, par)
            wait(act, S["proj_ready"], (n - 1) * NU)
            nc.scalar.activation(ctx_hi[par][:, :, :], ctx_raw[par][:, :, :], ACT.Copy
                                 ).then_inc(S["ctx_hi_ready"], 1)

        def act_pT(act, p, b):
            act.wait_ge(S["t_ready"], p * 4 + b * 2 + 1)
            wait(act, S["av_ready"], p * 2 + b - 1)
            nc.scalar.activation(pT[b][:, 0, :], tp[0][:, :], ACT.Copy).then_inc(S["pT0_ready"], 1)

        def act_exp(act, n, b):
            wait(act, S["inv_ready"], n * 2 + b - 1)
            for g in range(4):
                act.wait_ge(S["masked"], n * 8 + b * 4 + g + 1)
                nc.scalar.activation(prob[:, b, g, :], prob[:, b, g, :], ACT.Exp, bias=least[b][:, g:g + 1],
                                     scale=-1.0, accum_out=total[b][:, g:g + 1]).then_inc(S["exp_ready"], 1)

        def act_norm(act, n, b, gs):
            if gs[0] == 0:
                act.wait_ge(S["inv_ready"], n * 2 + b + 1)
            for g in gs:
                last = nc.scalar.activation(prob[:, b, g, :], prob[:, b, g, :], ACT.Copy, scale=inv[b][:, g:g + 1])
            if gs[-1] == 3:
                last.then_inc(S["norm_ready"], 1)

        def act_step(act, n, par, more=True):
            later = not isinstance(n, int) or n > 0
            act_k(act, n, par, 0)
            if later:
                act_norm(act, n - 1, 0, (1, 2))
            act_k(act, n, par, 1)
            if later:
                act_norm(act, n - 1, 0, (3,))
            act_k(act, n, par, 2)
            act_k(act, n, par, 3)
            if later:
                act_norm(act, n - 1, 1, (0, 1))
                act_pT(act, n - 1, 0)
                act_norm(act, n - 1, 1, (2, 3))
                act_pT(act, n - 1, 1)
            if more:
                act_ctx(act, n + 1, 1 - par)
            act_exp(act, n, 0)
            act_exp(act, n, 1)
            act_norm(act, n, 0, (0,))

        @block.scalar
        def _(act):
            act_ctx(act, 0, 0)
            act_step(act, 0, 0)
            act_step(act, 1, 1)
            with act.Fori(0, PAIRS // 2 - 2) as k:
                turn[0] = k
                act_step(act, k * 2 + 2, 0)
                act_step(act, k * 2 + 3, 1)
            act_step(act, PAIRS - 2, 0)
            act_step(act, PAIRS - 1, 1, False)
            act_norm(act, PAIRS - 1, 0, (1, 2, 3))
            act_norm(act, PAIRS - 1, 1, (0, 1, 2, 3))
            act_pT(act, PAIRS - 1, 0)
            act_pT(act, PAIRS - 1, 1)

        def pool_ctx(pool, n, par):
            pool.wait_ge(S["ctx_hi_ready"], n + 1)
            nc.gpsimd.tensor_tensor(ctx_lo[par][:, :, :], ctx_raw[par][:, :, :], ctx_hi[par][:, :, :].bitcast(F32),
                                    ALU.subtract).then_inc(S["ctx_lo_ready"], 1)

        def pool_q(pool, n, b):
            wait(pool, S["s_ready"], n * 8 - 4 + b * 4)
            for src, dst in ((c["qTh"], q_hi[b]), (c["qTl"], q_lo[b])):
                q = src[:, :, bass.ds((n * 2 + b) * SEQ, SEQ)].bitcast(F32)
                last = nc.gpsimd.tensor_tensor(
                    dst[:, :, :, :], q.unsqueeze(2).to_broadcast([P, CH, 8, SEQ]),
                    c["head_rows"][:, :].unsqueeze(1).unsqueeze(3).to_broadcast([P, CH, 8, SEQ]), ALU.mult)
            last.then_inc(S["q_ready"], 1)

        def pool_step(pool, n, par, more=True):
            pool_q(pool, n, 0)
            pool_q(pool, n, 1)
            if more:
                pool_ctx(pool, n + 1, 1 - par)

        @block.gpsimd
        def _(pool):
            for i in range(2):
                pool.memset(v_last[i][:, :, :], 0.0).then_inc(S["v_last_zero"], 1)
            pool_ctx(pool, 0, 0)
            pool_q(pool, 0, 0)
            pool_q(pool, 0, 1)
            pool_ctx(pool, 1, 1)
            pool_step(pool, 1, 1)
            with pool.Fori(0, PAIRS // 2 - 2) as k:
                turn[0] = k
                pool_step(pool, k * 2 + 2, 0)
                pool_step(pool, k * 2 + 3, 1)
            pool_step(pool, PAIRS - 2, 0)
            pool_step(pool, PAIRS - 1, 1, False)

        def dve_k(dve, n, par, u):
            dve.wait_ge(S["k_hi_ready"], n * 4 + u + 1)
            o, w = u // 2, u % 2
            lo, cols = ((0, WIN), (WIN, PK - WIN))[w]
            nc.vector.scalar_tensor_tensor(
                out=k_lo[:, o, lo:lo + cols], in0=proj[u % 3][:, 0:cols],
                scalar=c["b_qk"][:, 1, o:o + 1], in1=k_hi[:, o, lo:lo + cols].bitcast(F32),
                op0=ALU.add, op1=ALU.subtract).then_inc(S["k_lo_ready"], 1)

        def dve_pT(dve, p, b):
            dve.wait_ge(S["t_ready"], p * 4 + b * 2 + 2)
            wait(dve, S["av_ready"], p * 2 + b - 1)
            nc.vector.tensor_copy(pT[b][:, 1, :], tp[1][:, :]).then_inc(S["pT1_ready"], 1)

        def dve_v(dve, n, par, b):
            dve.wait_ge(S["proj_ready"], n * NU + 5 + b)
            wait(dve, S["av_ready"], n * 2 - 2)
            nc.vector.tensor_tensor(v_sb[par][:, b, :, :], proj[(4 + b) % 3][:, :].rearrange("p (k n) -> p k n", k=2),
                                    c["b_v"][:, :].unsqueeze(1).to_broadcast([P, 2, DM]), ALU.add
                                    ).then_inc(S["v_ready"], 1)

        def dve_p_last(dve, p):
            dve.wait_ge(S["t_last_ready"], p + 1)
            wait(dve, S["av_ready"], p * 2)
            nc.vector.tensor_copy(p_last[:, :], last_ps).then_inc(S["p_last_ready"], 1)

        def dve_mask_max(dve, n, units):
            for i in units:
                b, g = i // 4, i % 4
                off = b
                if g == 0:
                    wait(dve, S["t_ready"], (n - 1) * 4 + b * 2 + 2)
                    wait(dve, S["t_last_ready"], n)
                    wait(dve, S["exp_ready"], n * 8 + b * 4 - 4)
                dve.wait_ge(S["s_ready"], n * 8 + i + 1)
                settle(nc, spot[0:1, i:i + 1])
                nc.vector.tensor_tensor_reduce(
                    out=prob[:, b, g, :], in0=sc[i % 3][:, off:off + KEYS], in1=c["mask_add"][:, :],
                    scale=-SCALE, scalar=-NEG, op0=ALU.add, op1=ALU.min, accum_out=least[b][:, g:g + 1]
                ).then_inc(S["masked"], 1)

        def dve_inv(dve, n, b):
            dve.wait_ge(S["exp_ready"], n * 8 + b * 4 + 4)
            wait(dve, S["norm_ready"], n * 2 + b - 1)
            nc.vector.reciprocal(inv[b][:, :], total[b][:, :]).then_inc(S["inv_ready"], 1)

        def dve_o_even(dve, ch, p, b):
            dve.wait_ge(S["av_ready"], p * 2 + b + 1)
            o = o_ps[b].rearrange("p (g e q) -> p g e q", g=CH, e=2)
            ch.add(nc.vector.tensor_scalar(o_even[b][:, :, :], o[:, :, 0, :], c["odd_even"][:, 0:1], None, ALU.mult))

        def dve_o(dve, ch, p, ppar, b):
            ch.sync()
            o = o_ps[b].rearrange("p (g e q) -> p g e q", g=CH, e=2)
            if b == 0 and ppar == 0:
                wait(dve, S["y_ready"], so_far(p, ppar) - 1)
            q0 = (ppar * 2 + b) * SEQ
            nc.vector.scalar_tensor_tensor(out=oT[:, :, q0:q0 + SEQ], in0=o[:, :, 1, :], scalar=c["odd_even"][:, 1:2],
                                           in1=o_even[b][:, :, :], op0=ALU.mult, op1=ALU.add
                                           ).then_inc(S["oT_ready"], 1)

        def dve_x(dve, ch, t, part):
            if t is None:
                return
            if part == 0:
                dve.wait_ge(S["y_ready"], t + 1)
                xt = c["x_tok"][:, bass.ds(t, 1), :].rearrange("p a d -> p (a d)")
                nc.vector.tensor_tensor(xt, yb, xt, ALU.add).then_inc(S["x_ready"], 1)
            elif part == 1:
                dve.wait_ge(S["x_ready"], t + 1)
                settle(nc, spot[0:1, 8:9])
                xt = c["x_tok"][:, bass.ds(t, 1), :].rearrange("p a d -> p (a d)")
                ch.add(nc.vector.bn_stats(stats[:, :], xt))
            elif part == 2:
                ch.sync()
                settle(nc, spot[0:1, 9:10])
                ch.add(nc.vector.bn_aggr(mv_tile[:, :], stats[:, :]))
            else:
                ch.sync()
                ch.add(nc.vector.tensor_copy(c["mv"][:, bass.ds(t, 1), :].rearrange("p a d -> p (a d)"), mv_tile[:, :]))

        def dve_step(dve, ch, n, par, t=None):
            later = not isinstance(n, int) or n > 0
            dve_k(dve, n, par, 0)
            if later:
                dve_inv(dve, n - 1, 1)
            dve_k(dve, n, par, 1)
            dve_k(dve, n, par, 2)
            dve_k(dve, n, par, 3)
            if later:
                dve_pT(dve, n - 1, 0)
            dve_x(dve, ch, t, 0)
            dve_v(dve, n, par, 0)
            dve_x(dve, ch, t, 1)
            dve_v(dve, n, par, 1)
            dve_x(dve, ch, t, 2)
            if later:
                dve_p_last(dve, n - 1)
            dve_mask_max(dve, n, (0, 1))
            if later:
                dve_pT(dve, n - 1, 1)
            dve_x(dve, ch, t, 3)
            dve_mask_max(dve, n, (2, 3, 4))
            if later:
                dve_o_even(dve, ch, n - 1, 0)
            dve_mask_max(dve, n, (5,))
            if later:
                dve_o(dve, ch, n - 1, 1 - par, 0)
            dve_mask_max(dve, n, (6, 7))
            dve_inv(dve, n, 0)
            if later:
                dve_o_even(dve, ch, n - 1, 1)
                dve_o(dve, ch, n - 1, 1 - par, 1)

        @block.vector
        def _(dve):
            ch = Chain(dve, S["dve_chain"])
            dve_step(dve, ch, 0, 0)
            dve_step(dve, ch, 1, 1)
            first = ch.n
            with dve.Fori(0, PAIRS // 2 - 2) as k:
                per = 2 * 2 + 3
                ch.at(k * per + first)
                turn[0] = k
                dve_step(dve, ch, k * 2 + 2, 0)
                dve_step(dve, ch, k * 2 + 3, 1, k)
                assert ch.n == per
            ch.at(first + per * (PAIRS // 2 - 2))
            dve_step(dve, ch, PAIRS - 2, 0)
            dve_step(dve, ch, PAIRS - 1, 1, NT - 2)
            dve_inv(dve, PAIRS - 1, 1)
            dve_pT(dve, PAIRS - 1, 0)
            dve_pT(dve, PAIRS - 1, 1)
            dve_p_last(dve, PAIRS - 1)
            for b in range(2):
                dve_o_even(dve, ch, PAIRS - 1, b)
                dve_o(dve, ch, PAIRS - 1, 1, b)
            for part in range(4):
                dve_x(dve, ch, NT - 1, part)
            ch.sync()


HALF = 2
HB = NB // HALF
HTOK = TOK // HALF
HBATCH = BATCH // HALF


def recurrent_inputs(nc, a, c):
    with ExitStack() as ctx:
        m = Mem(nc, ctx, "rin")
        raw = m.sb("raw", [P, CH, 2 * EI])
        w_in, rest_in, split = m.sem("w_in"), m.sem("rest_in"), m.sem("split")
        block = ctx.enter_context(nc.Block())

        @block.sync
        def _(sp):
            sp.dma_start(raw[:, :, :], a["W_in"].rearrange("(c p) n -> p c n", p=P)).then_inc(w_in, 16)
            for name, src in (("A", a["A"].rearrange("(c p) n -> p c n", p=P)), ("C_T", a["C_T"]),
                              ("w_out", a["W_out"].rearrange("(c p) n -> p c n", p=P)), ("cols", a["cols"]),
                              ("b_out", a["b_out"])):
                dst = c[name]
                sp.dma_start(dst[tuple([slice(None)] * len(dst.shape))], src).then_inc(rest_in, 16)
            sp.wait_ge(rest_in, 5 * 16)

        @block.vector
        def _(dve):
            dve.wait_ge(w_in, 16)
            nc.vector.tensor_copy(c["wih"][:, :, :], raw[:, :, :]).then_inc(split, 1)
            dve.wait_ge(split, 1)
            nc.vector.tensor_tensor(c["wil"][:, :, :], raw[:, :, :], c["wih"][:, :, :].bitcast(F32), ALU.subtract
                                    ).then_inc(split, 1)
            dve.wait_ge(split, 2)


def recurrent(nc, c, xTh, xTl):
    with ExitStack() as ctx:
        m = Mem(nc, ctx, "rec")
        xpad = [m.sb(f"xpad{i}", [P, BPB, SEQ + TAPS - 1]) for i in range(2)]
        conv = m.sb("conv", [P, ECH, HTOK])
        gate = m.sb("gate", [P, ECH, HTOK])
        state = m.sb("state", [P, HTOK])
        step_sum = m.sb("step_sum", [NS, HBATCH])
        y = m.sb("y", [P, ECH, BLK])
        spot = m.sb("spot", [1, 4])
        stats, mv_tile = m.sb("stats", [P, 6]), m.sb("mv_tile", [P, 2])
        proj = [m.ps(f"proj{i}") for i in range(2)]
        up = m.ps("up", (NS, 512))
        yp = [m.ps(f"yp{i}") for i in range(2)]
        op = [m.ps(f"op{i}") for i in range(2)]
        S = {k: m.sem(k) for k in ("proj_ready", "x_part", "gate_part", "conv_start", "padded", "conv_step", "conv_ready", "up_ready", "u_ready",
                                   "sum_ready", "h_ready", "yp_ready", "dir_ready", "gated", "op_ready", "x_ready",
                                   "biased", "stat_step")}
        block = ctx.enter_context(nc.Block())

        HY = BLK // 2

        @block.tensor
        def _(pe):
            def inputs(g, before=None):
                cols = bass.ds(g * BLK, BLK)
                for j in range(ECH):
                    for bank, e, read in ((0, j, "x_part"), (1, ECH + j, "gate_part")):
                        wait(pe, S[read], g * ECH + j)
                        for ci in range(CH):
                            last = split_matmul(nc, proj[bank][:, :], (c["wih"][:, ci, e * P:(e + 1) * P],
                                                                       c["wil"][:, ci, e * P:(e + 1) * P]),
                                                (xTh[:, ci, cols], xTl[:, ci, cols]), ci == 0, ci == CH - 1)
                        last.then_inc(S["proj_ready"], 1)
                    if j == 1 and before is not None:
                        state_inputs(*before)

            def state_inputs(g, q):
                pe.wait_ge(S["conv_ready"], g * ECH + ECH)
                wait(pe, S["u_ready"], g)
                for j in range(ECH):
                    last = nc.tensor.matmul(up[:, :], c["A"][:, j, :], conv[:, j, bass.ds(q * BLK, BLK)],
                                            start=j == 0, stop=j == ECH - 1)
                last.then_inc(S["up_ready"], 1)

            def direct(g, q, js):
                for j in js:
                    wait(pe, S["dir_ready"], g * ECH + j - 1)
                    nc.tensor.matmul(yp[j % 2][:, :], c["C_T"][:, j * P:(j + 1) * P],
                                     state[:, bass.ds(q * BLK, BLK)], start=True, stop=True
                                     ).then_inc(S["yp_ready"], 1)

            def outputs(g, ts):
                pe.wait_ge(S["gated"], g * 2 * ECH + (ts[0] // 2 + 1) * ECH)
                for t in ts:
                    wait(pe, S["x_ready"], g * TPB + t - 1)
                    for j in range(ECH):
                        last = nc.tensor.matmul(op[t % 2][:, 0:DM], y[:, j, t * P:(t + 1) * P], c["w_out"][:, j, :],
                                                start=j == 0, stop=j == ECH - 1)
                    last.then_inc(S["op_ready"], 1)

            def step(g, q):
                direct(g, q, (0, 1))
                outputs(g - 1, (0, 1))
                direct(g, q, (2, 3))
                outputs(g - 1, (2, 3))

            for half in range(HALF):
                g0 = half * HB
                inputs(g0)
                inputs(g0 + 1, (g0, 0))
                with pe.Fori(2, HB) as q:
                    inputs(q + g0, (q + g0 - 1, q - 1))
                state_inputs(g0 + HB - 1, HB - 1)
                pe.wait_ge(S["h_ready"], half * SEQ + SEQ)
                direct(g0, 0, (0, 1, 2, 3))
                step(g0 + 1, 1)
                with pe.Fori(2, HB) as q:
                    step(q + g0, q)
                outputs(g0 + HB - 1, (0, 1))
                outputs(g0 + HB - 1, (2, 3))

        @block.scalar
        def _(act):
            cv = c["cols"]

            def inputs(g, q, before=None):
                cols = bass.ds(q * BLK, BLK)
                for j in range(ECH):
                    act.wait_ge(S["proj_ready"], g * 2 * ECH + 2 * j + 1)
                    wait(act, S["conv_ready"], g * ECH + j - 1)
                    nc.scalar.activation(xpad[j % 2][:, :, TAPS - 1:TAPS - 1 + SEQ],
                                         proj[0][:, :].rearrange("p (b s) -> p b s", s=SEQ), ACT.Identity,
                                         bias=cv[:, j:j + 1]).then_inc(S["x_part"], 1)
                    act.wait_ge(S["proj_ready"], g * 2 * ECH + 2 * j + 2)
                    nc.scalar.activation(gate[:, j, cols], proj[1][:, :], ACT.Sigmoid, bias=cv[:, ECH + j:ECH + j + 1]
                                         ).then_inc(S["gate_part"], 1)
                    act.wait_ge(S["x_part"], g * ECH + j + 1)
                    nc.scalar.activation(conv[:, j, cols].rearrange("p (b s) -> p b s", s=SEQ), xpad[j % 2][:, :, 0:SEQ], ACT.Identity,
                                         bias=cv[:, 8 + j:9 + j], scale=cv[:, 12 + j * TAPS:13 + j * TAPS]
                                         ).then_inc(S["conv_start"], 1)
                    if j == 1 and before is not None:
                        state_inputs(*before)

            def state_inputs(g, q):
                act.wait_ge(S["up_ready"], g + 1)
                nc.scalar.activation(state[0:NS, bass.ds(q * BLK, BLK)], up[:, :], ACT.Copy).then_inc(S["u_ready"], 1)

            hs = state[0:NS, :].rearrange("n (b s) -> n b s", s=SEQ)
            act.wait_ge(S["padded"], 3)
            for half in range(HALF):
                g0 = half * HB
                if half:
                    act.wait_ge(S["yp_ready"], g0 * ECH)
                    act.wait_ge(S["gated"], g0 * 2 * ECH)
                inputs(g0, 0)
                inputs(g0 + 1, 1, (g0, 0))
                with act.Fori(2, HB) as q:
                    inputs(q + g0, q, (q + g0 - 1, q - 1))
                state_inputs(g0 + HB - 1, HB - 1)
                act.wait_ge(S["u_ready"], g0 + HB)
                nc.scalar.activation(hs[:, :, 0], hs[:, :, 0], ACT.Tanh).then_inc(S["h_ready"], 1)
                with act.Fori(1, SEQ) as s:
                    act.wait_ge(S["sum_ready"], s + half * (SEQ - 1))
                    nc.scalar.activation(hs[:, :, bass.ds(s, 1)].rearrange("n b s -> n (b s)"), step_sum[:, :], ACT.Tanh
                                         ).then_inc(S["h_ready"], 1)

        @block.gpsimd
        def _(pool):
            pool.memset(state[:, :], 0.0).then_inc(S["padded"], 1)
            pool.memset(xpad[0][:, :, 0:TAPS - 1], 0.0).then_inc(S["padded"], 1)
            pool.memset(xpad[1][:, :, 0:TAPS - 1], 0.0).then_inc(S["padded"], 1)
            pool.tensor_tensor(c["x_tok"][:, :, :], c["x_tok"][:, :, :],
                               c["b_out"][:, :].unsqueeze(1).to_broadcast([P, NT, DM]), ALU.add
                               ).then_inc(S["biased"], 1)

            def gated(g, q):
                for part in range(2):
                    wait(pool, S["op_ready"], (g - 1) * TPB + part * 2 + 2)
                    for j in range(ECH):
                        pool.wait_ge(S["dir_ready"], g * ECH + j + 1)
                        cols = bass.ds(q * BLK + part * HY, HY)
                        nc.gpsimd.tensor_tensor(y[:, j, part * HY:(part + 1) * HY], conv[:, j, cols], gate[:, j, cols],
                                                ALU.mult).then_inc(S["gated"], 1)

            for half in range(HALF):
                g0 = half * HB
                gated(g0, 0)
                with pool.Fori(1, HB) as q:
                    gated(q + g0, q)

        @block.vector
        def _(dve):
            dve.wait_ge(S["padded"], 3)
            cv = c["cols"]

            def convolution(g, q):
                for j in range(ECH):
                    dve.wait_ge(S["conv_start"], g * ECH + j + 1)
                    acc = conv[:, j, bass.ds(q * BLK, BLK)].rearrange("p (b s) -> p b s", s=SEQ)
                    for i in range(1, TAPS):
                        if i > 1:
                            dve.wait_ge(S["conv_step"], (g * ECH + j) * (TAPS - 2) + i - 1)
                        ins = nc.vector.scalar_tensor_tensor(
                            out=acc, in0=xpad[j % 2][:, :, i:i + SEQ],
                            scalar=cv[:, 12 + j * TAPS + i:13 + j * TAPS + i], in1=acc, op0=ALU.mult, op1=ALU.add)
                        ins.then_inc(S["conv_ready"] if i == TAPS - 1 else S["conv_step"], 1)

            def direct(g, q, js):
                for j in js:
                    dve.wait_ge(S["yp_ready"], g * ECH + j + 1)
                    part = conv[:, j, bass.ds(q * BLK, BLK)]
                    nc.vector.scalar_tensor_tensor(
                        out=part, in0=part, scalar=cv[:, 28 + j:29 + j],
                        in1=yp[j % 2][:, :], op0=ALU.mult, op1=ALU.add).then_inc(S["dir_ready"], 1)

            def outputs(g, ts):
                for t in ts:
                    ti = g * TPB + t
                    dve.wait_ge(S["op_ready"], ti + 1)
                    xt = c["x_tok"][:, bass.ds(ti, 1), :].rearrange("p a d -> p (a d)")
                    nc.vector.tensor_tensor(xt, op[t % 2][:, 0:DM], xt, ALU.add).then_inc(S["x_ready"], 1)
                    dve.wait_ge(S["x_ready"], ti + 1)
                    settle(nc, spot[0:1, (t % 2) * 2:(t % 2) * 2 + 1])
                    nc.vector.bn_stats(stats[:, :], xt).then_inc(S["stat_step"], 1)
                    dve.wait_ge(S["stat_step"], ti * 3 + 1)
                    settle(nc, spot[0:1, (t % 2) * 2 + 1:(t % 2) * 2 + 2])
                    nc.vector.bn_aggr(mv_tile[:, :], stats[:, :]).then_inc(S["stat_step"], 1)
                    dve.wait_ge(S["stat_step"], ti * 3 + 2)
                    nc.vector.tensor_copy(c["mv"][:, bass.ds(ti, 1), :].rearrange("p a d -> p (a d)"), mv_tile[:, :]
                                          ).then_inc(S["stat_step"], 1)

            hs = state[0:NS, :].rearrange("n (b s) -> n b s", s=SEQ)
            for half in range(HALF):
                g0 = half * HB
                convolution(g0, 0)
                with dve.Fori(1, HB) as q:
                    convolution(q + g0, q)
                with dve.Fori(1, SEQ) as s:
                    dve.wait_ge(S["h_ready"], s + half * SEQ)
                    nc.vector.tensor_tensor(step_sum[:, :], hs[:, :, bass.ds(s, 1)].rearrange("n b s -> n (b s)"),
                                            hs[:, :, bass.ds(s - 1, 1)].rearrange("n b s -> n (b s)"), ALU.add
                                            ).then_inc(S["sum_ready"], 1)
                dve.wait_ge(S["biased"], 1)
                direct(g0, 0, (0, 1, 2, 3))
                with dve.Fori(1, HB) as q:
                    direct(q + g0, q, (0, 1))
                    outputs(q + g0 - 1, (0, 1))
                    direct(q + g0, q, (2, 3))
                    outputs(q + g0 - 1, (2, 3))
                outputs(g0 + HB - 1, (0, 1, 2, 3))
            dve.wait_ge(S["stat_step"], NT * 3)


def routing(nc, a, c, xTh, xTl):
    with ExitStack() as ctx:
        m = Mem(nc, ctx, "rt")
        gw_raw = m.sb("gw_raw", [P, CH, P])
        gwh, gwl = m.sb("gwh", [P, CH, P], F32R), m.sb("gwl", [P, CH, P], F32R)
        e_bias = m.sb("e_bias", [P, NE])
        logT = m.sb("logT", [NE, TOK])
        score, choice = m.sb("score", [P, NT, NE]), m.sb("choice", [P, NT, NE])
        beats = m.sb("beats", [P, NT, NE])
        rank, grank = m.sb("rank", [P, NT, NE]), m.sb("grank", [P, NT, NG])
        pair = [m.sb(f"pair{i}", [P, NT, NG]) for i in range(8)]
        norm = [m.sb(f"norm{i}", [P, NT]) for i in range(2)]
        weight = c["weight"][:, :, 1:]
        lg = [m.ps(f"lg{i}") for i in range(2)]
        tk = m.ps("tk")
        S = {k: m.sem(k) for k in ("gw_in", "bias_in", "zeroed", "gw_ready", "lg_ready", "logT_ready", "tk_ready",
                                   "score_ready", "chain")}
        block = ctx.enter_context(nc.Block())

        @block.sync
        def _(sp):
            sp.wait_ge(S["zeroed"], 1)
            sp.dma_start(gw_raw[:, :, 0:NE], a["gate_wT"].rearrange("(c p) n -> p c n", p=P)).then_inc(S["gw_in"], 16)
            sp.dma_start(e_bias[:, :], a["e_bias"]).then_inc(S["bias_in"], 16)

        @block.gpsimd
        def _(pool):
            pool.memset(gw_raw[:, :, :], 0.0).then_inc(S["zeroed"], 1)
            for i in range(NG):
                last = pool.memset(grank[:, :, i:i + 1], float(NG - 1 - i))
            for i in range(NE):
                last = pool.memset(rank[:, :, i:i + 1], float(NE - 1 - i))
            last.then_inc(S["zeroed"], 1)
            pool.memset(c["weight"][:, :, 0:1], 1.0).then_inc(S["zeroed"], 1)
            pool.wait_ge(S["zeroed"], 3)

        @block.tensor
        def _(pe):
            pe.wait_ge(S["gw_ready"], 2)
            for n in range(NB):
                wait(pe, S["logT_ready"], n - 1)
                for ci in range(CH):
                    cols = slice(n * BLK, (n + 1) * BLK)
                    last = split_matmul(nc, lg[n % 2][:, :], (gwh[:, ci, :], gwl[:, ci, :]),
                                        (xTh[:, ci, cols], xTl[:, ci, cols]), ci == 0, ci == CH - 1)
                last.then_inc(S["lg_ready"], 1)
            pe.wait_ge(S["logT_ready"], NB)
            for t in range(NT):
                last = nc.tensor.transpose(tk[:, t * NE:(t + 1) * NE], logT[:, t * P:(t + 1) * P],
                                           c["ident"][0:NE, 0:NE])
            last.then_inc(S["tk_ready"], 1)

        @block.scalar
        def _(act):
            for n in range(NB):
                act.wait_ge(S["lg_ready"], n + 1)
                nc.scalar.activation(logT[:, n * BLK:(n + 1) * BLK], lg[n % 2][0:NE, :], ACT.Copy
                                     ).then_inc(S["logT_ready"], 1)
            act.wait_ge(S["tk_ready"], 1)
            nc.scalar.activation(score[:, :, :].rearrange("p t e -> p (t e)"), tk[:, :], ACT.Sigmoid
                                 ).then_inc(S["score_ready"], 1)

        @block.vector
        def _(dve):
            ch = Chain(dve, S["chain"])
            dve.wait_ge(S["gw_in"], 16)
            nc.vector.tensor_copy(gwh[:, :, :], gw_raw[:, :, :]).then_inc(S["gw_ready"], 1)
            dve.wait_ge(S["gw_ready"], 1)
            nc.vector.tensor_tensor(gwl[:, :, :], gw_raw[:, :, :], gwh[:, :, :].bitcast(F32), ALU.subtract
                                    ).then_inc(S["gw_ready"], 1)
            dve.wait_ge(S["score_ready"], 1)
            dve.wait_ge(S["bias_in"], 16)
            dve.wait_ge(S["zeroed"], 2)
            tt = nc.vector.tensor_tensor
            ch.link(tt(choice[:, :, :], score[:, :, :], e_bias[:, :].unsqueeze(1).to_broadcast([P, NT, NE]), ALU.add))
            four = [choice[:, :, :].rearrange("p t (g i) -> p t g i", i=PG)[:, :, :, i] for i in range(PG)]
            q = [x[:, :, :] for x in pair]
            ch.add(tt(q[0], four[0], four[1], ALU.max))
            ch.add(tt(q[1], four[0], four[1], ALU.min))
            ch.add(tt(q[2], four[2], four[3], ALU.max))
            ch.link(tt(q[3], four[2], four[3], ALU.min))
            ch.add(tt(q[4], q[0], q[2], ALU.max))
            ch.add(tt(q[5], q[0], q[2], ALU.min))
            ch.link(tt(q[6], q[1], q[3], ALU.max))
            ch.link(tt(q[7], q[5], q[6], ALU.max))
            ch.link(tt(q[0], q[4], q[7], ALU.add))

            def ranks(value, place, n):
                for d in range(1, n):
                    b = beats[:, :, 0:n - d]
                    ch.link(tt(b, value[:, :, 0:n - d], value[:, :, d:n], ALU.is_ge))
                    ch.link(tt(place[:, :, d:n], place[:, :, d:n], b, ALU.add))
                    ch.link(tt(place[:, :, 0:n - d], place[:, :, 0:n - d], b, ALU.subtract))

            ranks(q[0], grank, NG)
            ch.link(nc.vector.tensor_scalar(q[1], grank[:, :, :], 2.0, None, ALU.is_lt))
            ch.link(tt(choice[:, :, :].rearrange("p t (g i) -> p (t g) i", i=PG),
                       choice[:, :, :].rearrange("p t (g i) -> p (t g) i", i=PG),
                       pair[1][:, :, :].rearrange("p t g -> p (t g)").unsqueeze(2).to_broadcast([P, NT * NG, PG]),
                       ALU.mult))
            ranks(choice, rank, NE)
            ch.link(nc.vector.tensor_scalar(beats[:, :, :], rank[:, :, :], 4.0, None, ALU.is_lt))
            ch.link(tt(weight, score[:, :, :], beats[:, :, :], ALU.mult))
            ch.link(nc.vector.reduce_sum(norm[0][:, :], weight, AX))
            ch.link(nc.vector.tensor_scalar(norm[0][:, :], norm[0][:, :], 1e-20, None, ALU.add))
            ch.link(nc.vector.reciprocal(norm[1][:, :], norm[0][:, :]))
            ch.link(tt(weight, weight, norm[1][:, :].unsqueeze(2).to_broadcast([P, NT, NE]), ALU.mult))
            ch.link(nc.vector.tensor_scalar(weight, weight, 2.5, None, ALU.mult))


def experts(nc, a, c, xTh, xTl, out):
    with ExitStack() as ctx:
        m = Mem(nc, ctx, "ex")
        WG, WD = 2 * CH * P, DM
        w_raw = [m.sb(f"w_raw{i}", [P, WG + WD]) for i in range(2)]
        w_hi = [m.sb(f"w_hi{i}", [P, WG + WD], F32R) for i in range(2)]
        w_lo = [m.sb(f"w_lo{i}", [P, WG + WD], F32R) for i in range(2)]
        act_g = m.sb("act_g", [P, BLK])
        h = [m.sb(f"h{i}", [P, BLK]) for i in range(2)]
        h_hi = [m.sb(f"h_hi{i}", [P, BLK], F32R) for i in range(2)]
        h_lo = [m.sb(f"h_lo{i}", [P, BLK], F32R) for i in range(2)]
        gp = [m.ps(f"gp{i}") for i in range(2)]
        up = [m.ps(f"up{i}") for i in range(2)]
        yp = m.ps("yp", (P, TPB, DM))
        S = {k: m.sem(k) for k in ("w_in0", "w_in1", "w_hi_ready", "w_lo_ready", "g_ready", "u_ready",
                                   "act_ready", "h_ready", "h_hi_ready", "h_lo_ready",
                                   "y_ready", "x_ready", "stored")}
        N = NE + 1
        block = ctx.enter_context(nc.Block())

        def over_experts(eng, start, first, other, end):
            def expert(e, par):
                first(e, par)
                other(e, 1, par, 1)
                with eng.Fori(1, NB // 2) as k:
                    other(e, k * 2, par, 0)
                    other(e, k * 2 + 1, par, 1)
            start()
            expert(0, 0)
            with eng.Fori(0, NE // 2) as k:
                expert(k * 2 + 1, 1)
                expert(k * 2 + 2, 0)
            end()

        def of(e, b):
            return e * NB + b

        @block.sync
        def _(sp):
            def load(e, par):
                if not isinstance(e, int):
                    e = sp.snap(e)
                wait(sp, S["w_lo_ready"], e - 1)
                sp.dma_start(w_raw[par][:, :], a["w_exp"][bass.ds(e, 1), :, :].rearrange("a p n -> (a p) n")
                             ).then_inc(S[f"w_in{par}"], 16)
            load(0, 0)
            load(1, 1)
            with sp.Fori(1, NE // 2) as k:
                load(k * 2, 0)
                load(k * 2 + 1, 1)
            load(NE, 0)
            for b in range(NB):
                sp.wait_ge(S["x_ready"], of(NE, b) + 1)
                sp.dma_start(out[b * BLK:(b + 1) * BLK, :].rearrange("(t p) d -> p t d", p=P),
                             c["x_tok"][:, b * TPB:(b + 1) * TPB, :]).then_inc(S["stored"], 16)
            sp.wait_ge(S["stored"], NB * 16)

        @block.tensor
        def _(pe):
            def up_products(e, b, par, bpar):
                i = of(e, b)
                wait(pe, S["act_ready"], i - 1)
                wait(pe, S["h_ready"], i - 1)
                cols = bass.ds(b * BLK, BLK)
                for kind, bank, done in ((0, gp[bpar], "g_ready"), (1, up[bpar], "u_ready")):
                    for ci in range(CH):
                        w0 = (kind * CH + ci) * P
                        last = split_matmul(nc, bank[:, :], (w_hi[par][:, w0:w0 + P], w_lo[par][:, w0:w0 + P]),
                                            (xTh[:, ci, cols], xTl[:, ci, cols]), ci == 0, ci == CH - 1)
                    last.then_inc(S[done], 1)

            def down_product(i, par, bpar):
                pe.wait_ge(S["h_hi_ready"], i + 1)
                pe.wait_ge(S["h_lo_ready"], i + 1)
                wait(pe, S["x_ready"], i)
                for t in range(TPB):
                    hs = slice(t * P, (t + 1) * P)
                    last = split_matmul(nc, yp[:, t, :], (h_hi[bpar][:, hs], h_lo[bpar][:, hs]),
                                        (w_hi[par][:, WG:WG + WD], w_lo[par][:, WG:WG + WD]), True, True)
                last.then_inc(S["y_ready"], 1)

            def first(e, par):
                pe.wait_ge(S["w_lo_ready"], e + 1)
                up_products(e, 0, par, 0)
                if not (isinstance(e, int) and e == 0):
                    down_product(of(e, 0) - 1, 1 - par, 1)

            def other(e, b, par, bpar):
                up_products(e, b, par, bpar)
                down_product(of(e, b) - 1, par, 1 - bpar)

            over_experts(pe, lambda: None, first, other, lambda: down_product(N * NB - 1, 0, 1))

        @block.scalar
        def _(act):
            def split(e, par):
                act.wait_ge(S["w_in%d" % par], pair_of(e) * 16)
                wait(act, S["y_ready"], (e - 1) * NB)
                nc.scalar.activation(w_hi[par][:, :], w_raw[par][:, :], ACT.Copy).then_inc(S["w_hi_ready"], 1)

            def block_of(i, bpar):
                act.wait_ge(S["g_ready"], i + 1)
                wait(act, S["h_ready"], i)
                nc.scalar.activation(act_g[:, :], gp[bpar][:, :], ACT.Silu).then_inc(S["act_ready"], 1)
                act.wait_ge(S["h_ready"], i + 1)
                wait(act, S["y_ready"], i - 1)
                nc.scalar.activation(h_hi[bpar][:, :], h[bpar][:, :], ACT.Copy).then_inc(S["h_hi_ready"], 1)

            def pair_of(e):
                return e // 2 + 1 if isinstance(e, int) else half[0] + 1

            half = [0]

            def expert(e, par, more=True):
                block_of(of(e, 0), 0)
                block_of(of(e, 1), 1)
                if more:
                    split(e + 1, 1 - par)
                with act.Fori(1, NB // 2) as k:
                    block_of(of(e, 0) + k * 2, 0)
                    block_of(of(e, 0) + k * 2 + 1, 1)

            split(0, 0)
            expert(0, 0)
            with act.Fori(0, NE // 2 - 1) as k:
                half[0] = k + 1
                expert(k * 2 + 1, 1)
                half[0] = k + 1
                expert(k * 2 + 2, 0)
            expert(NE - 1, 1)
            expert(NE, 0, False)

        @block.gpsimd
        def _(pool):
            def low(i, bpar):
                pool.wait_ge(S["h_hi_ready"], i + 1)
                nc.gpsimd.tensor_tensor(h_lo[bpar][:, :], h[bpar][:, :], h_hi[bpar][:, :].bitcast(F32), ALU.subtract
                                        ).then_inc(S["h_lo_ready"], 1)

            with pool.Fori(0, N * NB // 2) as k:
                low(k * 2, 0)
                low(k * 2 + 1, 1)

        @block.vector
        def _(dve):
            def prepare(e, par):
                wait(dve, S["y_ready"], (e - 1) * NB)
                dve.wait_ge(S["w_hi_ready"], e + 1)
                nc.vector.tensor_tensor(w_lo[par][:, :], w_raw[par][:, :], w_hi[par][:, :].bitcast(F32), ALU.subtract
                                        ).then_inc(S["w_lo_ready"], 1)

            def hidden(i, bpar):
                dve.wait_ge(S["act_ready"], i + 1)
                dve.wait_ge(S["u_ready"], i + 1)
                wait(dve, S["h_lo_ready"], i - 1)
                nc.vector.tensor_tensor(h[bpar][:, :], act_g[:, :], up[bpar][:, :], ALU.mult).then_inc(S["h_ready"], 1)

            def add(e, i, b):
                dve.wait_ge(S["y_ready"], i + 1)
                for t in range(TPB):
                    ti = b * TPB + t
                    xt = c["x_tok"][:, bass.ds(ti, 1), :].rearrange("p a d -> p (a d)")
                    last = nc.vector.scalar_tensor_tensor(
                        out=xt, in0=yp[:, t, :], scalar=c["weight"][:, bass.ds(ti, 1), bass.ds(e, 1)].rearrange("p a b -> p (a b)"),
                        in1=xt, op0=ALU.mult, op1=ALU.add)
                last.then_inc(S["x_ready"], 1)

            def expert(e, par, more=True):
                i0 = of(e, 0)
                hidden(i0, 0)
                if not (isinstance(e, int) and e == 0):
                    add(e - 1, i0 - 1, NB - 1)
                hidden(i0 + 1, 1)
                add(e, i0, 0)
                if more:
                    prepare(e + 1, 1 - par)
                with dve.Fori(1, NB // 2) as k:
                    hidden(i0 + k * 2, 0)
                    add(e, i0 + k * 2 - 1, k * 2 - 1)
                    hidden(i0 + k * 2 + 1, 1)
                    add(e, i0 + k * 2, k * 2)

            prepare(0, 0)
            expert(0, 0)
            with dve.Fori(0, NE // 2 - 1) as k:
                expert(k * 2 + 1, 1)
                expert(k * 2 + 2, 0)
            expert(NE - 1, 1)
            expert(NE, 0, False)
            add(NE, N * NB - 1, NB - 1)


def build(nc, a, out):
    with ExitStack() as ctx:
        m = Mem(nc, ctx, "g")
        c = {"x_tok": m.sb("x_tok", [P, NT, DM]), "mv": m.sb("mv", [P, NT, 2]), "rstd": m.sb("rstd", [P, NT]),
             "ident": m.sb("ident", [P, P])}
        with ExitStack() as actx:
            ma = Mem(nc, actx, "c")
            for name, shape, dt in (
                    ("head_rows", [P, 8], F32), ("odd_even", [P, 2], F32),
                    ("mask_add", [P, KEYS], F32), ("b_qk", [P, 2, CH], F32),
                    ("b_v", [P, DM], F32), ("b_o", [P, DM], F32), ("w_o", [P, CH, DM], F32),
                    ("wh", [P, 3, CH, DM], F32R), ("wl", [P, 3, CH, DM], F32R),
                    ("qTh", [P, CH, TOK], F32R), ("qTl", [P, CH, TOK], F32R)):
                c[name] = ma.sb(name, shape, dt)
            set_up(nc, a, c)
            inverse_deviation(nc, "n1", c["mv"], c["rstd"])
            with ExitStack() as tctx:
                mt = Mem(nc, tctx, "xt1")
                xTh, xTl = mt.sb("xTh", [P, CH, TOK], F32R), mt.sb("xTl", [P, CH, TOK], F32R)
                normalise_and_transpose(nc, "nt1", c["x_tok"], c["mv"], c["rstd"], c["ident"], xTh, xTl)
                queries(nc, a, c, xTh, xTl)
            attention(nc, a, c)
        inverse_deviation(nc, "n2", c["mv"], c["rstd"])
        with ExitStack() as rctx:
            mr = Mem(nc, rctx, "r")
            for name, shape, dt in (
                    ("A", [P, ECH, NS], F32), ("C_T", [P, EI], F32), ("w_out", [P, ECH, DM], F32),
                    ("cols", [P, 32], F32), ("b_out", [P, DM], F32),
                    ("wih", [P, CH, 2 * EI], F32R), ("wil", [P, CH, 2 * EI], F32R)):
                c[name] = mr.sb(name, shape, dt)
            recurrent_inputs(nc, a, c)
            xTh, xTl = mr.sb("xTh", [P, CH, TOK], F32R), mr.sb("xTl", [P, CH, TOK], F32R)
            normalise_and_transpose(nc, "nt2", c["x_tok"], c["mv"], c["rstd"], c["ident"], xTh, xTl)
            recurrent(nc, c, xTh, xTl)
        inverse_deviation(nc, "n3", c["mv"], c["rstd"])
        with ExitStack() as ectx:
            me = Mem(nc, ectx, "e")
            xTh, xTl = me.sb("xTh", [P, CH, TOK], F32R), me.sb("xTl", [P, CH, TOK], F32R)
            c["weight"] = me.sb("weight", [P, NT, NE + 1])
            normalise_and_transpose(nc, "nt3", c["x_tok"], c["mv"], c["rstd"], c["ident"], xTh, xTl)
            routing(nc, a, c, xTh, xTl)
            experts(nc, a, c, xTh, xTl, out)


def kernel(**inputs):
    import numpy as np
    import concourse.bacc as bacc
    from concourse.bass_utils import run_bass_kernel_spmd as run

    def f(name):
        return np.asarray(inputs[name])

    def padded_bytes(v):
        return np.pad(v.view(np.uint8)[..., None], ((0, 0), (0, 0), (0, 3))).view(np.int32)[..., 0]

    def per_row(v, n):
        return v.reshape(n, P).T

    arrays = {
        "x": f("x").reshape(TOK, DM),
        "ctxT": f("ctx_1024").reshape(BATCH * KEYS, CH, P).transpose(2, 1, 0),
        "ctx_lastT": f("ctx_1024")[:, KEYS - 1].reshape(BATCH, CH, P).transpose(2, 1, 0),
        "mask": padded_bytes(np.tile(f("mask_1x1xSxS2_bk0")[0, 0], (4, 1))),
        "Wq": f("L0_xattn_Wq"), "Wk": f("L0_xattn_Wk"), "Wv": f("L0_xattn_Wv"), "Wo": f("L0_xattn_Wo"),
        "b_qk": np.stack([per_row(f("L0_xattn_bq"), CH), per_row(f("L0_xattn_bk"), CH)], axis=1),
        "b_v": np.broadcast_to(f("L0_xattn_bv"), (P, DM)),
        "b_o": np.broadcast_to(f("L0_xattn_bo"), (P, DM)),
    }
    def transposed(w):
        return w.reshape(w.shape[0], P, CH, P).transpose(0, 3, 2, 1)

    gate, up, down = (np.concatenate([f(f"L0_ffn_shared_{s}")[None], f(f"L0_ffn_{r}")])
                      for s, r in (("gate_w", "gate_proj"), ("up_w", "up_proj"), ("down_w", "down_proj")))
    arrays |= {
        "W_in": f("L0_attn_W_in"), "A": f("L0_attn_A"), "C_T": np.pad(f("L0_attn_C").T, ((0, P - NS), (0, 0))), "W_out": f("L0_attn_W_out"),
        "b_out": np.broadcast_to(f("L0_attn_b_out"), (P, DM)),
        "cols": np.concatenate([per_row(f("L0_attn_b_in"), 8), per_row(f("L0_attn_conv_b"), ECH),
                                f("L0_attn_conv_w").reshape(ECH, P, TAPS).transpose(1, 0, 2).reshape(P, -1),
                                per_row(f("L0_attn_Dp"), ECH)], axis=1),
        "gate_wT": f("L0_ffn_gate_w").T, "e_bias": np.broadcast_to(f("L0_ffn_e_bias"), (P, NE)),
        "w_exp": np.concatenate([transposed(gate).reshape(NE + 1, P, -1), transposed(up).reshape(NE + 1, P, -1),
                                 down.transpose(0, 2, 1)], axis=2),
    }
    arrays = {f"in_{n}": np.ascontiguousarray(v) for n, v in arrays.items()}
    nc = bacc.Bacc("TRN2", target_bir_lowering=False, num_devices=1)
    a = {n[3:]: nc.dram_tensor(n, v.shape, mybir.dt.from_np(v.dtype), kind="ExternalInput").ap()
         for n, v in arrays.items()}
    a["v_last"] = nc.dram_tensor("v_last", (BATCH, 4, DM), F32, kind="Internal").ap()
    out = nc.dram_tensor("out", (TOK, DM), F32, kind="ExternalOutput").ap()
    build(nc, a, out)
    r = run(nc, [arrays], core_ids=[0])
    return np.asarray(r.results[0]["out"]).reshape(BATCH, SEQ, DM)
```

```python
import concourse.bass as bass
from concourse import mybir
from concourse.alu_op_type import AluOpType as ALU
from contextlib import ExitStack

F32 = mybir.dt.float32
F32R = mybir.dt.float32r
ACT = mybir.ActivationFunctionType
AX = mybir.AxisListType.X

P = 128
BATCH, SEQ, DM = 128, 32, 256
KEYS = 257
HEADS, DK = 16, 16
TOK = BATCH * SEQ
NT = TOK // P
CH = DM // P
BLK = 512
NB = TOK // BLK
TPB = BLK // P
BPB = BLK // SEQ
EI = 512
ECH = EI // P
NS = 16
TAPS = 4
NE = 16
NG = 4
PG = NE // NG
EPS = 1e-5
NEG = -3.0e38
SCALE = 0.25
PAIRS = BATCH // 2
PK = 2 * KEYS
WIN = 258


def wait(eng, sem, count):
    if isinstance(count, int) and count <= 0:
        return
    eng.wait_ge(sem, count)


class Chain:

    def __init__(self, eng, sem):
        self.eng, self.sem, self.base, self.n = eng, sem, 0, 0

    def at(self, base):
        self.base, self.n = base, 0

    def add(self, ins):
        self.n += 1
        ins.then_inc(self.sem, 1)

    def sync(self):
        wait(self.eng, self.sem, self.base + self.n)

    def link(self, ins):
        self.add(ins)
        self.sync()


def settle(nc, spot):
    nc.vector.memset(spot, 0.0)


def split_matmul(nc, out, lhs, rhs, start, stop, **kw):
    nc.tensor.matmul(out, lhs[0], rhs[0], start=start, stop=False, **kw)
    nc.tensor.matmul(out, lhs[1], rhs[0], start=False, stop=False, **kw)
    return nc.tensor.matmul(out, lhs[0], rhs[1], start=False, stop=stop, **kw)


class Mem:

    def __init__(self, nc, ctx, tag):
        self.nc, self.ctx, self.tag = nc, ctx, tag

    def sb(self, name, shape, dt=F32):
        return self.ctx.enter_context(self.nc.sbuf_tensor(f"{self.tag}_{name}", shape, dt))

    def ps(self, name, shape=(P, 512)):
        return self.ctx.enter_context(self.nc.psum_tensor(f"{self.tag}_{name}", list(shape), F32))

    def sem(self, name):
        return self.ctx.enter_context(self.nc.semaphore(f"{self.tag}_{name}"))


def inverse_deviation(nc, m, c):
    ve, sd = m.sb("ve", [P, NT]), m.sb("sd", [P, NT])
    var_ready, sqrt_ready, rstd_ready = m.sem("var_ready"), m.sem("sqrt_ready"), m.sem("rstd_ready")

    def on_dve(dve):
        nc.vector.tensor_scalar(ve[:, :], c["mv"][:, :, 1], EPS, None, ALU.add).then_inc(var_ready, 1)
        dve.wait_ge(sqrt_ready, 1)
        nc.vector.reciprocal(c["rstd"][:, :], sd[:, :]).then_inc(rstd_ready, 1)
        dve.wait_ge(rstd_ready, 1)

    def on_act(act):
        act.wait_ge(var_ready, 1)
        nc.scalar.activation(sd[:, :], ve[:, :], ACT.Sqrt).then_inc(sqrt_ready, 1)

    return on_dve, on_act


class NormStage:

    def __init__(self, nc, m, c, xn, tp, xTh, xTl):
        self.nc, self.c, self.xn, self.tp, self.xTh, self.xTl = nc, c, xn, tp, xTh, xTl
        self.xn_ready, self.tp_ready = m.sem("xn_ready"), m.sem("tp_ready")
        self.hi_ready, self.lo_ready = m.sem("hi_ready"), m.sem("lo_ready")

    def normalise(self, dve, n):
        c = self.c
        wait(dve, self.tp_ready, n)
        for t in range(TPB):
            ti = n * TPB + t
            last = self.nc.vector.tensor_scalar(
                self.xn[:, t * DM:(t + 1) * DM], c["x_tok"][:, bass.ds(ti, 1), :].rearrange("p a d -> p (a d)"),
                c["mv"][:, bass.ds(ti, 1), 0], c["rstd"][:, bass.ds(ti, 1)], ALU.subtract, ALU.mult)
        last.then_inc(self.xn_ready, 1)

    def transposes(self, pe, n):
        pe.wait_ge(self.xn_ready, n + 1)
        wait(pe, self.hi_ready, n * CH)
        wait(pe, self.lo_ready, n * CH)
        for ci in range(CH):
            for t in range(TPB):
                last = self.nc.tensor.transpose(self.tp[ci][:, t * P:(t + 1) * P],
                                                self.xn[:, t * DM + ci * P:t * DM + (ci + 1) * P],
                                                self.c["ident"][:, :])
        last.then_inc(self.tp_ready, 1)

    def high(self, act, n):
        for ci in range(CH):
            act.wait_ge(self.tp_ready, n + 1)
            self.nc.scalar.activation(self.xTh[:, ci, bass.ds(n * BLK, BLK)], self.tp[ci][:, :], ACT.Copy
                                      ).then_inc(self.hi_ready, 1)

    def low(self, dve, n):
        for ci in range(CH):
            cols = bass.ds(n * BLK, BLK)
            dve.wait_ge(self.hi_ready, n * CH + ci + 1)
            self.nc.vector.tensor_tensor(self.xTl[:, ci, cols], self.tp[ci][:, :],
                                         self.xTh[:, ci, cols].bitcast(F32), ALU.subtract
                                         ).then_inc(self.lo_ready, 1)

    def ready(self, pe, n):
        pe.wait_ge(self.lo_ready, (n + 1) * CH)


def set_up(nc, a, c):
    with ExitStack() as ctx:
        m = Mem(nc, ctx, "set")
        w_raw = m.sb("w_raw", [P, 3, CH, DM])
        mask_i = m.sb("mask_i", [P, KEYS], mybir.dt.int32)
        mask_f = m.sb("mask_f", [P, KEYS])
        keep = m.sb("keep", [P, 3])
        stats = m.sb("stats", [P, NT, 6])
        x_in = [m.sem(f"x_in{i}") for i in range(4)]
        w_in = [m.sem(f"w_in{i}") for i in range(3)]
        b_in, mask_in, w_high, w_low = m.sem("b_in"), m.sem("mask_in"), m.sem("w_high"), m.sem("w_low")
        XT = NT // 4
        made, chain, stat, aggr = m.sem("made"), m.sem("chain"), m.sem("stat"), m.sem("aggr")
        block = ctx.enter_context(nc.Block())

        @block.sync
        def _(sp):
            for i in range(4):
                sp.dma_start(c["x_tok"][:, i * XT:(i + 1) * XT, :],
                             a["x"][i * XT * P:(i + 1) * XT * P, :].rearrange("(t p) d -> p t d", p=P)
                             ).then_inc(x_in[i], 16)

        @block.scalar
        def _(act):
            for i, w in enumerate(("Wq", "Wk", "Wv")):
                act.dma_start(w_raw[:, i, :, :], a[w].rearrange("(c p) n -> p c n", p=P)).then_inc(w_in[i], 16)
            act.dma_start(mask_i[:, :], a["mask"]).then_inc(mask_in, 16)
            act.dma_start(c["w_o"][:, :, :], a["Wo"].rearrange("(c p) n -> p c n", p=P)).then_inc(b_in, 16)
            act.dma_start(c["b_qk"][:, :, :], a["b_qk"]).then_inc(b_in, 16)
            act.dma_start(c["b_v"][:, :], a["b_v"]).then_inc(b_in, 16)
            act.dma_start(c["b_o"][:, :], a["b_o"]).then_inc(b_in, 16)
            for i in range(3):
                act.wait_ge(w_in[i], 16)
                nc.scalar.activation(c["wh"][:, i, :, :], w_raw[:, i, :, :], ACT.Copy).then_inc(w_high, 1)
            act.wait_ge(b_in, 64)

        @block.gpsimd
        def _(pool):
            ch = Chain(pool, made)
            ch.add(pool.memset(c["ident"][:, :], 0.0))
            ch.add(pool.memset(c["head_rows"][:, :], 1.0))
            ch.sync()
            ch.link(pool.affine_select(out=c["ident"][:, :], in_=c["ident"][:, :], compare_op=ALU.not_equal,
                                       fill=1.0, base=0, pattern=[[-1, P]], channel_multiplier=1))
            ch.link(pool.affine_select(out=c["head_rows"][:, :], in_=c["head_rows"][:, :], compare_op=ALU.is_ge,
                                       fill=0.0, base=0, pattern=[[-DK, 8]], channel_multiplier=1))
            ch.link(pool.affine_select(out=c["head_rows"][:, :], in_=c["head_rows"][:, :], compare_op=ALU.is_ge,
                                       fill=0.0, base=DK - 1, pattern=[[DK, 8]], channel_multiplier=-1))
            for i in range(3):
                pool.wait_ge(w_high, i + 1)
                nc.gpsimd.tensor_tensor(c["wl"][:, i, :, :], w_raw[:, i, :, :], c["wh"][:, i, :, :].bitcast(F32),
                                        ALU.subtract).then_inc(w_low, 1)
            pool.wait_ge(w_low, 3)

        @block.vector
        def _(dve):
            ch = Chain(dve, chain)

            def aggregate(i):
                dve.wait_ge(stat, (i + 1) * XT)
                for t in range(i * XT, (i + 1) * XT):
                    nc.vector.bn_aggr(c["mv"][:, t, :], stats[:, t, :]).then_inc(aggr, 1)

            def mask():
                dve.wait_ge(mask_in, 16)
                ch.link(nc.vector.tensor_copy(mask_f[:, :], mask_i[:, :]))
                ch.link(nc.vector.tensor_scalar(c["mask_add"][:, :], mask_f[:, :], -NEG, NEG, ALU.mult, ALU.add))
                ch.link(nc.vector.reduce_sum(keep[:, 0:1], mask_f[:, :], AX))
                ch.link(nc.vector.reciprocal(keep[:, 1:2], keep[:, 0:1]))
                ch.link(nc.vector.tensor_scalar(keep[:, 2:3], keep[:, 1:2], 0.0, None, ALU.mult))
                ch.link(nc.vector.tensor_scalar(c["mask_add"][:, :], c["mask_add"][:, :], keep[:, 2:3], None, ALU.add))
                dve.wait_ge(made, 5)
                ch.link(nc.vector.tensor_reduce(c["odd_even"][:, :],
                                                c["head_rows"][:, :].rearrange("p (j e) -> p e j", e=2), AX, ALU.add))

            for i in range(4):
                dve.wait_ge(x_in[i], 16)
                for t in range(i * XT, (i + 1) * XT):
                    nc.vector.bn_stats(stats[:, t, :], c["x_tok"][:, t, :]).then_inc(stat, 1)
                if i > 0:
                    aggregate(i - 1)
            mask()
            aggregate(3)
            dve.wait_ge(aggr, NT)


def queries(nc, a, c, xTh, xTl):
    with ExitStack() as ctx:
        m = Mem(nc, ctx, "q")
        qp = [m.ps(f"qp{i}") for i in range(2)]
        vp = m.ps("vp")
        rstd_dve, rstd_act = inverse_deviation(nc, m, c)
        norm = NormStage(nc, m, c, m.sb("xn", [P, TPB * DM]), [m.ps(f"tp{i}") for i in range(CH)], xTh, xTl)
        last_raw = m.sb("last_raw", [P, CH, BATCH])
        last_hi, last_lo = m.sb("last_hi", [P, CH, BATCH], F32R), m.sb("last_lo", [P, CH, BATCH], F32R)
        v_rows = m.sb("v_rows", [BATCH, 4, DM])
        S = {k: m.sem(k) for k in ("last_in", "ctx_in", "rows_zero", "last_hi_ready", "last_lo_ready", "v_ready",
                                   "rows_ready", "rows_out")}
        q_ready, qh_ready, ql_ready, biased = m.sem("q_ready"), m.sem("qh_ready"), m.sem("ql_ready"), m.sem("biased")
        block = ctx.enter_context(nc.Block())

        @block.tensor
        def _(pe):
            norm.transposes(pe, 0)
            pe.wait_ge(S["last_lo_ready"], 1)
            for ci in range(CH):
                last = split_matmul(nc, vp[:, 0:DM], (last_hi[:, ci, :], last_lo[:, ci, :]),
                                    (c["wh"][:, 2, ci, :], c["wl"][:, 2, ci, :]), ci == 0, ci == CH - 1)
            last.then_inc(S["v_ready"], 1)

            def block_of_queries(n):
                norm.ready(pe, n)
                cols = bass.ds(n * BLK, BLK)
                for o in range(CH):
                    wait(pe, qh_ready, (n - 1) * CH + o + 1)
                    wait(pe, ql_ready, (n - 1) * CH + o + 1)
                    for ci in range(CH):
                        last = split_matmul(nc, qp[o][:, :], (c["wh"][:, 0, ci, o * P:(o + 1) * P],
                                                              c["wl"][:, 0, ci, o * P:(o + 1) * P]),
                                            (xTh[:, ci, cols], xTl[:, ci, cols]), ci == 0, ci == CH - 1)
                    last.then_inc(q_ready, 1)

            norm.transposes(pe, 1)
            block_of_queries(0)
            with pe.Fori(1, NB - 1) as n:
                norm.transposes(pe, n + 1)
                block_of_queries(n)
            block_of_queries(NB - 1)

        @block.scalar
        def _(act):
            def block_of_queries(n):
                for o in range(CH):
                    act.wait_ge(q_ready, n * CH + o + 1)
                    nc.scalar.activation(c["qTh"][:, o, bass.ds(n * BLK, BLK)], qp[o][:, :], ACT.Identity,
                                         bias=c["b_qk"][:, 0, o:o + 1]).then_inc(qh_ready, 1)

            rstd_act(act)
            norm.high(act, 0)
            with act.Fori(0, NB - 1) as n:
                norm.high(act, n + 1)
                block_of_queries(n)
            block_of_queries(NB - 1)

        @block.sync
        def _(sp):
            sp.dma_start(last_raw[:, :, :], a["ctx_lastT"]).then_inc(S["last_in"], 16)
            for i in range(2):
                sp.dma_start(c["ctx_raw"][i][:, :, :], a["ctxT"][:, :, i * PK:(i + 1) * PK]).then_inc(S["ctx_in"], 16)
            sp.wait_ge(S["ctx_in"], 32)
            sp.wait_ge(S["rows_ready"], 4)
            sp.dma_start(a["v_last"], v_rows[:, :, :]).then_inc(S["rows_out"], 16)
            sp.wait_ge(S["rows_out"], 16)

        @block.vector
        def _(dve):
            rstd_dve(dve)
            norm.normalise(dve, 0)
            dve.wait_ge(S["last_in"], 16)
            nc.vector.tensor_copy(last_hi[:, :, :], last_raw[:, :, :]).then_inc(S["last_hi_ready"], 1)
            dve.wait_ge(S["last_hi_ready"], 1)
            nc.vector.tensor_tensor(last_lo[:, :, :], last_raw[:, :, :], last_hi[:, :, :].bitcast(F32), ALU.subtract
                                    ).then_inc(S["last_lo_ready"], 1)
            norm.normalise(dve, 1)
            norm.low(dve, 0)
            dve.wait_ge(S["rows_zero"], 1)
            dve.wait_ge(S["v_ready"], 1)
            for g in range(4):
                cols = slice(g * 64, (g + 1) * 64)
                nc.vector.tensor_tensor(v_rows[:, g, cols], vp[:, cols], c["b_v"][:, cols], ALU.add
                                        ).then_inc(S["rows_ready"], 1)

            def block_of_queries(n):
                for o in range(CH):
                    dve.wait_ge(qh_ready, n * CH + o + 1)
                    cols = bass.ds(n * BLK, BLK)
                    nc.vector.scalar_tensor_tensor(
                        out=c["qTl"][:, o, cols], in0=qp[o][:, :], scalar=c["b_qk"][:, 0, o:o + 1],
                        in1=c["qTh"][:, o, cols].bitcast(F32), op0=ALU.add, op1=ALU.subtract).then_inc(ql_ready, 1)

            norm.normalise(dve, 2)
            norm.low(dve, 1)
            block_of_queries(0)
            with dve.Fori(1, NB - 2) as n:
                norm.normalise(dve, n + 2)
                norm.low(dve, n + 1)
                block_of_queries(n)
            norm.low(dve, NB - 1)
            block_of_queries(NB - 2)
            block_of_queries(NB - 1)
            dve.wait_ge(ql_ready, NB * CH)

        @block.gpsimd
        def _(pool):
            pool.memset(v_rows[:, :, :], 0.0).then_inc(S["rows_zero"], 1)
            with pool.Fori(0, NB) as n:
                pool.wait_ge(norm.xn_ready, n + 1)
                xb = c["x_tok"][:, bass.ds(n * TPB, TPB), :]
                nc.gpsimd.tensor_tensor(xb, xb, c["b_o"][:, :].unsqueeze(1).to_broadcast([P, TPB, DM]), ALU.add
                                        ).then_inc(biased, 1)
            pool.wait_ge(biased, NB)


def attention(nc, a, c):
    with ExitStack() as ctx:
        m = Mem(nc, ctx, "at")
        ctx_raw = c["ctx_raw"]
        ctx_hi = [m.sb(f"ctx_hi{i}", [P, CH, PK], F32R) for i in range(2)]
        ctx_lo = [m.sb(f"ctx_lo{i}", [P, CH, PK], F32R) for i in range(2)]
        k_hi, k_lo = m.sb("k_hi", [P, CH, PK], F32R), m.sb("k_lo", [P, CH, PK], F32R)
        v_sb = [m.sb(f"v_sb{i}", [P, 2, 2, DM]) for i in range(2)]
        v_last = [m.sb(f"v_last{i}", [8, 2, DM]) for i in range(2)]
        q_hi = [m.sb(f"q_hi{i}", [P, CH, 8, SEQ], F32R) for i in range(2)]
        q_lo = [m.sb(f"q_lo{i}", [P, CH, 8, SEQ], F32R) for i in range(2)]
        prob = m.sb("prob", [P, 2, 4, KEYS])
        least = [m.sb(f"least{i}", [P, 4]) for i in range(2)]
        total = [m.sb(f"total{i}", [P, 4]) for i in range(2)]
        inv = [m.sb(f"inv{i}", [P, 4]) for i in range(2)]
        pT = [m.sb(f"pT{i}", [P, 2, 512]) for i in range(2)]
        p_last = m.sb("p_last", [8, P])
        o_even = [m.sb(f"o_even{i}", [P, CH, SEQ]) for i in range(2)]
        oT = m.sb("oT", [P, CH, P])
        spot = m.sb("spot", [1, 10])
        stats, mv_tile = m.sb("stats", [P, 6]), m.sb("mv_tile", [P, 2])

        proj = [m.ps(f"proj{i}") for i in range(3)]
        sc = [m.ps(f"sc{i}") for i in range(2)] + [proj[1]]
        tp = [m.ps(f"tp{i}") for i in range(2)]
        ob = m.ps("ob")
        o_ps = [ob[:, 0:P], proj[2][:, 0:P]]
        yb = ob[:, DM:2 * DM]
        last_ps = proj[0][0:8, 0:P]

        S = {k: m.sem(k) for k in (
            "ctx_in0", "ctx_in1", "ctx_hi_ready", "ctx_lo_ready", 
            "proj_ready", "k_hi_ready", "k_lo_ready", "v_ready", "v_last_in0", "v_last_in1", "v_last_zero",
            "q_ready", "s_ready", "masked", "exp_ready", "inv_ready", 
            "norm_ready", "t_ready", "t_last_ready", "pT0_ready", "pT1_ready", "p_last_ready",
            "av_ready", "oT_ready", "y_ready", "x_ready", "dve_chain")}

        NU = 6

        block = ctx.enter_context(nc.Block())

        def load(sp, n, par):
            if not isinstance(n, int):
                n = sp.snap(n)
            wait(sp, S["proj_ready"], (n - 1) * NU)
            sp.dma_start(ctx_raw[par][:, :, :], a["ctxT"][:, :, bass.ds(n * PK, PK)]
                         ).then_inc(S[f"ctx_in{par}"], 16)

        def load_last(eng, n, par):
            if not isinstance(n, int):
                n = eng.snap(n)
            wait(eng, S["av_ready"], n * 2 - 2)
            for b in range(2):
                eng.dma_start(v_last[par][4 * b:4 * b + 4, b, :],
                              a["v_last"][bass.ds(n * 2 + b, 1), :, :].rearrange("a g n -> (a g) n")
                              ).then_inc(S[f"v_last_in{par}"], 16)

        @block.sync
        def _(sp):
            sp.wait_ge(S["v_last_zero"], 2)
            load_last(sp, 0, 0)
            load_last(sp, 1, 1)
            with sp.Fori(1, PAIRS // 2) as k:
                load(sp, k * 2, 0)
                load_last(sp, k * 2, 0)
                load(sp, k * 2 + 1, 1)
                load_last(sp, k * 2 + 1, 1)

        def arrived(eng, n, par):
            wait(eng, S[f"ctx_in{par}"], (n // 2 if isinstance(n, int) else turn[0] + 2 - par) * 16)

        def so_far(p, ppar):
            return p // 2 + 1 if isinstance(p, int) else turn[0] + 2 - ppar

        turn = [None]

        def pe_k(pe, n, par):
            pe.wait_ge(S["ctx_hi_ready"], n + 1)
            pe.wait_ge(S["ctx_lo_ready"], n + 1)
            for o in range(CH):
                for w, (lo, cols) in enumerate(((0, WIN), (WIN, PK - WIN))):
                    u = o * 2 + w
                    proj_free(pe, n, par, u)
                    bank = proj[u % 3]
                    for ci in range(CH):
                        last = split_matmul(nc, bank[:, 0:cols],
                                            (c["wh"][:, 1, ci, o * P:(o + 1) * P], c["wl"][:, 1, ci, o * P:(o + 1) * P]),
                                            (ctx_hi[par][:, ci, lo:lo + cols], ctx_lo[par][:, ci, lo:lo + cols]),
                                            ci == 0, ci == CH - 1)
                    last.then_inc(S["proj_ready"], 1)

        def proj_free(pe, n, par, u):
            if u == 0:
                wait(pe, S["k_lo_ready"], n * 4)
                wait(pe, S["p_last_ready"], n - 1)
            elif u == 1:
                wait(pe, S["masked"], n * 8 - 2)
            elif u == 2:
                wait(pe, S["oT_ready"], n * 2 - 2)
            else:
                wait(pe, S["k_lo_ready"], n * 4 + u - 2)

        def pe_v(pe, n, par):
            for b in range(2):
                u = 4 + b
                proj_free(pe, n, par, u)
                bank = proj[u % 3]
                for kt in range(2):
                    lo = b * KEYS + kt * P
                    for ci in range(CH):
                        last = split_matmul(nc, bank[:, kt * DM:(kt + 1) * DM],
                                            (ctx_hi[par][:, ci, lo:lo + P], ctx_lo[par][:, ci, lo:lo + P]),
                                            (c["wh"][:, 2, ci, :], c["wl"][:, 2, ci, :]), ci == 0, ci == CH - 1)
                last.then_inc(S["proj_ready"], 1)

        def pe_scores(pe, n, par, first, end):
            for i in range(first, end):
                b, g = i // 4, i % 4
                off = 0 if b == 0 else KEYS - 1
                if g == 0:
                    pe.wait_ge(S["q_ready"], n * 2 + b + 1)
                if i == 0:
                    pe.wait_ge(S["k_lo_ready"], n * 4 + 4)
                    wait(pe, S["masked"], n * 8 - 1)
                elif i == 1:
                    wait(pe, S["masked"], n * 8)
                elif i == 2:
                    pe.wait_ge(S["v_ready"], n * 2 + 1)
                else:
                    pe.wait_ge(S["masked"], n * 8 + i - 2)
                ci, q0 = g // 2, (g % 2) * P
                qh = q_hi[b][:, ci, :, :].rearrange("p h q -> p (h q)")[:, q0:q0 + P]
                ql = q_lo[b][:, ci, :, :].rearrange("p h q -> p (h q)")[:, q0:q0 + P]
                split_matmul(nc, sc[i % 3][:, 0:WIN], (qh, ql),
                             (k_hi[:, ci, off:off + WIN], k_lo[:, ci, off:off + WIN]), True, True
                             ).then_inc(S["s_ready"], 1)

        def pe_transposes(pe, p, b):
            pe.wait_ge(S["norm_ready"], p * 2 + b + 1)
            for kt in range(2):
                wait(pe, S[f"pT{kt}_ready"], p * 2 + b)
                for g in range(4):
                    last = nc.tensor.transpose(tp[kt][:, g * P:(g + 1) * P], prob[:, b, g, kt * P:(kt + 1) * P],
                                               c["ident"][:, :])
                last.then_inc(S["t_ready"], 1)

        def pe_last_transpose(pe, p, last_pair=False):
            pe.wait_ge(S["k_lo_ready"], p * 4 + 8 if not last_pair else p * 4 + 4)
            wait(pe, S["p_last_ready"], p)
            nc.tensor.transpose(last_ps, prob[:, :, :, KEYS - 1].rearrange("p b g -> p (b g)"), c["ident"][:, :]
                                ).then_inc(S["t_last_ready"], 1)

        def pe_av(pe, p, ppar, b, g):
            if g == 0:
                pe.wait_ge(S["pT0_ready"], p * 2 + b + 1)
                pe.wait_ge(S["pT1_ready"], p * 2 + b + 1)
                pe.wait_ge(S["p_last_ready"], p + 1)
                pe.wait_ge(S["v_ready"], p * 2 + b + 1)
                pe.wait_ge(S[f"v_last_in{ppar}"], so_far(p, ppar) * 32)
                wait(pe, S["oT_ready"], p * 2 + b - 1)
            for kt in range(3):
                for j in range(4):
                    h0 = g * 8 + 2 * j
                    hd = slice(g * P + 32 * j, g * P + 32 * j + 32)
                    out = o_ps[b][32 * j:32 * j + 32, g * 64:(g + 1) * 64]
                    if kt < 2:
                        last = nc.tensor.matmul(out, v_sb[ppar][:, b, kt, hd], pT[b][:, kt, h0 * SEQ:(h0 + 2) * SEQ],
                                                start=kt == 0, stop=False, tile_position=(0, 32 * j))
                    else:
                        q0 = (h0 % 4) * SEQ
                        last = nc.tensor.matmul(out, v_last[ppar][0:8, b, hd], p_last[0:8, q0:q0 + 2 * SEQ],
                                                start=False, stop=True, tile_position=(0, 32 * j))
            if g == CH - 1:
                last.then_inc(S["av_ready"], 1)

        def pe_out(pe, t):
            pe.wait_ge(S["oT_ready"], t * 4 + 4)
            wait(pe, S["x_ready"], t)
            for ci in range(CH):
                last = nc.tensor.matmul(yb, oT[:, ci, :], c["w_o"][:, ci, :], start=ci == 0, stop=ci == CH - 1)
            last.then_inc(S["y_ready"], 1)

        def pe_step(pe, n, par, t=None):
            pe_k(pe, n, par)
            if t is not None:
                pe_out(pe, t)
            later = not isinstance(n, int) or n > 0
            if later:
                pe_transposes(pe, n - 1, 0)
            pe_v(pe, n, par)
            if later:
                pe_transposes(pe, n - 1, 1)
                pe_last_transpose(pe, n - 1)
            done = 0
            for i, end in enumerate((3, 5, 7, 8)):
                pe_scores(pe, n, par, done, end)
                done = end
                if later:
                    pe_av(pe, n - 1, 1 - par, i // 2, i % 2)

        @block.tensor
        def _(pe):
            pe_step(pe, 0, 0)
            pe_step(pe, 1, 1)
            with pe.Fori(0, PAIRS // 2 - 1) as k:
                turn[0] = k
                pe_step(pe, k * 2 + 2, 0)
                pe_step(pe, k * 2 + 3, 1, k)
            pe_transposes(pe, PAIRS - 1, 0)
            pe_transposes(pe, PAIRS - 1, 1)
            pe_last_transpose(pe, PAIRS - 1, True)
            for b in range(2):
                for g in range(2):
                    pe_av(pe, PAIRS - 1, 1, b, g)
            pe_out(pe, NT - 1)

        def act_k(act, n, par, u):
            act.wait_ge(S["proj_ready"], n * NU + u + 1)
            if u == 0:
                wait(act, S["s_ready"], n * 8)
            o, w = u // 2, u % 2
            lo, cols = ((0, WIN), (WIN, PK - WIN))[w]
            nc.scalar.activation(k_hi[:, o, lo:lo + cols], proj[u % 3][:, 0:cols], ACT.Identity,
                                 bias=c["b_qk"][:, 1, o:o + 1]).then_inc(S["k_hi_ready"], 1)

        def act_ctx(act, n, par):
            arrived(act, n, par)
            wait(act, S["proj_ready"], (n - 1) * NU)
            nc.scalar.activation(ctx_hi[par][:, :, :], ctx_raw[par][:, :, :], ACT.Copy
                                 ).then_inc(S["ctx_hi_ready"], 1)

        def act_pT(act, p, b):
            act.wait_ge(S["t_ready"], p * 4 + b * 2 + 1)
            wait(act, S["av_ready"], p * 2 + b - 1)
            nc.scalar.activation(pT[b][:, 0, :], tp[0][:, :], ACT.Copy).then_inc(S["pT0_ready"], 1)

        def act_exp(act, n, b):
            wait(act, S["inv_ready"], n * 2 + b - 1)
            for g in range(4):
                act.wait_ge(S["masked"], n * 8 + b * 4 + g + 1)
                nc.scalar.activation(prob[:, b, g, :], prob[:, b, g, :], ACT.Exp, bias=least[b][:, g:g + 1],
                                     scale=-1.0, accum_out=total[b][:, g:g + 1]).then_inc(S["exp_ready"], 1)

        def act_norm(act, n, b, gs):
            if gs[0] == 0:
                act.wait_ge(S["inv_ready"], n * 2 + b + 1)
            for g in gs:
                last = nc.scalar.activation(prob[:, b, g, :], prob[:, b, g, :], ACT.Copy, scale=inv[b][:, g:g + 1])
            if gs[-1] == 3:
                last.then_inc(S["norm_ready"], 1)

        def act_step(act, n, par, more=True):
            later = not isinstance(n, int) or n > 0
            act_k(act, n, par, 0)
            if later:
                act_norm(act, n - 1, 0, (1, 2))
            act_k(act, n, par, 1)
            if later:
                act_norm(act, n - 1, 0, (3,))
            act_k(act, n, par, 2)
            act_k(act, n, par, 3)
            if later:
                act_norm(act, n - 1, 1, (0, 1))
                act_pT(act, n - 1, 0)
                act_norm(act, n - 1, 1, (2, 3))
                act_pT(act, n - 1, 1)
            if more:
                act_ctx(act, n + 1, 1 - par)
            act_exp(act, n, 0)
            act_exp(act, n, 1)
            act_norm(act, n, 0, (0,))

        @block.scalar
        def _(act):
            act_ctx(act, 0, 0)
            act_step(act, 0, 0)
            act_step(act, 1, 1)
            with act.Fori(0, PAIRS // 2 - 2) as k:
                turn[0] = k
                act_step(act, k * 2 + 2, 0)
                act_step(act, k * 2 + 3, 1)
            act_step(act, PAIRS - 2, 0)
            act_step(act, PAIRS - 1, 1, False)
            act_norm(act, PAIRS - 1, 0, (1, 2, 3))
            act_norm(act, PAIRS - 1, 1, (0, 1, 2, 3))
            act_pT(act, PAIRS - 1, 0)
            act_pT(act, PAIRS - 1, 1)

        def pool_ctx(pool, n, par):
            pool.wait_ge(S["ctx_hi_ready"], n + 1)
            nc.gpsimd.tensor_tensor(ctx_lo[par][:, :, :], ctx_raw[par][:, :, :], ctx_hi[par][:, :, :].bitcast(F32),
                                    ALU.subtract).then_inc(S["ctx_lo_ready"], 1)

        def pool_q(pool, n, b):
            wait(pool, S["s_ready"], n * 8 - 4 + b * 4)
            for src, dst in ((c["qTh"], q_hi[b]), (c["qTl"], q_lo[b])):
                q = src[:, :, bass.ds((n * 2 + b) * SEQ, SEQ)].bitcast(F32)
                last = nc.gpsimd.tensor_tensor(
                    dst[:, :, :, :], q.unsqueeze(2).to_broadcast([P, CH, 8, SEQ]),
                    c["head_rows"][:, :].unsqueeze(1).unsqueeze(3).to_broadcast([P, CH, 8, SEQ]), ALU.mult)
            last.then_inc(S["q_ready"], 1)

        def pool_step(pool, n, par, more=True):
            pool_q(pool, n, 0)
            pool_q(pool, n, 1)
            if more:
                pool_ctx(pool, n + 1, 1 - par)

        @block.gpsimd
        def _(pool):
            pool_ctx(pool, 0, 0)
            for i in range(2):
                pool.memset(v_last[i][:, :, :], 0.0).then_inc(S["v_last_zero"], 1)
            pool_q(pool, 0, 0)
            pool_q(pool, 0, 1)
            pool_ctx(pool, 1, 1)
            pool_step(pool, 1, 1)
            with pool.Fori(0, PAIRS // 2 - 2) as k:
                turn[0] = k
                pool_step(pool, k * 2 + 2, 0)
                pool_step(pool, k * 2 + 3, 1)
            pool_step(pool, PAIRS - 2, 0)
            pool_step(pool, PAIRS - 1, 1, False)

        def dve_k(dve, n, par, u):
            dve.wait_ge(S["k_hi_ready"], n * 4 + u + 1)
            o, w = u // 2, u % 2
            lo, cols = ((0, WIN), (WIN, PK - WIN))[w]
            nc.vector.scalar_tensor_tensor(
                out=k_lo[:, o, lo:lo + cols], in0=proj[u % 3][:, 0:cols],
                scalar=c["b_qk"][:, 1, o:o + 1], in1=k_hi[:, o, lo:lo + cols].bitcast(F32),
                op0=ALU.add, op1=ALU.subtract).then_inc(S["k_lo_ready"], 1)

        def dve_pT(dve, p, b):
            dve.wait_ge(S["t_ready"], p * 4 + b * 2 + 2)
            wait(dve, S["av_ready"], p * 2 + b - 1)
            nc.vector.tensor_copy(pT[b][:, 1, :], tp[1][:, :]).then_inc(S["pT1_ready"], 1)

        def dve_v(dve, n, par, b):
            dve.wait_ge(S["proj_ready"], n * NU + 5 + b)
            wait(dve, S["av_ready"], n * 2 - 2)
            nc.vector.tensor_tensor(v_sb[par][:, b, :, :], proj[(4 + b) % 3][:, :].rearrange("p (k n) -> p k n", k=2),
                                    c["b_v"][:, :].unsqueeze(1).to_broadcast([P, 2, DM]), ALU.add
                                    ).then_inc(S["v_ready"], 1)

        def dve_p_last(dve, p):
            dve.wait_ge(S["t_last_ready"], p + 1)
            wait(dve, S["av_ready"], p * 2)
            nc.vector.tensor_copy(p_last[:, :], last_ps).then_inc(S["p_last_ready"], 1)

        def dve_mask_max(dve, n, units):
            for i in units:
                b, g = i // 4, i % 4
                off = b
                if g == 0:
                    wait(dve, S["t_ready"], (n - 1) * 4 + b * 2 + 2)
                    wait(dve, S["t_last_ready"], n)
                    wait(dve, S["exp_ready"], n * 8 + b * 4 - 4)
                dve.wait_ge(S["s_ready"], n * 8 + i + 1)
                settle(nc, spot[0:1, i:i + 1])
                nc.vector.tensor_tensor_reduce(
                    out=prob[:, b, g, :], in0=sc[i % 3][:, off:off + KEYS], in1=c["mask_add"][:, :],
                    scale=-SCALE, scalar=-NEG, op0=ALU.add, op1=ALU.min, accum_out=least[b][:, g:g + 1]
                ).then_inc(S["masked"], 1)

        def dve_inv(dve, n, b):
            dve.wait_ge(S["exp_ready"], n * 8 + b * 4 + 4)
            wait(dve, S["norm_ready"], n * 2 + b - 1)
            nc.vector.reciprocal(inv[b][:, :], total[b][:, :]).then_inc(S["inv_ready"], 1)

        def dve_o_even(dve, ch, p, b):
            dve.wait_ge(S["av_ready"], p * 2 + b + 1)
            o = o_ps[b].rearrange("p (g e q) -> p g e q", g=CH, e=2)
            ch.add(nc.vector.tensor_scalar(o_even[b][:, :, :], o[:, :, 0, :], c["odd_even"][:, 0:1], None, ALU.mult))

        def dve_o(dve, ch, p, ppar, b):
            ch.sync()
            o = o_ps[b].rearrange("p (g e q) -> p g e q", g=CH, e=2)
            if b == 0 and ppar == 0:
                wait(dve, S["y_ready"], so_far(p, ppar) - 1)
            q0 = (ppar * 2 + b) * SEQ
            nc.vector.scalar_tensor_tensor(out=oT[:, :, q0:q0 + SEQ], in0=o[:, :, 1, :], scalar=c["odd_even"][:, 1:2],
                                           in1=o_even[b][:, :, :], op0=ALU.mult, op1=ALU.add
                                           ).then_inc(S["oT_ready"], 1)

        def dve_x(dve, ch, t, part):
            if t is None:
                return
            if part == 0:
                dve.wait_ge(S["y_ready"], t + 1)
                xt = c["x_tok"][:, bass.ds(t, 1), :].rearrange("p a d -> p (a d)")
                nc.vector.tensor_tensor(xt, yb, xt, ALU.add).then_inc(S["x_ready"], 1)
            elif part == 1:
                dve.wait_ge(S["x_ready"], t + 1)
                settle(nc, spot[0:1, 8:9])
                xt = c["x_tok"][:, bass.ds(t, 1), :].rearrange("p a d -> p (a d)")
                ch.add(nc.vector.bn_stats(stats[:, :], xt))
            elif part == 2:
                ch.sync()
                settle(nc, spot[0:1, 9:10])
                ch.add(nc.vector.bn_aggr(mv_tile[:, :], stats[:, :]))
            else:
                ch.sync()
                ch.add(nc.vector.tensor_copy(c["mv"][:, bass.ds(t, 1), :].rearrange("p a d -> p (a d)"), mv_tile[:, :]))

        def dve_step(dve, ch, n, par, t=None):
            later = not isinstance(n, int) or n > 0
            dve_k(dve, n, par, 0)
            if later:
                dve_inv(dve, n - 1, 1)
            dve_k(dve, n, par, 1)
            dve_k(dve, n, par, 2)
            dve_k(dve, n, par, 3)
            if later:
                dve_pT(dve, n - 1, 0)
            dve_x(dve, ch, t, 0)
            dve_v(dve, n, par, 0)
            dve_x(dve, ch, t, 1)
            dve_v(dve, n, par, 1)
            dve_x(dve, ch, t, 2)
            if later:
                dve_p_last(dve, n - 1)
            dve_mask_max(dve, n, (0, 1))
            if later:
                dve_pT(dve, n - 1, 1)
            dve_x(dve, ch, t, 3)
            dve_mask_max(dve, n, (2, 3, 4))
            if later:
                dve_o_even(dve, ch, n - 1, 0)
            dve_mask_max(dve, n, (5,))
            if later:
                dve_o(dve, ch, n - 1, 1 - par, 0)
            dve_mask_max(dve, n, (6, 7))
            dve_inv(dve, n, 0)
            if later:
                dve_o_even(dve, ch, n - 1, 1)
                dve_o(dve, ch, n - 1, 1 - par, 1)

        @block.vector
        def _(dve):
            ch = Chain(dve, S["dve_chain"])
            dve_step(dve, ch, 0, 0)
            dve_step(dve, ch, 1, 1)
            first = ch.n
            with dve.Fori(0, PAIRS // 2 - 2) as k:
                per = 2 * 2 + 3
                ch.at(k * per + first)
                turn[0] = k
                dve_step(dve, ch, k * 2 + 2, 0)
                dve_step(dve, ch, k * 2 + 3, 1, k)
                assert ch.n == per
            ch.at(first + per * (PAIRS // 2 - 2))
            dve_step(dve, ch, PAIRS - 2, 0)
            dve_step(dve, ch, PAIRS - 1, 1, NT - 2)
            dve_inv(dve, PAIRS - 1, 1)
            dve_pT(dve, PAIRS - 1, 0)
            dve_pT(dve, PAIRS - 1, 1)
            dve_p_last(dve, PAIRS - 1)
            for b in range(2):
                dve_o_even(dve, ch, PAIRS - 1, b)
                dve_o(dve, ch, PAIRS - 1, 1, b)
            for part in range(4):
                dve_x(dve, ch, NT - 1, part)
            ch.sync()


HALF = 2
HB = NB // HALF
HTOK = TOK // HALF
HBATCH = BATCH // HALF
WG, WD = 2 * CH * P, DM


def recurrent(nc, a, c, xTh, xTl):
    with ExitStack() as ctx:
        m = Mem(nc, ctx, "rec")
        xpad = [m.sb(f"xpad{i}", [P, BPB, SEQ + TAPS - 1]) for i in range(2)]
        conv = m.sb("conv", [P, ECH, TOK])
        state = m.sb("state", [P, HTOK])
        rows = [slice(half * 32, half * 32 + NS) for half in range(HALF)]
        h_block = m.sb("h_block", [NS, BLK])
        step_sum = m.sb("step_sum", [P, HBATCH])
        y = m.sb("y", [P, ECH, BLK])
        spot = m.sb("spot", [1, 4])
        stats, mv_tile = m.sb("stats", [P, 6]), m.sb("mv_tile", [P, 2])
        proj = [m.ps(f"proj{i}") for i in range(2)]
        up = m.ps("up", (NS, 512))
        yp = [m.ps(f"yp{i}") for i in range(2)]
        op = [m.ps(f"op{i}") for i in range(2)]
        S = {k: m.sem(k) for k in ("proj_ready", "x_part", "conv_start", "padded", "conv_step", "conv_ready",
                                   "up_ready", "u_ready", "sum_ready", "h_ready", "h_block_ready", "gate_ready",
                                   "sig_ready", "yp_ready",
                                   "dir_ready", "gated", "y_ready", "op_ready", "x_ready", "biased", "stat_step")}
        block = ctx.enter_context(nc.Block())
        HY = BLK // 2
        rstd_dve, rstd_act = inverse_deviation(nc, m, c)
        w_in = [m.sem(f"w_in{i}") for i in range(CH)]
        w_raw = conv[:, ECH - 1, HTOK:].rearrange("p (c n) -> p c n", c=CH)
        rest_in, w_high, w_low = m.sem("rest_in"), m.sem("w_high"), m.sem("w_low")
        norm = NormStage(nc, m, c, y[:, 0:2, :].rearrange("p a n -> p (a n)"), yp, xTh, xTl)

        @block.sync
        def _(sp):
            for i in range(CH):
                sp.dma_start(w_raw[:, i, :], a["W_in"][i * P:(i + 1) * P, :]).then_inc(w_in[i], 16)
            for name, src in (("A", a["A"].rearrange("(c p) n -> p c n", p=P)), ("C_T", a["C_T"]),
                              ("w_out", a["W_out"].rearrange("(c p) n -> p c n", p=P)), ("cols", a["cols"]),
                              ("b_out", a["b_out"])):
                dst = c[name]
                sp.dma_start(dst[tuple([slice(None)] * len(dst.shape))], src).then_inc(rest_in, 16)

        @block.tensor
        def _(pe):
            def product(bank, e, cols):
                for ci in range(CH):
                    last = split_matmul(nc, bank[:, :], (c["wih"][:, ci, e * P:(e + 1) * P],
                                                         c["wil"][:, ci, e * P:(e + 1) * P]),
                                        (xTh[:, ci, cols], xTl[:, ci, cols]), ci == 0, ci == CH - 1)
                return last

            def inputs(g, before=None, more=True):
                norm.ready(pe, g)
                for j in range(ECH):
                    wait(pe, S["x_part"], g * ECH + j - 1)
                    product(proj[j % 2], j, bass.ds(g * BLK, BLK)).then_inc(S["proj_ready"], 1)
                    if j == 1 and more:
                        norm.transposes(pe, g + 1)
                    if j == 2 and before is not None:
                        state_inputs(before)

            def state_inputs(g):
                pe.wait_ge(S["conv_ready"], g * ECH + ECH)
                wait(pe, S["u_ready"], g)
                for j in range(ECH):
                    last = nc.tensor.matmul(up[:, :], c["A"][:, j, :], conv[:, j, bass.ds(g * BLK, BLK)],
                                            start=j == 0, stop=j == ECH - 1)
                last.then_inc(S["up_ready"], 1)

            def gates(g, js):
                for j in js:
                    if isinstance(g, int) and g == 0 and j < 2:
                        pe.wait_ge(S["x_part"], NB * ECH - 1 + j)
                    else:
                        pe.wait_ge(S["gated"], g * ECH + j - 1)
                    product(proj[j % 2], ECH + j, bass.ds(g * BLK, BLK)).then_inc(S["gate_ready"], 1)

            def direct(g, js):
                pe.wait_ge(S["h_block_ready"], g + 1)
                for j in js:
                    wait(pe, S["dir_ready"], g * ECH + j - 1)
                    nc.tensor.matmul(yp[j % 2][:, :], c["C_T"][:, j * P:(j + 1) * P], h_block[:, :], start=True, stop=True
                                     ).then_inc(S["yp_ready"], 1)

            def outputs(g, ts):
                pe.wait_ge(S["y_ready"], g * 2 + ts[0] // 2 + 1)
                for t in ts:
                    wait(pe, S["x_ready"], g * TPB + t - 1)
                    for j in range(ECH):
                        last = nc.tensor.matmul(op[t % 2][:, 0:DM], y[:, j, t * P:(t + 1) * P], c["w_out"][:, j, :],
                                                start=j == 0, stop=j == ECH - 1)
                    last.then_inc(S["op_ready"], 1)

            def step(g):
                for js in ((0, 1), (2, 3)):
                    gates(g, js)
                    direct(g, js)
                    outputs(g - 1, js)

            norm.transposes(pe, 0)
            pe.wait_ge(w_low, CH)
            pe.wait_ge(rest_in, 5 * 16)
            inputs(0)
            with pe.Fori(1, NB - 1) as g:
                inputs(g, g - 1)
            inputs(NB - 1, NB - 2, False)
            gates(0, (0, 1))
            state_inputs(NB - 1)
            direct(0, (0, 1))
            gates(0, (2, 3))
            direct(0, (2, 3))
            step(1)
            with pe.Fori(2, NB) as g:
                step(g)
            outputs(NB - 1, (0, 1))
            outputs(NB - 1, (2, 3))

        @block.scalar
        def _(act):
            cv = c["cols"]

            def inputs(g, before=None, steps=None, more=True):
                cols = bass.ds(g * BLK, BLK)
                for j in range(ECH):
                    act.wait_ge(S["proj_ready"], g * ECH + j + 1)
                    wait(act, S["conv_ready"], g * ECH + j - 1)
                    nc.scalar.activation(xpad[j % 2][:, :, TAPS - 1:TAPS - 1 + SEQ],
                                         proj[j % 2][:, :].rearrange("p (b s) -> p b s", s=SEQ), ACT.Identity,
                                         bias=cv[:, j:j + 1]).then_inc(S["x_part"], 1)
                    if steps is not None:
                        recur(0, steps, j * 2)
                    act.wait_ge(S["x_part"], g * ECH + j + 1)
                    nc.scalar.activation(conv[:, j, cols].rearrange("p (b s) -> p b s", s=SEQ), xpad[j % 2][:, :, 0:SEQ],
                                         ACT.Identity, bias=cv[:, 8 + j:9 + j],
                                         scale=cv[:, 12 + j * TAPS:13 + j * TAPS]).then_inc(S["conv_start"], 1)
                    if j == 1 and more:
                        norm.high(act, g + 1)
                    if j == 2 and before is not None:
                        state_inputs(before, half_now[0])
                    if steps is not None:
                        recur(0, steps, j * 2 + 1)

            half_now = [0]

            def state_inputs(g, half):
                act.wait_ge(S["up_ready"], g + 1)
                nc.scalar.activation(state[rows[half], bass.ds((g - half * HB) * BLK, BLK)], up[:, :], ACT.Copy
                                     ).then_inc(S["u_ready"], 1)

            def block_of_states(g, half):
                wait(act, S["yp_ready"], g * ECH)
                act.wait_ge(S["h_ready"], (half + 1) * SEQ)
                nc.scalar.activation(h_block[:, :], state[rows[half], bass.ds((g - half * HB) * BLK, BLK)], ACT.Copy
                                     ).then_inc(S["h_block_ready"], 1)

            def recur(half, base, i):
                s = base + i
                if isinstance(s, int) and s < 0:
                    return
                hs = state[rows[half], :].rearrange("n (b s) -> n b s", s=SEQ)
                if isinstance(s, int) and s == 0:
                    act.wait_ge(S["u_ready"], (half + 1) * HB)
                    nc.scalar.activation(hs[:, :, 0], hs[:, :, 0], ACT.Tanh).then_inc(S["h_ready"], 1)
                else:
                    act.wait_ge(S["sum_ready"], half * (SEQ - 1) + s)
                    nc.scalar.activation(hs[:, :, bass.ds(s, 1)].rearrange("n b s -> n (b s)"),
                                         step_sum[rows[half], :], ACT.Tanh).then_inc(S["h_ready"], 1)

            def gates(g, js, steps=None):
                for j in js:
                    act.wait_ge(S["gate_ready"], g * ECH + j + 1)
                    nc.scalar.activation(proj[j % 2][:, :], proj[j % 2][:, :], ACT.Sigmoid,
                                         bias=cv[:, ECH + j:ECH + j + 1]).then_inc(S["sig_ready"], 1)
                    if steps is not None:
                        recur(1, steps, j * 2)
                        recur(1, steps, j * 2 + 1)

            def gated_block(g, part):
                act.wait_ge(S["gated"], g * ECH + ECH)
                wait(act, S["op_ready"], (g - 1) * TPB + part * 2 + 2)
                nc.scalar.activation(y[:, :, part * HY:(part + 1) * HY], conv[:, :, bass.ds(g * BLK + part * HY, HY)],
                                     ACT.Copy).then_inc(S["y_ready"], 1)

            rstd_act(act)
            for i in range(CH):
                act.wait_ge(w_in[i], 16)
                nc.scalar.activation(c["wih"][:, i, :], w_raw[:, i, :], ACT.Copy).then_inc(w_high, 1)
            act.wait_ge(S["padded"], 2)
            act.wait_ge(rest_in, 5 * 16)
            norm.high(act, 0)
            inputs(0)
            with act.Fori(1, HB) as g:
                inputs(g, g - 1)
            inputs(HB, HB - 1, -5)
            half_now[0] = 1
            with act.Fori(1, HB - 1) as q:
                inputs(q + HB, q + HB - 1, q * 8 - 5)
            inputs(NB - 1, NB - 2, (HB - 1) * 8 - 5, False)
            for i in range(5):
                recur(0, SEQ - 5, i)
            block_of_states(0, 0)
            gates(0, (0, 1))
            state_inputs(NB - 1, 1)
            gates(0, (2, 3), -4)
            gated_block(0, 0)
            gated_block(0, 1)
            for i in range(4):
                recur(1, 4, i)
            with act.Fori(1, HB) as g:
                block_of_states(g, 0)
                gates(g, (0, 1, 2, 3), g * 8)
                gated_block(g, 0)
                gated_block(g, 1)
            with act.Fori(HB, NB) as g:
                block_of_states(g, 1)
                gates(g, (0, 1, 2, 3))
                gated_block(g, 0)
                gated_block(g, 1)

        @block.gpsimd
        def _(pool):
            pool.memset(xpad[0][:, :, 0:TAPS - 1], 0.0).then_inc(S["padded"], 1)
            pool.memset(xpad[1][:, :, 0:TAPS - 1], 0.0).then_inc(S["padded"], 1)
            for half in range(HALF):
                hs = state[rows[half], :].rearrange("n (b s) -> n b s", s=SEQ)
                with pool.Fori(1, SEQ) as s:
                    pool.wait_ge(S["h_ready"], s + half * SEQ)
                    nc.gpsimd.tensor_tensor(step_sum[rows[half], :],
                                            hs[:, :, bass.ds(s, 1)].rearrange("n b s -> n (b s)"),
                                            hs[:, :, bass.ds(s - 1, 1)].rearrange("n b s -> n (b s)"), ALU.add
                                            ).then_inc(S["sum_ready"], 1)

        @block.vector
        def _(dve):
            dve.wait_ge(S["padded"], 2)
            cv = c["cols"]

            def convolution(g, turned=True, normalised=True):
                for j in range(ECH):
                    if j == 2 and turned:
                        norm.low(dve, g + 1)
                        if normalised:
                            norm.normalise(dve, g + 2)
                    dve.wait_ge(S["conv_start"], g * ECH + j + 1)
                    acc = conv[:, j, bass.ds(g * BLK, BLK)].rearrange("p (b s) -> p b s", s=SEQ)
                    for i in range(1, TAPS):
                        if i > 1:
                            dve.wait_ge(S["conv_step"], (g * ECH + j) * (TAPS - 2) + i - 1)
                        ins = nc.vector.scalar_tensor_tensor(
                            out=acc, in0=xpad[j % 2][:, :, i:i + SEQ],
                            scalar=cv[:, 12 + j * TAPS + i:13 + j * TAPS + i], in1=acc, op0=ALU.mult, op1=ALU.add)
                        ins.then_inc(S["conv_ready"] if i == TAPS - 1 else S["conv_step"], 1)

            def gated(g, js):
                for j in js:
                    part = conv[:, j, bass.ds(g * BLK, BLK)]
                    dve.wait_ge(S["yp_ready"], g * ECH + j + 1)
                    nc.vector.scalar_tensor_tensor(
                        out=part, in0=part, scalar=cv[:, 28 + j:29 + j],
                        in1=yp[j % 2][:, :], op0=ALU.mult, op1=ALU.add).then_inc(S["dir_ready"], 1)
                    dve.wait_ge(S["sig_ready"], g * ECH + j + 1)
                    dve.wait_ge(S["dir_ready"], g * ECH + j + 1)
                    nc.vector.tensor_tensor(part, proj[j % 2][:, :], part, ALU.mult).then_inc(S["gated"], 1)

            def outputs(g, ts):
                for t in ts:
                    ti = g * TPB + t
                    xt = c["x_tok"][:, bass.ds(ti, 1), :].rearrange("p a d -> p (a d)")
                    nc.vector.tensor_tensor(xt, xt, c["b_out"][:, :], ALU.add).then_inc(S["biased"], 1)
                    dve.wait_ge(S["biased"], ti + 1)
                    dve.wait_ge(S["op_ready"], ti + 1)
                    nc.vector.tensor_tensor(xt, op[t % 2][:, 0:DM], xt, ALU.add).then_inc(S["x_ready"], 1)
                    dve.wait_ge(S["x_ready"], ti + 1)
                    settle(nc, spot[0:1, (t % 2) * 2:(t % 2) * 2 + 1])
                    nc.vector.bn_stats(stats[:, :], xt).then_inc(S["stat_step"], 1)
                    dve.wait_ge(S["stat_step"], ti * 3 + 1)
                    settle(nc, spot[0:1, (t % 2) * 2 + 1:(t % 2) * 2 + 2])
                    nc.vector.bn_aggr(mv_tile[:, :], stats[:, :]).then_inc(S["stat_step"], 1)
                    dve.wait_ge(S["stat_step"], ti * 3 + 2)
                    nc.vector.tensor_copy(c["mv"][:, bass.ds(ti, 1), :].rearrange("p a d -> p (a d)"), mv_tile[:, :]
                                          ).then_inc(S["stat_step"], 1)

            rstd_dve(dve)
            norm.normalise(dve, 0)
            for i in range(CH):
                dve.wait_ge(w_high, i + 1)
                nc.vector.tensor_tensor(c["wil"][:, i, :], w_raw[:, i, :], c["wih"][:, i, :].bitcast(F32),
                                        ALU.subtract).then_inc(w_low, 1)
            dve.wait_ge(rest_in, 5 * 16)
            norm.normalise(dve, 1)
            norm.low(dve, 0)
            with dve.Fori(0, NB - 2) as g:
                convolution(g)
            convolution(NB - 2, True, False)
            convolution(NB - 1, False)
            gated(0, (0, 1, 2, 3))
            with dve.Fori(1, NB) as g:
                for js in ((0, 1), (2, 3)):
                    gated(g, js)
                    outputs(g - 1, js)
            outputs(NB - 1, (0, 1, 2, 3))
            dve.wait_ge(S["stat_step"], NT * 3)


def routing(nc, a, c, xTh, xTl):
    with ExitStack() as ctx:
        m = Mem(nc, ctx, "rt")
        gw_raw = m.sb("gw_raw", [P, CH, P])
        gwh, gwl = m.sb("gwh", [P, CH, P], F32R), m.sb("gwl", [P, CH, P], F32R)
        e_bias = m.sb("e_bias", [P, NE])
        logT = m.sb("logT", [NE, TOK])
        score, choice = m.sb("score", [P, NT, NE]), m.sb("choice", [P, NT, NE])
        beats = [m.sb(f"beats{i}", [P, NT, NE]) for i in range(3)]
        rank, grank = m.sb("rank", [P, NT, NE]), m.sb("grank", [P, NT, NG])
        wins, gwins = m.sb("wins", [P, NT, NE]), m.sb("gwins", [P, NT, NG])
        pair = [m.sb(f"pair{i}", [P, NT, NG]) for i in range(8)]
        norm = [m.sb(f"norm{i}", [P, NT]) for i in range(2)]
        weight = c["weight"][:, :, :]
        rstd_dve, rstd_act = inverse_deviation(nc, m, c)
        norm_block = NormStage(nc, m, c, m.sb("xn", [P, TPB * DM]), [m.ps(f"tp{i}") for i in range(CH)], xTh, xTl)
        lg = [m.ps(f"lg{i}") for i in range(2)]
        tk = m.ps("tk")
        w_raw = m.sb("w_raw", [P, WG + WD])
        w_hi, w_lo = m.sb("w_hi", [P, WG + WD], F32R), m.sb("w_lo", [P, WG + WD], F32R)
        act_g, up_sb = ([m.sb(f"{k}{i}", [P, BLK]) for i in range(2)] for k in ("act_g", "up_sb"))
        h = m.sb("h", [P, BLK])
        h_hi, h_lo = m.sb("h_hi", [P, BLK], F32R), m.sb("h_lo", [P, BLK], F32R)
        y_sb = m.sb("y_sb", [P, TPB * DM])
        gp, up, yp = [lg[0], m.ps("gp1")], [lg[1], m.ps("up1")], norm_block.tp
        S = {k: m.sem(k) for k in ("gw_in", "bias_in", "zeroed", "gw_ready", "lg_ready", "logT_ready", "tk_ready",
                                   "score_ready", "chain", "w_in", "w_ready", "g_ready", "u_ready", "act_ready", "up_ready",
                                   "h_ready", "h_hi_ready", "h_lo_ready", "y_ready", "y_read", "x_ready", "next_in")}
        block = ctx.enter_context(nc.Block())

        @block.sync
        def _(sp):
            sp.wait_ge(S["zeroed"], 1)
            sp.dma_start(gw_raw[:, :, 0:NE], a["gate_wT"].rearrange("(c p) n -> p c n", p=P)).then_inc(S["gw_in"], 16)
            sp.dma_start(e_bias[:, :], a["e_bias"]).then_inc(S["bias_in"], 16)
            sp.dma_start(w_raw[:, :], a["w_exp"][0]).then_inc(S["w_in"], 16)
            for e in range(2):
                sp.dma_start(c["w_raw"][e][:, :], a["w_exp"][e + 1]).then_inc(S["next_in"], 16)
            sp.wait_ge(S["next_in"], 32)

        LATE = NB - 4

        def add(pool, b):
            pool.wait_ge(S["y_read"], b + 1)
            xb = c["x_tok"][:, b * TPB:(b + 1) * TPB, :].rearrange("p t d -> p (t d)")
            pool.tensor_tensor(xb, xb, y_sb[:, :], ALU.add).then_inc(S["x_ready"], 1)

        @block.gpsimd
        def _(pool):
            pool.memset(gw_raw[:, :, :], 0.0).then_inc(S["zeroed"], 1)
            pool.memset(gwins[:, :, :], 0.0)
            pool.memset(wins[:, :, :], 0.0)
            for i in range(NG):
                last = pool.memset(grank[:, :, i:i + 1], float(NG - 1 - i))
            for i in range(NE):
                last = pool.memset(rank[:, :, i:i + 1], float(NE - 1 - i))
            last.then_inc(S["zeroed"], 1)

            for b in range(NB):
                pool.wait_ge(S["act_ready"], b + 1)
                pool.wait_ge(S["up_ready"], b + 1)
                wait(pool, S["h_lo_ready"], b)
                pool.tensor_tensor(h[:, :], act_g[b % 2][:, :], up_sb[b % 2][:, :], ALU.mult).then_inc(S["h_ready"], 1)
                if 2 <= b < LATE + 2:
                    add(pool, b - 2)
                pool.wait_ge(S["h_hi_ready"], b + 1)
                wait(pool, S["y_ready"], b)
                pool.tensor_tensor(h_lo[:, :], h[:, :], h_hi[:, :].bitcast(F32), ALU.subtract
                                   ).then_inc(S["h_lo_ready"], 1)
            pool.wait_ge(S["x_ready"], LATE)

        @block.tensor
        def _(pe):
            norm_block.transposes(pe, 0)
            pe.wait_ge(S["gw_ready"], 2)
            for n in range(NB):
                if n < NB - 1:
                    norm_block.transposes(pe, n + 1)
                norm_block.ready(pe, n)
                wait(pe, S["logT_ready"], n - 1)
                for ci in range(CH):
                    cols = slice(n * BLK, (n + 1) * BLK)
                    last = split_matmul(nc, lg[n % 2][:, :], (gwh[:, ci, :], gwl[:, ci, :]),
                                        (xTh[:, ci, cols], xTl[:, ci, cols]), ci == 0, ci == CH - 1)
                last.then_inc(S["lg_ready"], 1)
            pe.wait_ge(S["logT_ready"], NB)
            for t in range(NT):
                last = nc.tensor.transpose(tk[:, t * NE:(t + 1) * NE], logT[:, t * P:(t + 1) * P],
                                           c["ident"][0:NE, 0:NE])
            last.then_inc(S["tk_ready"], 1)

            def down(b):
                pe.wait_ge(S["h_lo_ready"], b + 1)
                if b == 0:
                    pe.wait_ge(norm_block.lo_ready, NB * CH)
                wait(pe, S["y_read"], b)
                for t in range(TPB):
                    hs = slice(t * P, (t + 1) * P)
                    last = split_matmul(nc, yp[t // 2][:, t % 2 * DM:(t % 2 + 1) * DM], (h_hi[:, hs], h_lo[:, hs]),
                                        (w_hi[:, WG:WG + WD], w_lo[:, WG:WG + WD]), True, True)
                last.then_inc(S["y_ready"], 1)

            pe.wait_ge(S["w_ready"], 2)

            def gate_and_up(b):
                cols = slice(b * BLK, (b + 1) * BLK)
                for kind, bank, done, read in ((0, gp, "g_ready", "act_ready"), (1, up, "u_ready", "up_ready")):
                    wait(pe, S[read], b - 1)
                    for ci in range(CH):
                        w0 = (kind * CH + ci) * P
                        last = split_matmul(nc, bank[b % 2][:, :], (w_hi[:, w0:w0 + P], w_lo[:, w0:w0 + P]),
                                            (xTh[:, ci, cols], xTl[:, ci, cols]), ci == 0, ci == CH - 1)
                    last.then_inc(S[done], 1)

            gate_and_up(0)
            gate_and_up(1)
            for b in range(NB):
                if b + 2 < NB:
                    gate_and_up(b + 2)
                down(b)

        @block.scalar
        def _(act):
            rstd_act(act)
            norm_block.high(act, 0)
            for n in range(NB):
                if n < NB - 1:
                    norm_block.high(act, n + 1)
                act.wait_ge(S["lg_ready"], n + 1)
                nc.scalar.activation(logT[:, n * BLK:(n + 1) * BLK], lg[n % 2][0:NE, :], ACT.Copy
                                     ).then_inc(S["logT_ready"], 1)
            act.wait_ge(S["tk_ready"], 1)
            nc.scalar.activation(score[:, :, :].rearrange("p t e -> p (t e)"), tk[:, :], ACT.Sigmoid
                                 ).then_inc(S["score_ready"], 1)

            def read_out(b):
                act.wait_ge(S["y_ready"], b + 1)
                wait(act, S["x_ready"], b)
                for i in range(2):
                    last = nc.scalar.activation(y_sb[:, i * BLK:(i + 1) * BLK], yp[i][:, :], ACT.Copy)
                last.then_inc(S["y_read"], 1)

            def gate_and_up(b):
                wait(act, S["h_ready"], b - 1)
                act.wait_ge(S["g_ready"], b + 1)
                nc.scalar.activation(act_g[b % 2][:, :], gp[b % 2][:, :], ACT.Silu).then_inc(S["act_ready"], 1)
                act.wait_ge(S["u_ready"], b + 1)
                nc.scalar.activation(up_sb[b % 2][:, :], up[b % 2][:, :], ACT.Copy).then_inc(S["up_ready"], 1)

            gate_and_up(0)
            for b in range(NB):
                if b + 1 < NB:
                    gate_and_up(b + 1)
                act.wait_ge(S["h_ready"], b + 1)
                wait(act, S["y_ready"], b)
                nc.scalar.activation(h_hi[:, :], h[:, :], ACT.Copy).then_inc(S["h_hi_ready"], 1)
                if 0 < b <= LATE:
                    read_out(b - 1)

        @block.vector
        def _(dve):
            ch = Chain(dve, S["chain"])
            rstd_dve(dve)
            norm_block.normalise(dve, 0)
            dve.wait_ge(S["gw_in"], 16)
            nc.vector.tensor_copy(gwh[:, :, :], gw_raw[:, :, :]).then_inc(S["gw_ready"], 1)
            dve.wait_ge(S["gw_ready"], 1)
            nc.vector.tensor_tensor(gwl[:, :, :], gw_raw[:, :, :], gwh[:, :, :].bitcast(F32), ALU.subtract
                                    ).then_inc(S["gw_ready"], 1)
            for n in range(NB):
                if n < NB - 1:
                    norm_block.normalise(dve, n + 1)
                norm_block.low(dve, n)
                if n == 2:
                    dve.wait_ge(S["w_in"], 16)
                    nc.vector.tensor_copy(w_hi[:, :], w_raw[:, :]).then_inc(S["w_ready"], 1)
                    dve.wait_ge(S["w_ready"], 1)
                    nc.vector.tensor_tensor(w_lo[:, :], w_raw[:, :], w_hi[:, :].bitcast(F32), ALU.subtract
                                            ).then_inc(S["w_ready"], 1)
            dve.wait_ge(S["score_ready"], 1)
            dve.wait_ge(S["bias_in"], 16)
            dve.wait_ge(S["zeroed"], 2)
            tt = nc.vector.tensor_tensor
            ch.link(tt(choice[:, :, :], score[:, :, :], e_bias[:, :].unsqueeze(1).to_broadcast([P, NT, NE]), ALU.add))
            four = [choice[:, :, :].rearrange("p t (g i) -> p t g i", i=PG)[:, :, :, i] for i in range(PG)]
            q = [x[:, :, :] for x in pair]
            ch.add(tt(q[0], four[0], four[1], ALU.max))
            ch.add(tt(q[1], four[0], four[1], ALU.min))
            ch.add(tt(q[2], four[2], four[3], ALU.max))
            ch.link(tt(q[3], four[2], four[3], ALU.min))
            ch.add(tt(q[4], q[0], q[2], ALU.max))
            ch.add(tt(q[5], q[0], q[2], ALU.min))
            ch.link(tt(q[6], q[1], q[3], ALU.max))
            ch.link(tt(q[7], q[5], q[6], ALU.max))
            ch.link(tt(q[0], q[4], q[7], ALU.add))

            def trail(ins):
                ch.add(ins)
                wait(dve, S["chain"], ch.n - 2)

            def ranks(value, place, won, n):
                def compare(d):
                    trail(tt(beats[d % 3][:, :, 0:n - d], value[:, :, 0:n - d], value[:, :, d:n], ALU.is_ge))

                ch.sync()
                compare(1)
                for d in range(1, n):
                    if d + 1 < n:
                        compare(d + 1)
                    if d == 1 or d + 1 == n:
                        ch.sync()
                    b = beats[d % 3][:, :, 0:n - d]
                    trail(tt(place[:, :, d:n], place[:, :, d:n], b, ALU.add))
                    trail(tt(won[:, :, 0:n - d], won[:, :, 0:n - d], b, ALU.add))
                ch.sync()
                ch.link(tt(place[:, :, :], place[:, :, :], won[:, :, :], ALU.subtract))

            ranks(q[0], grank, gwins, NG)
            ch.link(nc.vector.tensor_scalar(q[1], grank[:, :, :], 2.0, None, ALU.is_lt))
            ch.link(tt(choice[:, :, :].rearrange("p t (g i) -> p (t g) i", i=PG),
                       choice[:, :, :].rearrange("p t (g i) -> p (t g) i", i=PG),
                       pair[1][:, :, :].rearrange("p t g -> p (t g)").unsqueeze(2).to_broadcast([P, NT * NG, PG]),
                       ALU.mult))
            ranks(choice, rank, wins, NE)
            ch.link(nc.vector.tensor_scalar(beats[0][:, :, :], rank[:, :, :], 4.0, None, ALU.is_lt))
            ch.link(tt(weight, score[:, :, :], beats[0][:, :, :], ALU.mult))
            ch.link(nc.vector.reduce_sum(norm[0][:, :], weight, AX))
            ch.link(nc.vector.tensor_scalar(norm[0][:, :], norm[0][:, :], 1e-20, None, ALU.add))
            ch.link(nc.vector.reciprocal(norm[1][:, :], norm[0][:, :]))
            ch.link(tt(weight, weight, norm[1][:, :].unsqueeze(2).to_broadcast([P, NT, NE]), ALU.mult))
            ch.link(nc.vector.tensor_scalar(weight, weight, 2.5, None, ALU.mult))
            for b in range(LATE, NB):
                dve.wait_ge(S["y_ready"], b + 1)
                for i in range(2):
                    xb = c["x_tok"][:, b * TPB + 2 * i:b * TPB + 2 * i + 2, :].rearrange("p t d -> p (t d)")
                    last = tt(xb, xb, yp[i][:, :], ALU.add)
                last.then_inc(S["y_read"], 1)
            dve.wait_ge(S["y_read"], NB)


def experts(nc, a, c, xTh, xTl, out):
    with ExitStack() as ctx:
        m = Mem(nc, ctx, "ex")
        w_raw = c["w_raw"]
        w_hi = [m.sb(f"w_hi{i}", [P, WG + WD], F32R) for i in range(2)]
        w_lo = [m.sb(f"w_lo{i}", [P, WG + WD], F32R) for i in range(2)]
        act_g = m.sb("act_g", [P, BLK])
        h = [m.sb(f"h{i}", [P, BLK]) for i in range(2)]
        h_hi = [m.sb(f"h_hi{i}", [P, BLK], F32R) for i in range(2)]
        h_lo = [m.sb(f"h_lo{i}", [P, BLK], F32R) for i in range(2)]
        gp = [m.ps(f"gp{i}") for i in range(2)]
        up = [m.ps(f"up{i}") for i in range(2)]
        yp = m.ps("yp", (P, TPB, DM))
        S = {k: m.sem(k) for k in ("w_in0", "w_in1", "w_hi_ready", "w_lo_ready", "g_ready", "u_ready",
                                   "act_ready", "h_ready", "h_hi_ready", "h_lo_ready",
                                   "y_ready", "x_ready", "stored")}
        block = ctx.enter_context(nc.Block())

        def over_experts(eng, first, other, end):
            def expert(e, par):
                first(e, par)
                other(e, 1, par, 1)
                with eng.Fori(1, NB // 2) as k:
                    other(e, k * 2, par, 0)
                    other(e, k * 2 + 1, par, 1)
            expert(0, 0)
            with eng.Fori(0, NE // 2 - 1) as k:
                expert(k * 2 + 1, 1)
                expert(k * 2 + 2, 0)
            expert(NE - 1, 1)
            end()

        def of(e, b):
            return e * NB + b

        @block.sync
        def _(sp):
            def load(e, par):
                if not isinstance(e, int):
                    e = sp.snap(e)
                wait(sp, S["w_lo_ready"], e - 1)
                sp.dma_start(w_raw[par][:, :], a["w_exp"][bass.ds(e + 1, 1), :, :].rearrange("a p n -> (a p) n")
                             ).then_inc(S[f"w_in{par}"], 16)
            with sp.Fori(1, NE // 2) as k:
                load(k * 2, 0)
                load(k * 2 + 1, 1)
            for b in range(NB):
                sp.wait_ge(S["x_ready"], of(NE - 1, b) + 1)
                sp.dma_start(out[b * BLK:(b + 1) * BLK, :].rearrange("(t p) d -> p t d", p=P),
                             c["x_tok"][:, b * TPB:(b + 1) * TPB, :]).then_inc(S["stored"], 16)
            sp.wait_ge(S["stored"], NB * 16)

        @block.tensor
        def _(pe):
            def up_products(e, b, par, bpar):
                i = of(e, b)
                wait(pe, S["act_ready"], i - 1)
                wait(pe, S["h_ready"], i - 1)
                cols = bass.ds(b * BLK, BLK)
                for kind, bank, done in ((0, gp[bpar], "g_ready"), (1, up[bpar], "u_ready")):
                    for ci in range(CH):
                        w0 = (kind * CH + ci) * P
                        last = split_matmul(nc, bank[:, :], (w_hi[par][:, w0:w0 + P], w_lo[par][:, w0:w0 + P]),
                                            (xTh[:, ci, cols], xTl[:, ci, cols]), ci == 0, ci == CH - 1)
                    last.then_inc(S[done], 1)

            def down_product(i, par, bpar):
                pe.wait_ge(S["h_hi_ready"], i + 1)
                pe.wait_ge(S["h_lo_ready"], i + 1)
                wait(pe, S["x_ready"], i)
                for t in range(TPB):
                    hs = slice(t * P, (t + 1) * P)
                    last = split_matmul(nc, yp[:, t, :], (h_hi[bpar][:, hs], h_lo[bpar][:, hs]),
                                        (w_hi[par][:, WG:WG + WD], w_lo[par][:, WG:WG + WD]), True, True)
                last.then_inc(S["y_ready"], 1)

            def first(e, par):
                pe.wait_ge(S["w_lo_ready"], e + 1)
                up_products(e, 0, par, 0)
                if not (isinstance(e, int) and e == 0):
                    down_product(of(e, 0) - 1, 1 - par, 1)

            def other(e, b, par, bpar):
                up_products(e, b, par, bpar)
                down_product(of(e, b) - 1, par, 1 - bpar)

            over_experts(pe, first, other, lambda: down_product(NE * NB - 1, 1, 1))

        @block.scalar
        def _(act):
            def split(e, par):
                wait(act, S["w_in%d" % par], pair_of(e) * 16)
                wait(act, S["y_ready"], (e - 1) * NB)
                nc.scalar.activation(w_hi[par][:, :], w_raw[par][:, :], ACT.Copy).then_inc(S["w_hi_ready"], 1)

            def block_of(i, bpar):
                act.wait_ge(S["g_ready"], i + 1)
                wait(act, S["h_ready"], i)
                nc.scalar.activation(act_g[:, :], gp[bpar][:, :], ACT.Silu).then_inc(S["act_ready"], 1)
                act.wait_ge(S["h_ready"], i + 1)
                wait(act, S["y_ready"], i - 1)
                nc.scalar.activation(h_hi[bpar][:, :], h[bpar][:, :], ACT.Copy).then_inc(S["h_hi_ready"], 1)

            def pair_of(e):
                return e // 2 if isinstance(e, int) else half[0]

            half = [0]

            def expert(e, par, more=True):
                block_of(of(e, 0), 0)
                block_of(of(e, 1), 1)
                if more:
                    split(e + 1, 1 - par)
                with act.Fori(1, NB // 2) as k:
                    block_of(of(e, 0) + k * 2, 0)
                    block_of(of(e, 0) + k * 2 + 1, 1)

            split(0, 0)
            expert(0, 0)
            with act.Fori(0, NE // 2 - 1) as k:
                half[0] = k + 1
                expert(k * 2 + 1, 1)
                half[0] = k + 1
                expert(k * 2 + 2, 0)
            expert(NE - 1, 1, False)

        @block.gpsimd
        def _(pool):
            def low(i, bpar):
                pool.wait_ge(S["h_hi_ready"], i + 1)
                nc.gpsimd.tensor_tensor(h_lo[bpar][:, :], h[bpar][:, :], h_hi[bpar][:, :].bitcast(F32), ALU.subtract
                                        ).then_inc(S["h_lo_ready"], 1)

            with pool.Fori(0, NE * NB // 2) as k:
                low(k * 2, 0)
                low(k * 2 + 1, 1)

        @block.vector
        def _(dve):
            def prepare(e, par):
                wait(dve, S["y_ready"], (e - 1) * NB)
                dve.wait_ge(S["w_hi_ready"], e + 1)
                nc.vector.tensor_tensor(w_lo[par][:, :], w_raw[par][:, :], w_hi[par][:, :].bitcast(F32), ALU.subtract
                                        ).then_inc(S["w_lo_ready"], 1)

            def hidden(i, bpar):
                dve.wait_ge(S["act_ready"], i + 1)
                dve.wait_ge(S["u_ready"], i + 1)
                wait(dve, S["h_lo_ready"], i - 1)
                nc.vector.tensor_tensor(h[bpar][:, :], act_g[:, :], up[bpar][:, :], ALU.mult).then_inc(S["h_ready"], 1)

            def add(e, i, b):
                dve.wait_ge(S["y_ready"], i + 1)
                for t in range(TPB):
                    ti = b * TPB + t
                    xt = c["x_tok"][:, bass.ds(ti, 1), :].rearrange("p a d -> p (a d)")
                    last = nc.vector.scalar_tensor_tensor(
                        out=xt, in0=yp[:, t, :],
                        scalar=c["weight"][:, bass.ds(ti, 1), bass.ds(e, 1)].rearrange("p a b -> p (a b)"), in1=xt,
                        op0=ALU.mult, op1=ALU.add)
                last.then_inc(S["x_ready"], 1)

            def expert(e, par, more=True):
                i0 = of(e, 0)
                hidden(i0, 0)
                if not (isinstance(e, int) and e == 0):
                    add(e - 1, i0 - 1, NB - 1)
                hidden(i0 + 1, 1)
                add(e, i0, 0)
                if more:
                    prepare(e + 1, 1 - par)
                with dve.Fori(1, NB // 2) as k:
                    hidden(i0 + k * 2, 0)
                    add(e, i0 + k * 2 - 1, k * 2 - 1)
                    hidden(i0 + k * 2 + 1, 1)
                    add(e, i0 + k * 2, k * 2)

            prepare(0, 0)
            expert(0, 0)
            with dve.Fori(0, NE // 2 - 1) as k:
                expert(k * 2 + 1, 1)
                expert(k * 2 + 2, 0)
            expert(NE - 1, 1, False)
            add(NE - 1, NE * NB - 1, NB - 1)


def build(nc, a, out):
    with ExitStack() as ctx:
        m = Mem(nc, ctx, "g")
        c = {"x_tok": m.sb("x_tok", [P, NT, DM]), "mv": m.sb("mv", [P, NT, 2]), "rstd": m.sb("rstd", [P, NT]),
             "ident": m.sb("ident", [P, P])}
        with ExitStack() as actx:
            ma = Mem(nc, actx, "c")
            for name, shape, dt in (
                    ("head_rows", [P, 8], F32), ("odd_even", [P, 2], F32),
                    ("mask_add", [P, KEYS], F32), ("b_qk", [P, 2, CH], F32),
                    ("b_v", [P, DM], F32), ("b_o", [P, DM], F32), ("w_o", [P, CH, DM], F32),
                    ("wh", [P, 3, CH, DM], F32R), ("wl", [P, 3, CH, DM], F32R),
                    ("qTh", [P, CH, TOK], F32R), ("qTl", [P, CH, TOK], F32R)):
                c[name] = ma.sb(name, shape, dt)
            c["ctx_raw"] = [ma.sb(f"ctx_raw{i}", [P, CH, PK]) for i in range(2)]
            set_up(nc, a, c)
            with ExitStack() as tctx:
                mt = Mem(nc, tctx, "xt1")
                xTh, xTl = mt.sb("xTh", [P, CH, TOK], F32R), mt.sb("xTl", [P, CH, TOK], F32R)
                queries(nc, a, c, xTh, xTl)
            attention(nc, a, c)
        with ExitStack() as rctx:
            mr = Mem(nc, rctx, "r")
            for name, shape, dt in (
                    ("A", [P, ECH, NS], F32), ("C_T", [NS, EI], F32), ("w_out", [P, ECH, DM], F32),
                    ("cols", [P, 32], F32), ("b_out", [P, DM], F32),
                    ("wih", [P, CH, 2 * EI], F32R), ("wil", [P, CH, 2 * EI], F32R)):
                c[name] = mr.sb(name, shape, dt)
            xTh, xTl = mr.sb("xTh", [P, CH, TOK], F32R), mr.sb("xTl", [P, CH, TOK], F32R)
            recurrent(nc, a, c, xTh, xTl)
        with ExitStack() as ectx:
            me = Mem(nc, ectx, "e")
            xTh, xTl = me.sb("xTh", [P, CH, TOK], F32R), me.sb("xTl", [P, CH, TOK], F32R)
            c["weight"] = me.sb("weight", [P, NT, NE])
            c["w_raw"] = [me.sb(f"w_raw{i}", [P, WG + WD]) for i in range(2)]
            routing(nc, a, c, xTh, xTl)
            experts(nc, a, c, xTh, xTl, out)


def kernel(**inputs):
    import numpy as np
    import concourse.bacc as bacc
    from concourse.bass_utils import run_bass_kernel_spmd as run

    def f(name):
        return np.asarray(inputs[name])

    def padded_bytes(v):
        return np.pad(v.view(np.uint8)[..., None], ((0, 0), (0, 0), (0, 3))).view(np.int32)[..., 0]

    def per_row(v, n):
        return v.reshape(n, P).T

    arrays = {
        "x": f("x").reshape(TOK, DM),
        "ctxT": f("ctx_1024").reshape(BATCH * KEYS, CH, P).transpose(2, 1, 0),
        "ctx_lastT": f("ctx_1024")[:, KEYS - 1].reshape(BATCH, CH, P).transpose(2, 1, 0),
        "mask": padded_bytes(np.tile(f("mask_1x1xSxS2_bk0")[0, 0], (4, 1))),
        "Wq": f("L0_xattn_Wq"), "Wk": f("L0_xattn_Wk"), "Wv": f("L0_xattn_Wv"), "Wo": f("L0_xattn_Wo"),
        "b_qk": np.stack([per_row(f("L0_xattn_bq"), CH), per_row(f("L0_xattn_bk"), CH)], axis=1),
        "b_v": np.broadcast_to(f("L0_xattn_bv"), (P, DM)),
        "b_o": np.broadcast_to(f("L0_xattn_bo"), (P, DM)),
    }
    def transposed(w):
        return w.reshape(w.shape[0], P, CH, P).transpose(0, 3, 2, 1)

    gate, up, down = (np.concatenate([f(f"L0_ffn_shared_{s}")[None], f(f"L0_ffn_{r}")])
                      for s, r in (("gate_w", "gate_proj"), ("up_w", "up_proj"), ("down_w", "down_proj")))
    arrays |= {
        "W_in": f("L0_attn_W_in"), "A": f("L0_attn_A"), "C_T": f("L0_attn_C").T, "W_out": f("L0_attn_W_out"),
        "b_out": np.broadcast_to(f("L0_attn_b_out"), (P, DM)),
        "cols": np.concatenate([per_row(f("L0_attn_b_in"), 8), per_row(f("L0_attn_conv_b"), ECH),
                                f("L0_attn_conv_w").reshape(ECH, P, TAPS).transpose(1, 0, 2).reshape(P, -1),
                                per_row(f("L0_attn_Dp"), ECH)], axis=1),
        "gate_wT": f("L0_ffn_gate_w").T, "e_bias": np.broadcast_to(f("L0_ffn_e_bias"), (P, NE)),
        "w_exp": np.concatenate([transposed(gate).reshape(NE + 1, P, -1), transposed(up).reshape(NE + 1, P, -1),
                                 down.transpose(0, 2, 1)], axis=2),
    }
    arrays = {f"in_{n}": np.ascontiguousarray(v) for n, v in arrays.items()}
    nc = bacc.Bacc("TRN2", target_bir_lowering=False, num_devices=1)
    a = {n[3:]: nc.dram_tensor(n, v.shape, mybir.dt.from_np(v.dtype), kind="ExternalInput").ap()
         for n, v in arrays.items()}
    a["v_last"] = nc.dram_tensor("v_last", (BATCH, 4, DM), F32, kind="Internal").ap()
    out = nc.dram_tensor("out", (TOK, DM), F32, kind="ExternalOutput").ap()
    build(nc, a, out)
    r = run(nc, [arrays], core_ids=[0])
    return np.asarray(r.results[0]["out"]).reshape(BATCH, SEQ, DM)
```
